# Optimizing a Trainium2 kernel written in Bass

```python
import numpy as np
import jax
import jax.numpy as jnp

def _softmax(x, axis=-1):
    return jax.nn.softmax(x, axis=axis)

def _gelu(x):
    return jax.nn.gelu(x, approximate=True)

def _silu(x):
    return jax.nn.silu(x)

def _sigmoid(x):
    return jax.nn.sigmoid(x)

def _layernorm(x, axis=-1, eps=1e-05):
    m = jnp.mean(x, axis=axis, keepdims=True)
    v = jnp.var(x, axis=axis, keepdims=True)
    return (x - m) / jnp.sqrt(v + eps)

def _scatter_add(tgt, idx, src, axis=0):
    return tgt.at[idx].add(src)

def _segment_sum(src, seg, n):
    return jax.ops.segment_sum(src, seg, n)
kernel_name = 'mk_macaron_d1_jaxref_r4_acb5e0'

def setup_inputs(seed: int=0):
    np.random.seed(seed)
    _w = jnp.asarray

    def _L0_attn_setup():
        import jax, jax.numpy as jnp
        import numpy as np
        B, S, D, H = (2, 512, 256, 16)
        DK = D // H
        NEG = -65504.0
        key = jax.random.key(seed)
        ks = jax.random.split(key, 5)
        scale = 1.0 / np.sqrt(D)
        return {'x': jax.random.normal(ks[0], (B, S, D), dtype=jnp.float32), 'W_q': jax.random.normal(ks[1], (D, D), dtype=jnp.float32) * scale, 'W_k': jax.random.normal(ks[2], (D, D), dtype=jnp.float32) * scale, 'W_v': jax.random.normal(ks[3], (D, D), dtype=jnp.float32) * scale, 'W_o': jax.random.normal(ks[4], (D, D), dtype=jnp.float32) * scale}
    _L0_attn_in = _L0_attn_setup()

    def _L0_ffn_setup():
        import jax, jax.numpy as jnp
        import numpy as np
        B, S, D = (4, 1024, 256)
        H = 1024
        RH = 256
        E = 16
        K = 2
        NS = 1

        def _swiglu(x, w1, w2, w3):
            return jax.nn.silu(x @ w1) * (x @ w2) @ w3
        key = jax.random.key(seed)
        ks = jax.random.split(key, 9)
        s = 0.02
        return {'x': jax.random.normal(ks[0], (B, S, D), dtype=jnp.float32), 'router_w': jax.random.normal(ks[1], (D, E), dtype=jnp.float32) * s, 'expert_bias': jnp.zeros((E,), dtype=jnp.float32), 'shared_w1': jax.random.normal(ks[2], (NS, D, H), dtype=jnp.float32) * s, 'shared_w2': jax.random.normal(ks[3], (NS, D, H), dtype=jnp.float32) * s, 'shared_w3': jax.random.normal(ks[4], (NS, H, D), dtype=jnp.float32) * s, 'routed_w1': jax.random.normal(ks[5], (E, D, RH), dtype=jnp.float32) * s, 'routed_w2': jax.random.normal(ks[6], (E, D, RH), dtype=jnp.float32) * s, 'routed_w3': jax.random.normal(ks[7], (E, RH, D), dtype=jnp.float32) * s}
    _L0_ffn_in = _L0_ffn_setup()
    _d = {'L0_attn_x': _L0_attn_in['x'], 'L0_attn_W_q': _L0_attn_in['W_q'], 'L0_attn_W_k': _L0_attn_in['W_k'], 'L0_attn_W_v': _L0_attn_in['W_v'], 'L0_attn_W_o': _L0_attn_in['W_o'], 'L0_ffn_router_w': _L0_ffn_in['router_w'], 'L0_ffn_expert_bias': _L0_ffn_in['expert_bias'], 'L0_ffn_shared_w1': _L0_ffn_in['shared_w1'], 'L0_ffn_shared_w2': _L0_ffn_in['shared_w2'], 'L0_ffn_shared_w3': _L0_ffn_in['shared_w3'], 'L0_ffn_routed_w1': _L0_ffn_in['routed_w1'], 'L0_ffn_routed_w2': _L0_ffn_in['routed_w2'], 'L0_ffn_routed_w3': _L0_ffn_in['routed_w3']}
    _x0 = _d['L0_attn_x']
    _d['L0_attn_x'] = jax.random.normal(jax.random.fold_in(jax.random.key(seed), 1), (8, 512, 256), dtype=_x0.dtype)
    del _x0
    return _d

def reference(L0_attn_x, L0_attn_W_q, L0_attn_W_k, L0_attn_W_v, L0_attn_W_o, L0_ffn_router_w, L0_ffn_expert_bias, L0_ffn_shared_w1, L0_ffn_shared_w2, L0_ffn_shared_w3, L0_ffn_routed_w1, L0_ffn_routed_w2, L0_ffn_routed_w3):

    def _L0_attn_ref(x, W_q, W_k, W_v, W_o):
        import jax, jax.numpy as jnp
        import numpy as np
        B, S, D, H = (2, 512, 256, 16)
        DK = D // H
        NEG = -65504.0
        b, s, d = x.shape

        def proj(W):
            return (x @ W.T).reshape(b, s, H, DK).transpose(0, 2, 1, 3)
        q, k, v = (proj(W_q), proj(W_k), proj(W_v))
        scores = jnp.einsum('bhqd,bhkd->bhqk', q, k) / jnp.sqrt(jnp.float32(DK))
        causal = jnp.tril(jnp.ones((s, s), dtype=bool))
        scores = jnp.where(causal, scores, NEG)
        attn = jax.nn.softmax(scores, axis=-1)
        out = jnp.einsum('bhqk,bhkd->bhqd', attn, v)
        out = out.transpose(0, 2, 1, 3).reshape(b, s, d)
        return out @ W_o.T

    def _L0_ffn_ref(x, router_w, expert_bias, shared_w1, shared_w2, shared_w3, routed_w1, routed_w2, routed_w3):
        import jax, jax.numpy as jnp
        import numpy as np
        B, S, D = (4, 1024, 256)
        H = 1024
        RH = 256
        E = 16
        K = 2
        NS = 1

        def _swiglu(x, w1, w2, w3):
            return jax.nn.silu(x @ w1) * (x @ w2) @ w3
        shared_out = jnp.sum(jax.vmap(lambda w1, w2, w3: _swiglu(x, w1, w2, w3))(shared_w1, shared_w2, shared_w3), axis=0)
        scores = jax.nn.sigmoid(x @ router_w)
        sel_scores = scores + expert_bias
        _, top_idx = jax.lax.top_k(sel_scores, K)
        top_scores = jnp.take_along_axis(scores, top_idx, axis=-1)
        gates = jnp.sum(jax.nn.one_hot(top_idx, E, dtype=scores.dtype) * top_scores[..., None], axis=-2)
        xf = x.reshape(-1, D)
        gf = gates.reshape(-1, E).T

        def body(acc, ws):
            w1, w2, w3, g = ws
            return (acc + _swiglu(xf, w1, w2, w3) * g[:, None], None)
        routed_out, _ = jax.lax.scan(body, jnp.zeros_like(xf), (routed_w1, routed_w2, routed_w3, gf))
        return shared_out + routed_out.reshape(x.shape)
    x = L0_attn_x
    x = x + 0.5 * _L0_ffn_ref(_layernorm(x, axis=-1), L0_ffn_router_w, L0_ffn_expert_bias, L0_ffn_shared_w1, L0_ffn_shared_w2, L0_ffn_shared_w3, L0_ffn_routed_w1, L0_ffn_routed_w2, L0_ffn_routed_w3)
    x = x + _L0_attn_ref(_layernorm(x, axis=-1), L0_attn_W_q, L0_attn_W_k, L0_attn_W_v, L0_attn_W_o)
    x = x + 0.5 * _L0_ffn_ref(_layernorm(x, axis=-1), L0_ffn_router_w, L0_ffn_expert_bias, L0_ffn_shared_w1, L0_ffn_shared_w2, L0_ffn_shared_w3, L0_ffn_routed_w1, L0_ffn_routed_w2, L0_ffn_routed_w3)
    return x

_drawn_inputs = setup_inputs


def setup_inputs(seed=0):
    import zlib

    import numpy as np

    out = dict(_drawn_inputs(seed))
    spreads = {'L0_ffn_expert_bias': (0.0, 0.54)}
    factors = {'L0_ffn_router_w': 5.86,
     'L0_ffn_routed_w1': 4.339,
     'L0_ffn_routed_w2': 4.295,
     'L0_ffn_routed_w3': 4.292}
    for name, (base, spread) in spreads.items():
        noise = np.random.default_rng([zlib.crc32(name.encode()), seed]).standard_normal(out[name].shape)
        drawn = base * np.exp(spread * noise) if base else spread * noise
        out[name] = jnp.asarray(drawn.astype(out[name].dtype))
    for name, factor in factors.items():
        out[name] = (out[name] * factor).astype(out[name].dtype)
    return out
```

```python
import math
from contextlib import ExitStack

import concourse.bass as bass
from concourse import mybir

P = 128
F32 = mybir.dt.float32
F32R = mybir.dt.float32r
BF16 = mybir.dt.bfloat16
I32 = mybir.dt.int32
U32 = mybir.dt.uint32
ALU = mybir.AluOpType
ACT = mybir.ActivationFunctionType
AX = mybir.AxisListType

CT = 4
CHUNK = CT * P
EPS = 1e-5
TOPK = 2


class Shapes:

    def __init__(self, x, router_w, shared_w1, routed_w1):
        self.B, self.S, self.D = x.shape
        self.T = self.B * self.S
        self.NT = self.T // P
        self.NC = self.T // CHUNK
        self.KD = self.D // P
        self.E = router_w.shape[1]
        self.RH = routed_w1.shape[2]
        self.KR = self.RH // P
        self.SH = shared_w1.shape[-1]
        self.JS = self.SH // P
        most = (self.T * TOPK + self.E * (P - 1)) // P
        self.NB = -(-most // 4) * 4
        assert self.S == CHUNK and self.D % P == 0 and self.RH == self.D


class Mem:

    def __init__(self, nc, ctx, tag=""):
        self.nc, self.ctx, self.tag = nc, ctx, tag

    def sb(self, name, shape, dt=F32):
        return self.ctx.enter_context(self.nc.sbuf_tensor(self.tag + name, shape, dt))

    def ps(self, name, shape, dt=F32):
        return self.ctx.enter_context(self.nc.psum_tensor(self.tag + name, shape, dt))

    def sem(self, name):
        return self.ctx.enter_context(self.nc.semaphore(self.tag + name))

    def sems(self, name, n):
        return [self.sem(f"{name}{i}") for i in range(n)]


def setup(nc, z, g, dram):
    with ExitStack() as ctx:
        m = Mem(nc, ctx, "set_")
        zero = m.sb("zero", [P, z.D])
        made = m.sem("made")
        zeroed = m.sem("zeroed")
        stored = m.sem("stored")
        loaded = m.sem("loaded")
        block = ctx.enter_context(nc.Block())
        KD, E = z.KD, z.E

        @block.gpsimd
        def _(pool):
            n = [0]

            def done(ins):
                n[0] += 1
                ins.then_inc(made, 1)
                pool.wait_ge(made, n[0])

            done(nc.gpsimd.memset(g.ident[:], 0.0))
            done(nc.gpsimd.affine_select(out=g.ident[:], in_=g.ident[:], compare_op=ALU.not_equal, fill=1.0,
                                         base=0, pattern=[[-1, P]], channel_multiplier=1))
            done(nc.gpsimd.memset(g.before[:], 1.0))
            done(nc.gpsimd.affine_select(out=g.before[:], in_=g.before[:], compare_op=ALU.is_gt, fill=0.0,
                                         base=0, pattern=[[1, P]], channel_multiplier=-1))
            done(nc.gpsimd.memset(g.ones[:], 1.0))
            done(nc.gpsimd.memset(g.mhalf[:], -0.5))
            done(nc.gpsimd.memset(g.eps[:], EPS))
            done(nc.gpsimd.iota(g.rev_i[:], pattern=[[-1, E]], base=E, channel_multiplier=0))
            done(nc.gpsimd.iota(g.blk_i[:], pattern=[[1, z.NB]], base=0, channel_multiplier=0))
            done(nc.gpsimd.tensor_copy(g.rev[:], g.rev_i[:]))
            done(nc.gpsimd.tensor_copy(g.blk[:], g.blk_i[:]))
            done(nc.gpsimd.memset(g.keep[:], 1.0))
            done(nc.gpsimd.memset(g.keep[:, :, 0:1], 0.0))

        @block.vector
        def _(dve):
            nc.vector.memset(zero[:], 0.0).then_inc(zeroed, 1)

        @block.sync
        def _(sp):
            n = 0

            def load(dst, src):
                nonlocal n
                sp.dma_start(dst, src).then_inc(loaded, 16)
                n += 16

            load(g.rw[:], dram.router_w.rearrange("(k p) e -> p k e", p=P))
            load(g.bias[:], dram.expert_bias.rearrange("(o e) -> o e", o=1).to_broadcast([P, E]))
            sp.wait_ge(zeroed, 1)
            for b0 in range(0, z.NB, 8):
                sp.dma_start(dram.xs[b0 * P:(b0 + 8) * P, :].rearrange("(b p) d -> p b d", p=P),
                             zero[:].rearrange("p (o d) -> p o d", o=1).to_broadcast([P, 8, z.D])).then_inc(stored, 16)
            sp.wait_ge(loaded, n)
            sp.wait_ge(stored, 16 * (z.NB // 8))


def norm_first(nc, z, g, dram, x_src):
    with ExitStack() as ctx:
        m = Mem(nc, ctx, "nf_")
        x = m.sb("x", [P, 2, CT, z.D])
        xn = m.sb("xn", [P, 2, CT, z.D])
        xnT = m.sb("xnT", [P, 2, z.KD, CHUNK])
        stat = m.sb("stat", [P, 2, CT, 6])
        mv = m.sb("mv", [P, 2, CT, 2])
        veps = m.sb("veps", [P, 2, CT])
        rstd = m.sb("rstd", [P, 2, CT])
        psT = m.ps("psT", [P, 2, z.KD, CHUNK])
        psL = m.ps("psL", [P, 512])
        x_in = m.sems("x_in", 2)
        stats = m.sem("stats")
        var = m.sem("var")
        eps_in = m.sem("eps_in")
        rs = m.sem("rs")
        normed = m.sem("normed")
        turned = m.sem("turned")
        xnT_in = m.sem("xnT_in")
        logit = m.sem("logit")
        logit_in = m.sem("logit_in")
        held = m.sem("held")
        xn_out = m.sems("xn_out", 2)
        block = ctx.enter_context(nc.Block())

        @block.sync
        def _(sp):
            def load(c, u):
                sp.dma_start(x[:, u], x_src[bass.ds(c * CHUNK, CHUNK), :].rearrange("(t p) d -> p t d", p=P)
                             ).then_inc(x_in[u], 16)

            def store(c, u):
                sp.wait_ge(normed, c + 1)
                sp.sem_inc(held, 1)
                sp.dma_start(dram.xn[bass.ds(c * CHUNK, CHUNK), :].rearrange("(t p) d -> p t d", p=P), xn[:, u]
                             ).then_inc(xn_out[u], 16)
                sp.wait_ge(xnT_in, c + 1)
                sp.sem_inc(held, 1)
                sp.dma_start(dram.xnT[:, :, bass.ds(c * CHUNK, CHUNK)], xnT[:, u]).then_inc(xn_out[u], 16)

            load(0, 0)
            load(1, 1)
            with sp.Fori(0, z.NC // 2 - 1) as c2:
                for u in range(2):
                    store(c2 * 2 + u, u)
                    load(c2 * 2 + u + 2, u)
            for u in range(2):
                store(z.NC - 2 + u, u)
            for u in range(2):
                sp.wait_ge(xn_out[u], 32 * (z.NC // 2))

        @block.vector
        def _(dve):
            def chunk(c2, u, first):
                c = c2 * 2 + u
                dve.wait_ge(x_in[u], c2 * 16 + 16)
                for t in range(CT):
                    nc.vector.bn_stats(stat[:, u, t, :], x[:, u, t, :]).then_inc(stats, 1)
                dve.wait_ge(stats, c * CT + CT)
                dve.sem_inc(held, 1)
                for t in range(CT):
                    ins = nc.vector.bn_aggr(mv[:, u, t, :], stat[:, u, t, :])
                ins.then_inc(var, 1)
                dve.wait_ge(rs, c + 1)
                if not first:
                    dve.wait_ge(xn_out[u], c2 * 32)
                for t in range(CT):
                    ins = nc.vector.tensor_scalar(xn[:, u, t, :], x[:, u, t, :], mv[:, u, t, 0:1],
                                                  rstd[:, u, t:t + 1], ALU.subtract, ALU.mult)
                ins.then_inc(normed, 1)
                dve.wait_ge(logit, c + 1)
                nc.vector.tensor_copy(g.logits[:, bass.ds(c * (CT * z.E), CT * z.E)],
                                      psL[:, 0:CT * z.E]).then_inc(logit_in, 1)

            for u in range(2):
                chunk(0, u, True)
            with dve.Fori(1, z.NC // 2) as c2:
                for u in range(2):
                    chunk(c2, u, False)

        @block.gpsimd
        def _(pool):
            with pool.Fori(0, z.NC // 2) as c2:
                for u in range(2):
                    c = c2 * 2 + u
                    pool.wait_ge(var, c + 1)
                    nc.gpsimd.tensor_tensor(veps[:, u, :], mv[:, u, :, 1], g.eps[:, 0:CT], ALU.add).then_inc(eps_in, 1)
                    pool.wait_ge(eps_in, c + 1)
                    nc.gpsimd.tensor_tensor(rstd[:, u, :], veps[:, u, :], g.mhalf[:, 0:CT], ALU.pow).then_inc(rs, 1)

        @block.tensor
        def _(pe):
            def turn(c, u, first):
                pe.wait_ge(normed, c + 1)
                if not first:
                    pe.wait_ge(xnT_in, c - 1)
                for t in range(CT):
                    for k in range(z.KD):
                        ins = pe.transpose(psT[:, u, k, t * P:(t + 1) * P], xn[:, u, t, k * P:(k + 1) * P],
                                           g.ident[:, :])
                ins.then_inc(turned, 1)

            def route(c, u, first):
                pe.wait_ge(xnT_in, c + 1)
                if not first:
                    pe.wait_ge(logit_in, c)
                for t in range(CT):
                    for k in range(z.KD):
                        ins = pe.matmul(psL[:, t * z.E:(t + 1) * z.E], xnT[:, u, k, t * P:(t + 1) * P],
                                        g.rw[:, k, :], start=(k == 0), stop=(k == z.KD - 1))
                ins.then_inc(logit, 1)

            for u in range(2):
                turn(u, u, True)
                route(u, u, u == 0)
            with pe.Fori(1, z.NC // 2) as c2:
                for u in range(2):
                    turn(c2 * 2 + u, u, False)
                    route(c2 * 2 + u, u, False)

        @block.scalar
        def _(act):
            def chunk(c, c2, u, first):
                act.wait_ge(turned, c + 1)
                if not first:
                    act.wait_ge(xn_out[u], c2 * 32)
                    act.wait_ge(logit, c - 1)
                nc.scalar.copy(xnT[:, u], psT[:, u]).then_inc(xnT_in, 1)

            for u in range(2):
                chunk(u, 0, u, True)
            with act.Fori(1, z.NC // 2) as c2:
                for u in range(2):
                    chunk(c2 * 2 + u, c2, u, False)


def feed_forward(nc, z, g, dram, tag, x_src):
    KD, KR, E, NT, RH = z.KD, z.KR, z.E, z.NT, z.RH
    TE = NT * E
    NB, NC = z.NB, z.NC
    with ExitStack() as ctx:
        m = Mem(nc, ctx, tag)
        ew12 = m.sb("ew12", [P, E, KD, 2 * RH])
        ew3 = m.sb("ew3", [P, E, KR, z.D])
        sw12 = m.sb("sw12", [P, KD, 2 * z.SH])
        sw3 = m.sb("sw3", [P, z.JS, z.D])
        xnT = m.sb("xnT", [P, 2, KD, CHUNK])
        xr = m.sb("xr", [P, 2, CT, z.D])
        sil = m.sb("sil", [P, 2, CHUNK])
        hT = m.sb("hT", [P, z.JS, CHUNK])
        score = m.sb("score", [P, NT, E])
        sel = m.sb("sel", [P, NT, E])
        tmp = m.sb("tmp", [P, NT, E])
        one1 = m.sb("one1", [P, NT, E])
        one2 = m.sb("one2", [P, NT, E])
        both = m.sb("both", [P, NT, E], BF16)
        top = m.sb("top", [P, 6, NT])
        count = m.sb("count", [P, E, NT])
        upto = m.sb("upto", [P, E, NT])
        small = m.sb("small", [P, 8, E])
        small_i = m.sb("small_i", [P, 2, E], I32)
        bexp = m.sb("bexp", [1, NB])
        bexp_i = m.sb("bexp_i", [1, NB], I32)
        slot_f = m.sb("slot_f", [P, NT, TOPK])
        xq = m.sb("xq", [P, 2, CT, z.D])
        idx = m.sb("idx", [P, 2, CT * TOPK], U32)
        bcmp = xq[0:1].rearrange("p u t d -> p (u t d)")[:, 0:NB * E].rearrange("p (b e) -> p b e", e=E)
        xs = m.sb("xs", [P, 4, z.D])
        xsT = m.sb("xsT", [P, 2, KD * P])
        silr = m.sb("silr", [P, 2, RH])
        hr = m.sb("hr", [P, 2, RH])
        hrT = m.sb("hrT", [P, 2, KR * P])
        yr = m.sb("yr", [P, 4, z.D])
        bank = [m.ps(f"bank{i}", [P, 512]) for i in range(8)]
        psA, psB, psO = bank[0:2], bank[2:4], bank[4:8]
        psR, psC = bank[4], bank[5]
        rUp, rTx, rTh, rY = bank[0:2], bank[2], bank[3], bank[4:6]

        sw_in = m.sem("sw_in")
        ew_in = m.sem("ew_in")
        held = m.sem("held")
        xnT_ld = m.sems("xnT_ld", 2)
        xr_ld = m.sems("xr_ld", 2)
        sh_st = m.sems("sh_st", 2)
        scored = m.sem("scored")
        rt = m.sem("rt")
        picked = m.sem("picked")
        ranked = m.sem("ranked")
        placed = m.sem("placed")
        a_done = m.sem("a_done")
        b_done = m.sem("b_done")
        s_done = m.sem("s_done")
        h_done = m.sem("h_done")
        o_done = m.sem("o_done")
        sh_done = m.sem("sh_done")
        xq_ld = m.sems("xq_ld", 2)
        idx_in = m.sem("idx_in")
        scat = m.sems("scat", 2)
        all_scat = m.sem("all_scat")
        xs_ld = m.sems("xs_ld", 4)
        tx_done = m.sem("tx_done")
        xT_ev = m.sem("xT_ev")
        rup_done = m.sem("rup_done")
        rs_done = m.sem("rs_done")
        rh_done = m.sem("rh_done")
        th_done = m.sem("th_done")
        hT_ev = m.sem("hT_ev")
        dn_done = m.sem("dn_done")
        y_done = m.sem("y_done")
        y_st = m.sems("y_st", 4)
        block = ctx.enter_context(nc.Block())

        LAST = NB + 1

        def steps(eng, body):
            for r in range(4):
                body(0, r, lambda lag, n=r: 0 <= n - lag < NB)
            with eng.Fori(1, NB // 4 - 1) as q:
                for r in range(4):
                    body(q, r, lambda lag: True)
            for n in range(NB - 4, LAST + 1):
                body(n // 4, n % 4, lambda lag, n=n: 0 <= n - lag < NB)

        @block.sync
        def _(sp):
            sp.dma_start(sw12[:, :, 0:z.SH], dram.shared_w1.rearrange("(k p) n -> p k n", p=P)).then_inc(sw_in, 16)
            sp.dma_start(sw12[:, :, z.SH:], dram.shared_w2.rearrange("(k p) n -> p k n", p=P)).then_inc(sw_in, 16)
            sp.dma_start(sw3[:], dram.shared_w3.rearrange("(j p) n -> p j n", p=P)).then_inc(sw_in, 16)

            def load(c, c2, u, first):
                if not first:
                    sp.wait_ge(b_done, (c - 1) * z.JS)
                    sp.sem_inc(held, 1)
                    sp.wait_ge(sh_st[u], c2 * 16)
                    sp.sem_inc(held, 1)
                sp.dma_start(xnT[:, u], dram.xnT[:, :, bass.ds(c * CHUNK, CHUNK)]).then_inc(xnT_ld[u], 16)
                sp.dma_start(xr[:, u], x_src[bass.ds(c * CHUNK, CHUNK), :].rearrange("(t p) d -> p t d", p=P)
                             ).then_inc(xr_ld[u], 16)

            def store(c, u):
                sp.wait_ge(sh_done, c * 4 + 8)
                sp.sem_inc(held, 1)
                sp.dma_start(dram.sh[bass.ds(c * CHUNK, CHUNK), :].rearrange("(t p) d -> p t d", p=P), xr[:, u]
                             ).then_inc(sh_st[u], 16)

            load(0, 0, 0, True)
            load(1, 0, 1, True)
            for e in range(E):
                for dst, src in ((ew12[:, e, :, 0:RH], dram.routed_w1), (ew12[:, e, :, RH:], dram.routed_w2),
                                 (ew3[:, e], dram.routed_w3)):
                    sp.dma_start(dst, src[e].rearrange("(k p) n -> p k n", p=P)).then_inc(ew_in, 16)
            with sp.Fori(1, NC // 2) as c2:
                for u in range(2):
                    store(c2 * 2 + u - 2, u)
                    load(c2 * 2 + u, c2, u, False)
            for u in range(2):
                store(NC - 2 + u, u)

            def fetch(q, r):
                sp.wait_ge(tx_done, q * 4 + r + 1)
                sp.sem_inc(held, 1)
                sp.dma_start(xs[:, r], dram.xs[bass.ds(q * (4 * P) + r * P, P), :]).then_inc(xs_ld[r], 16)

            def put(q, r):
                sp.wait_ge(y_done, q * 4 + r + 3)
                sp.sem_inc(held, 1)
                sp.dma_start(dram.ys[bass.ds(q * (4 * P) + r * P, P), :], yr[:, r]).then_inc(y_st[r], 16)

            sp.wait_ge(all_scat, 1)
            for r in range(4):
                fetch(0, r)
            with sp.Fori(0, NB // 4 - 1) as q:
                for r in range(4):
                    fetch(q + 1, r)
                    put(q, r)
            for r in range(4):
                put(NB // 4 - 1, r)
            for u in range(2):
                sp.wait_ge(sh_st[u], 16 * (NC // 2))
            for r in range(4):
                sp.wait_ge(y_st[r], 16 * (NB // 4 + 1))

        @block.gpsimd
        def _(pool):
            pool.wait_ge(placed, 1)

            def load(c, u):
                pool.dma_start(xq[:, u], dram.xn[bass.ds(c * CHUNK, CHUNK), :].rearrange("(t p) d -> p t d", p=P)
                               ).then_inc(xq_ld[u], 16)

            def send(c, c2, u):
                pool.wait_ge(xq_ld[u], c2 * 16 + 16)
                nc.gpsimd.tensor_copy(idx[:, u, :], g.slot[:, bass.ds(c * (CT * TOPK), CT * TOPK)]
                                      ).then_inc(idx_in, 1)
                pool.wait_ge(idx_in, c + 1)
                pool.sem_inc(held, 1)
                for t in range(CT):
                    for k in range(TOPK):
                        nc.gpsimd.indirect_dma_start(
                            dram.xs, bass.IndirectOffsetOnAxis(ap=idx[:, u, TOPK * t + k:TOPK * t + k + 1], axis=0),
                            xq[:, u, t, :], None).then_inc(scat[u], 16)

            per = 16 * CT * TOPK
            load(0, 0)
            load(1, 1)
            send(0, 0, 0)
            send(1, 0, 1)
            with pool.Fori(1, NC // 2) as c2:
                for u in range(2):
                    pool.wait_ge(scat[u], c2 * per)
                    load(c2 * 2 + u, u)
                for u in range(2):
                    send(c2 * 2 + u, c2, u)
            for u in range(2):
                pool.wait_ge(scat[u], per * (NC // 2))
            pool.sem_inc(all_scat, 1)

        @block.scalar
        def _(act):
            nc.scalar.activation(score[:].rearrange("p t e -> p (t e)"), g.logits[:], ACT.Sigmoid).then_inc(scored, 1)
            with act.Fori(0, NC) as c:
                for j in range(z.JS):
                    n = c * z.JS + j
                    act.wait_ge(a_done, n + 1)
                    act.wait_ge(h_done, n + 1)
                    nc.scalar.activation(sil[:, j % 2, :], psA[j % 2][:, :], ACT.Silu).then_inc(s_done, 1)
            act.sem_inc(xT_ev, 1)

            def step(q, r, has):
                i = q * 4 + r
                if has(0):
                    act.wait_ge(rup_done, i + 3)
                    nc.scalar.activation(silr[:, r % 2, :], rUp[r % 2][:, 0:RH], ACT.Silu).then_inc(rs_done, 1)
                if has(-1):
                    evacuate(i + 1, (r + 1) % 2)

            def evacuate(i, s):
                act.wait_ge(tx_done, i + 5)
                act.wait_ge(rup_done, i + 1)
                nc.scalar.copy(xsT[:, s, :], rTx[:, 0:KD * P]).then_inc(xT_ev, 1)

            evacuate(0, 0)
            steps(act, step)

        @block.vector
        def _(dve):
            dve.sem_inc(h_done, 2)
            dve.sem_inc(sh_done, 4)
            n = [0]

            def link(ins):
                n[0] += 1
                ins.then_inc(rt, 1)
                dve.wait_ge(rt, n[0])

            v = nc.vector
            flat = lambda a: a[:].rearrange("p t e -> p (t e)")
            over_t = lambda a: a.rearrange("p (o e) -> p o e", o=1).to_broadcast([P, NT, E])
            over_e = lambda a: a.rearrange("p (t o) -> p t o", o=1).to_broadcast([P, NT, E])
            dve.wait_ge(scored, 1)
            link(v.tensor_tensor(sel[:], score[:], over_t(g.bias[:]), ALU.add))
            for k, one in enumerate((one1, one2)):
                link(v.tensor_reduce(top[:, k, :], sel[:], AX.X, ALU.max))
                link(v.tensor_tensor(tmp[:], sel[:], over_e(top[:, k, :]), ALU.is_equal))
                link(v.tensor_tensor(tmp[:], tmp[:], over_t(g.rev[:]), ALU.mult))
                link(v.tensor_reduce(top[:, 2 + k, :], tmp[:], AX.X, ALU.max))
                link(v.tensor_tensor(one[:], over_t(g.rev[:]), over_e(top[:, 2 + k, :]), ALU.is_equal))
                if k == 0:
                    link(v.scalar_tensor_tensor(sel[:], one[:], -3.0e38, sel[:], ALU.mult, ALU.add))
            link(v.tensor_tensor(both[:], one1[:], one2[:], ALU.add))
            dve.sem_inc(picked, 1)
            for k, one in enumerate((one1, one2)):
                link(v.tensor_tensor(tmp[:], score[:], one[:], ALU.mult))
                link(v.tensor_reduce(top[:, 4 + k, :], tmp[:], AX.X, ALU.add))
                link(v.tensor_scalar(g.gate[:, :, k], top[:, 4 + k, :], 0.5, None, ALU.mult))
            dve.wait_ge(ranked, 1)
            link(v.tensor_copy(count[:], psC[:, :].rearrange("p (t e) -> p e t", e=E)))
            link(v.tensor_tensor_scan(upto[:].rearrange("p e t -> p (e t)"), g.keep[:].rearrange("p e t -> p (e t)"),
                                      count[:].rearrange("p e t -> p (e t)"), 0.0, ALU.mult, ALU.add))
            link(v.tensor_scalar(small[:, 0, :], upto[:, :, NT - 1], float(P - 1), None, ALU.add))
            link(v.tensor_copy(small_i[:, 0, :], small[:, 0, :]))
            link(v.tensor_single_scalar(small_i[:, 1, :], small_i[:, 0, :], int(math.log2(P)), ALU.logical_shift_right))
            link(v.tensor_copy(small[:, 1, :], small_i[:, 1, :]))
            link(v.memset(small[:, 2, :], 1.0))
            link(v.tensor_tensor_scan(small[:, 3, :], small[:, 2, :], small[:, 1, :], 0.0, ALU.mult, ALU.add))
            link(v.tensor_tensor(small[:, 4, :], small[:, 3, :], small[:, 1, :], ALU.subtract))
            link(v.tensor_scalar(small[:, 5, :], small[:, 4, :], float(P), None, ALU.mult))
            link(v.tensor_tensor(upto[:], upto[:], count[:], ALU.subtract))
            link(v.tensor_tensor(upto[:], upto[:], small[:, 5, :].rearrange("p (e o) -> p e o", o=1)
                                 .to_broadcast([P, E, NT]), ALU.add))
            link(v.tensor_tensor(sel[:], psR[:, :].rearrange("p (t e) -> p t e", e=E),
                                 upto[:].rearrange("p e t -> p t e"), ALU.add))
            for k, one in enumerate((one1, one2)):
                link(v.tensor_tensor(tmp[:], sel[:], one[:], ALU.mult))
                link(v.tensor_reduce(slot_f[:, :, k], tmp[:], AX.X, ALU.add))
            link(v.tensor_copy(g.slot[:], slot_f[:].rearrange("p t k -> p (t k)")))
            link(v.tensor_tensor(bcmp, small[0:1, 3, :].rearrange("p (o e) -> p o e", o=1).to_broadcast([1, NB, E]),
                                 g.blk[0:1, :].rearrange("p (b o) -> p b o", o=1).to_broadcast([1, NB, E]), ALU.is_le))
            link(v.tensor_reduce(bexp[:], bcmp, AX.X, ALU.add))
            link(v.tensor_scalar(bexp[:], bexp[:], float(E - 1), None, ALU.min))
            link(v.tensor_copy(bexp_i[:], bexp[:]))
            dve.sem_inc(placed, 1)

            def shared(c2, u):
                c = c2 * 2 + u
                for j in range(z.JS):
                    dve.wait_ge(s_done, c * z.JS + j + 1)
                    dve.wait_ge(b_done, c * z.JS + j + 1)
                    v.tensor_tensor(hT[:, j, :], sil[:, j % 2, :], psB[j % 2][:, :], ALU.mult).then_inc(h_done, 1)
                dve.wait_ge(xr_ld[u], c2 * 16 + 16)
                for t in range(CT):
                    dve.wait_ge(o_done, c * CT + t + 1)
                    v.scalar_tensor_tensor(xr[:, u, t, :], psO[t][:, 0:z.D], 0.5, xr[:, u, t, :],
                                           ALU.mult, ALU.add).then_inc(sh_done, 1)

            with dve.Fori(0, NC // 2) as c2:
                for u in range(2):
                    shared(c2, u)

            dve.sem_inc(rh_done, 2)
            dve.sem_inc(hT_ev, 1)
            dve.sem_inc(y_done, 2)
            for r in range(4):
                dve.sem_inc(y_st[r], 16)

            def step(q, r, has):
                i = q * 4 + r
                if has(1):
                    dve.wait_ge(th_done, i)
                    v.tensor_copy(hrT[:, (r - 1) % 2, :], rTh[:, 0:KR * P]).then_inc(hT_ev, 1)
                if has(0):
                    dve.wait_ge(rs_done, i + 1)
                    v.tensor_tensor(hr[:, r % 2, :], silr[:, r % 2, :], rUp[r % 2][:, RH:2 * RH], ALU.mult
                                    ).then_inc(rh_done, 1)
                if has(2):
                    s = (r - 2) % 4
                    dve.wait_ge(dn_done, i - 1)
                    dve.wait_ge(y_st[s], (q * 16 if r < 2 else q * 16 + 16))
                    v.tensor_copy(yr[:, s, :], rY[r % 2][:, 0:z.D]).then_inc(y_done, 1)

            steps(dve, step)

        @block.tensor
        def _(pe):
            pe.sem_inc(tx_done, 4)
            pe.sem_inc(rup_done, 2)
            pe.wait_ge(picked, 1)
            marks = both[:].rearrange("p t e -> p (t e)")
            pe.matmul(psR[:, 0:TE], g.before[:, :], marks, start=True, stop=True)
            pe.matmul(psC[:, 0:TE], g.ones[:, :], marks, start=True, stop=True).then_inc(ranked, 1)
            pe.wait_ge(sw_in, 48)

            def shared(c2, u, first):
                c = c2 * 2 + u
                pe.wait_ge(xnT_ld[u], c2 * 16 + 16)
                for j in range(z.JS):
                    pe.wait_ge(h_done, c * z.JS + j + 1)
                    for ps, w, sem in ((psA, 0, a_done), (psB, z.SH, b_done)):
                        for k in range(KD):
                            ins = pe.matmul(ps[j % 2][:, :], sw12[:, k, w + j * P:w + (j + 1) * P], xnT[:, u, k, :],
                                            start=(k == 0), stop=(k == KD - 1))
                        ins.then_inc(sem, 1)
                if first:
                    pe.wait_ge(placed, 1)
                for j in range(z.JS):
                    pe.wait_ge(h_done, c * z.JS + j + 3)
                    for t in range(CT):
                        if j == 0:
                            pe.wait_ge(sh_done, c * CT + t + 1)
                        ins = pe.matmul(psO[t][:, 0:z.D], hT[:, j, t * P:(t + 1) * P], sw3[:, j, :],
                                        start=(j == 0), stop=(j == z.JS - 1))
                        if j == z.JS - 1:
                            ins.then_inc(o_done, 1)

            shared(0, 0, True)
            shared(0, 1, False)
            with pe.Fori(1, NC // 2) as c2:
                for u in range(2):
                    shared(c2, u, False)
            pe.wait_ge(sh_done, NC * CT + 4)
            pe.wait_ge(ew_in, 3 * 16 * E)
            w12 = ew12[:].rearrange("p e k n -> p (e k n)")
            w3 = ew3[:].rearrange("p e k n -> p (e k n)")

            def turn_x(q, r):
                i = q * 4 + r
                pe.wait_ge(xs_ld[r], q * 16 + 16)
                pe.wait_ge(xT_ev, i + 1)
                for k in range(KD):
                    ins = pe.transpose(rTx[:, k * P:(k + 1) * P], xs[:, r, k * P:(k + 1) * P], g.ident[:, :])
                ins.then_inc(tx_done, 1)

            def expert(i):
                return pe.value_load(bexp_i[0:1, bass.ds(i, 1)], min_val=0, max_val=E - 1)

            def step(q, r, has):
                i = q * 4 + r
                if has(0):
                    e = expert(i)
                    pe.wait_ge(xT_ev, i + 2)
                    pe.wait_ge(rh_done, i + 1)
                    for k in range(KD):
                        ins = pe.matmul(rUp[r % 2][:, :], xsT[:, r % 2, k * P:(k + 1) * P],
                                        w12[:, bass.ds(e * (KD * 2 * RH) + k * 2 * RH, 2 * RH)],
                                        start=(k == 0), stop=(k == KD - 1))
                    ins.then_inc(rup_done, 1)
                if has(1):
                    pe.wait_ge(rh_done, i + 2)
                    pe.wait_ge(hT_ev, i)
                    for k in range(KR):
                        ins = pe.transpose(rTh[:, k * P:(k + 1) * P], hr[:, (r - 1) % 2, k * P:(k + 1) * P],
                                           g.ident[:, :])
                    ins.then_inc(th_done, 1)
                if has(-1):
                    if r == 3:
                        turn_x(q + 1, 0)
                    else:
                        turn_x(q, r + 1)
                if has(2):
                    e = expert(i - 2)
                    pe.wait_ge(hT_ev, i)
                    pe.wait_ge(y_done, i - 1)
                    for k in range(KR):
                        ins = pe.matmul(rY[r % 2][:, 0:z.D], hrT[:, r % 2, k * P:(k + 1) * P],
                                        w3[:, bass.ds(e * (KR * z.D) + k * z.D, z.D)],
                                        start=(k == 0), stop=(k == KR - 1))
                    ins.then_inc(dn_done, 1)

            turn_x(0, 0)
            steps(pe, step)


def combine_last(nc, z, g, dram, out_flat):
    with ExitStack() as ctx:
        m = Mem(nc, ctx, "cl_")
        NC = z.NC
        acc = m.sb("acc", [P, 2, CT, z.D])
        yg = m.sb("yg", [P, 2, CT, TOPK, z.D])
        idx = m.sb("idx", [P, 2, CT * TOPK], U32)
        acc_ld = m.sems("acc_ld", 2)
        idx_in = m.sem("idx_in")
        y_ld = m.sems("y_ld", 2)
        mid = m.sem("mid")
        done = m.sem("done")
        held = m.sem("held")
        out_st = m.sems("out_st", 2)
        block = ctx.enter_context(nc.Block())
        per = 16 * CT * TOPK

        @block.gpsimd
        def _(pool):
            def gather(c, u, first):
                if not first:
                    pool.wait_ge(done, c - 1)
                nc.gpsimd.tensor_copy(idx[:, u, :], g.slot[:, bass.ds(c * (CT * TOPK), CT * TOPK)]
                                      ).then_inc(idx_in, 1)
                pool.wait_ge(idx_in, c + 1)
                pool.sem_inc(held, 1)
                for t in range(CT):
                    for k in range(TOPK):
                        nc.gpsimd.indirect_dma_start(
                            yg[:, u, t, k, :], None, dram.ys,
                            bass.IndirectOffsetOnAxis(ap=idx[:, u, TOPK * t + k:TOPK * t + k + 1], axis=0)
                        ).then_inc(y_ld[u], 16)

            gather(0, 0, True)
            gather(1, 1, True)
            with pool.Fori(1, NC // 2) as c2:
                for u in range(2):
                    gather(c2 * 2 + u, u, False)

        @block.sync
        def _(sp):
            def load(c, u):
                sp.dma_start(acc[:, u], dram.sh[bass.ds(c * CHUNK, CHUNK), :].rearrange("(t p) d -> p t d", p=P)
                             ).then_inc(acc_ld[u], 16)

            def store(c, c2, u):
                sp.wait_ge(done, c + 1)
                sp.sem_inc(held, 1)
                sp.dma_start(out_flat[bass.ds(c * CHUNK, CHUNK), :].rearrange("(t p) d -> p t d", p=P), acc[:, u]
                             ).then_inc(out_st[u], 16)

            load(0, 0)
            load(1, 1)
            with sp.Fori(0, NC // 2 - 1) as c2:
                for u in range(2):
                    store(c2 * 2 + u, c2, u)
                    sp.wait_ge(out_st[u], c2 * 16 + 16)
                    sp.sem_inc(held, 1)
                    load(c2 * 2 + u + 2, u)
            for u in range(2):
                store(NC - 2 + u, NC // 2 - 1, u)
            for u in range(2):
                sp.wait_ge(out_st[u], 16 * (NC // 2))

        @block.vector
        def _(dve):
            with dve.Fori(0, NC // 2) as c2:
                for u in range(2):
                    c = c2 * 2 + u
                    dve.wait_ge(acc_ld[u], c2 * 16 + 16)
                    dve.wait_ge(y_ld[u], c2 * per + per)
                    for k in range(TOPK):
                        for t in range(CT):
                            ins = nc.vector.scalar_tensor_tensor(
                                acc[:, u, t, :], yg[:, u, t, k, :], g.gate[:, bass.ds(c * CT + t, 1), k],
                                acc[:, u, t, :], ALU.mult, ALU.add)
                            if k == 0:
                                ins.then_inc(mid, 1)
                        if k == 0:
                            dve.wait_ge(mid, c * CT + CT)
                    ins.then_inc(done, 1)


class Names:
    pass


def residents(nc, z, ctx):
    m = Mem(nc, ctx)
    g = Names()
    g.rw = m.sb("rw", [P, z.KD, z.E])
    g.bias = m.sb("bias", [P, z.E])
    g.ident = m.sb("ident", [P, P])
    g.before = m.sb("before", [P, P], BF16)
    g.ones = m.sb("ones", [P, P], BF16)
    g.mhalf = m.sb("mhalf", [P, CT])
    g.eps = m.sb("eps", [P, CT])
    g.rev_i = m.sb("rev_i", [P, z.E], I32)
    g.rev = m.sb("rev", [P, z.E])
    g.blk_i = m.sb("blk_i", [P, z.NB], I32)
    g.blk = m.sb("blk", [P, z.NB])
    g.keep = m.sb("keep", [P, z.E, z.NT])
    g.logits = m.sb("logits", [P, z.NT * z.E])
    g.slot = m.sb("slot", [P, z.NT * TOPK], U32)
    g.gate = m.sb("gate", [P, z.NT, TOPK])
    return g


def scratch(nc, z):
    d = Names()
    d.xn = nc.dram_tensor("xn_rows", [z.T, z.D], F32).ap()
    d.xnT = nc.dram_tensor("xn_turned", [P, z.KD, z.T], F32).ap()
    d.x1 = nc.dram_tensor("x1_rows", [z.T, z.D], F32).ap()
    d.x2 = nc.dram_tensor("x2_rows", [z.T, z.D], F32).ap()
    d.sh = nc.dram_tensor("x_plus_shared", [z.T, z.D], F32).ap()
    d.xs = nc.dram_tensor("rows_by_slot", [z.NB * P, z.D], F32).ap()
    d.ys = nc.dram_tensor("outputs_by_slot", [z.NB * P, z.D], F32).ap()
    return d


def attention(nc, z, g, dram):
    KD, E, D = z.KD, z.E, z.D
    H, DK = 16, 16
    HG = 4
    NG = H // HG
    MASK = -65536.0
    SL = 64
    NB_ = z.B
    UNITS1 = [(0, 0, 4), (1, 0, 2), (1, 2, 2)] + [(t, h, 1) for t in (2, 3) for h in range(HG)]
    UNITS2 = [(t, h, 1) for t in (0, 1) for h in range(HG)] + [(2, 0, 2), (2, 2, 2), (3, 0, 4)]
    UN = len(UNITS1)
    LAG = 2
    LAST_UNIT = [3, 7, 9, 10]
    STEPS = UN + LAG
    QSCALE = float(DK) ** -0.5
    with ExitStack() as ctx:
        m = Mem(nc, ctx, "at_")
        wqkv = m.sb("wqkv", [P, KD, 3 * D])
        wo = m.sb("wo", [P, KD, D])
        identb = m.sb("identb", [P, P], BF16)
        maskq = m.sb("maskq", [P, P], BF16)
        maskk = m.sb("maskk", [P, P], BF16)
        x1 = m.sb("x1", [P, 2, CT, D])
        yg = m.sb("yg", [P, CT, TOPK, D])
        idx = m.sb("idx", [P, CT * TOPK], U32)
        xn = m.sb("xn", [P, CT, D])
        xnT = m.sb("xnT", [P, KD, CHUNK])
        qk = m.sb("qk", [P, CT, 2 * D])
        va = m.sb("va", [P, 2, CT, H, 32])
        q4 = m.sb("q4", [P, 2, CT, HG, SL], F32R)
        k4 = m.sb("k4", [P, 2, CT, HG, SL], F32R)
        identr = m.sb("identr", [P, P], F32R)
        qT = m.sb("qT", [P, 2, HG, CHUNK], F32R)
        kT = m.sb("kT", [P, NG, HG // 2, CHUNK], F32R)
        q2T = m.sb("q2T", [P, 2, HG, CHUNK], F32R)
        pT = m.sb("pT", [P, 8, CHUNK])
        oT = m.sb("oT", [P, CHUNK])
        rec = m.sb("rec", [P, CT, HG])
        attn = m.sb("attn", [P, CT, D])
        attnT = m.sb("attnT", [P, KD, CHUNK])
        xres = m.sb("xres", [P, CT, D])
        xn2 = m.sb("xn2", [P, CT, D])
        xnT2 = m.sb("xnT2", [P, KD, CHUNK])
        stat = m.sb("stat", [P, 2, CT, 6])
        mv = m.sb("mv", [P, 2, CT, 2])
        veps = m.sb("veps", [P, 2, CT])
        rstd = m.sb("rstd", [P, 2, CT])
        ps1 = [m.ps(f"ps1_{i}", [P, 512]) for i in range(2)]
        ps2 = [m.ps(f"ps2_{i}", [P, 512]) for i in range(2)]
        psO = m.ps("psO", [P, 512])
        psG = m.ps("psG", [P, 2, 512])
        psM = m.ps("psM", [P, 512])

        w_in = m.sem("w_in")
        made = m.sem("made")
        identr_in = m.sem("identr_in")
        consts = m.sem("consts")
        x1_ld = m.sems("x1_ld", 2)
        y_ld = m.sem("y_ld")
        idx_in = m.sem("idx_in")
        x1_mid = m.sem("x1_mid")
        x1_done = m.sem("x1_done")
        x1_st = m.sems("x1_st", 2)
        st = m.sem("st")
        var1 = m.sem("var1")
        eps1 = m.sem("eps1")
        rs1 = m.sem("rs1")
        normed1 = m.sem("normed1")
        g_full = m.sem("g_full")
        g_free = m.sem("g_free")
        hi_done = m.sem("hi_done")
        lo_done = m.sem("lo_done")
        s1_done = m.sem("s1_done")
        mx_done = m.sem("mx_done")
        s2_done = m.sem("s2_done")
        ex_done = m.sem("ex_done")
        pv_done = m.sem("pv_done")
        o_ev = m.sem("o_ev")
        rc = m.sem("rc")
        m_full = m.sem("m_full")
        m_free = m.sem("m_free")
        xr_ld = m.sem("xr_ld")
        var2 = m.sem("var2")
        eps2 = m.sem("eps2")
        rs2 = m.sem("rs2")
        normed2 = m.sem("normed2")
        x2_st = m.sem("x2_st")
        xn2_st = m.sem("xn2_st")
        xnT2_st = m.sem("xnT2_st")
        held = m.sem("held")
        block = ctx.enter_context(nc.Block())

        def g_uses(c, gr):
            has_last, has_next = c != 0, c != NB_ - 1
            names = []
            if gr == 0 and has_last:
                names.append("attnT")
            if gr == 1 and has_next:
                names += [f"proj{t}" for t in range(CT)]
            if gr == 2 and has_last:
                names.append("x2T")
            if gr < 2 or has_next:
                names += [f"TQ_{gr}", f"TK_{gr}"]
            if gr == 0 and has_next:
                names.append("xnT")
            if gr < NG - 1 or has_next:
                names.append(f"T2_{gr}")
            return names

        def g_batch(c):
            return sum((g_uses(c, gr) for gr in range(NG)), [])

        FIRST_G = ["xnT"] + [f"proj{t}" for t in range(CT)] + ["TQ_0", "TK_0", "TQ_1", "TK_1", "T2"]
        PER_G = len(g_batch(1))

        def g_base(c, kind):
            if kind == 0:
                return len(FIRST_G)
            return c * PER_G + (len(FIRST_G) + len(g_batch(0)) - PER_G)

        def g_before(c, kind, gr):
            return g_base(c, kind) + sum(len(g_uses(kind, i)) for i in range(gr))

        def gu(c, kind, name):
            if kind == "first":
                return FIRST_G.index(name)
            if kind == "end":
                return g_base(NB_ - 1, NB_ - 1) + len(g_batch(NB_ - 1)) + ["attnT", "x2T"].index(name)
            return g_base(c, kind) + g_batch(kind).index(name)

        M_FIRST = ["OT_0", "OT_1", "OT_2"]
        M_USES = ["OT_3"] + [f"out{t}" for t in range(CT)] + ["OT_0", "OT_1", "rt", "OT_2"]
        M_END = ["OT_3"] + [f"out{t}" for t in range(CT)] + ["rt"]

        def mu(c, kind, name):
            if kind == 0:
                return M_FIRST.index(name)
            return c * len(M_USES) + (len(M_FIRST) - len(M_USES) + M_USES.index(name))

        def mu_end(name):
            return len(M_FIRST) + len(M_USES) * (NB_ - 1) + M_END.index(name)


        VALUES_AT = [LAG + 5, LAG + 9, STEPS - 1]
        AT = dict(attnT=5, x2T=3, xnT=11, T2=STEPS - 1)
        PROJECT_AT = [2, 3, 5, 6]

        def turns(gr, n):
            q, k = {0: (7, 9), 1: (8, 10)}.get(gr, (6, 9))
            return "TQ" if n == q else "TK" if n == k else None

        def phases(eng, first, phase, last):
            first()
            for u in range(2):
                for gr in range(NG):
                    phase(u, 0, u, u, gr)
            with eng.Fori(1, NB_ // 2 - 1) as c2:
                for u in range(2):
                    for gr in range(NG):
                        phase(c2 * 2 + u, c2, u, 2, gr)
            for u in range(2):
                for gr in range(NG):
                    phase(NB_ - 2 + u, NB_ // 2 - 1, u, 2 if u == 0 else NB_ - 1, gr)
            last()

        def rows(ap, c):
            return ap[bass.ds(c * CHUNK, CHUNK), :].rearrange("(t p) d -> p t d", p=P)

        @block.sync
        def _(sp):
            for i, w in enumerate((dram.W_q, dram.W_k, dram.W_v)):
                sp.dma_start(wqkv[:, :, i * D:(i + 1) * D], w.rearrange("(k p) n -> p k n", p=P)).then_inc(w_in, 16)
            sp.dma_start(wo[:], dram.W_o.rearrange("(k p) n -> p k n", p=P)).then_inc(w_in, 16)

            def hold(sem, value):
                sp.wait_ge(sem, value)
                sp.sem_inc(held, 1)

            def load_x1(c, c2, u, first):
                if not first:
                    hold(x1_st[u], c2 * 16)
                    hold(normed1, c - 1)
                sp.dma_start(x1[:, u], rows(dram.sh, c)).then_inc(x1_ld[u], 16)

            def store_x1(c, u):
                hold(x1_done, c + 1)
                sp.dma_start(rows(dram.x1, c), x1[:, u]).then_inc(x1_st[u], 16)

            def load_res(c, c2, u, first):
                hold(x1_st[u], c2 * 16 + 16)
                if not first:
                    hold(x2_st, c * 16)
                    hold(normed2, c)
                sp.dma_start(xres[:], rows(dram.x1, c)).then_inc(xr_ld, 16)

            def store_x2(c):
                hold(var2, c + 1)
                sp.dma_start(rows(dram.x2, c), xres[:]).then_inc(x2_st, 16)
                hold(normed2, c + 1)
                sp.dma_start(rows(dram.xn, c), xn2[:]).then_inc(xn2_st, 16)

            def store_x2T(c, done):
                hold(g_free, done)
                sp.dma_start(dram.xnT[:, :, bass.ds(c * CHUNK, CHUNK)], xnT2[:]).then_inc(xnT2_st, 16)

            def first():
                load_x1(0, 0, 0, True)
                load_x1(1, 0, 1, True)
                store_x1(0, 0)
                load_res(0, 0, 0, True)

            def phase(c, c2, u, kind, gr):
                if gr == 0 and kind != NB_ - 1:
                    store_x1(c + 1, 1 - u)
                if gr == 1 and kind != 0:
                    store_x2(c - 1)
                    load_res(c, c2, u, False)
                if gr == 2 and kind != 0:
                    store_x2T(c - 1, gu(c, kind, "x2T") + 2)
                if gr == 2 and (kind in (0, 1) or (kind == 2 and not isinstance(c, int))):
                    load_x1(c + 2, c2 + 1, u, False)

            def last():
                store_x2(NB_ - 1)
                store_x2T(NB_ - 1, gu(0, "end", "x2T") + 2)
                sp.wait_ge(x2_st, 16 * NB_)
                sp.wait_ge(xn2_st, 16 * NB_ + 16)
                sp.wait_ge(xnT2_st, 16 * NB_ + 16)
                for u in range(2):
                    sp.wait_ge(x1_st[u], 16 * (NB_ // 2))

            phases(sp, first, phase, last)

        @block.gpsimd
        def _(pool):
            n = [0]

            def done(ins):
                n[0] += 1
                ins.then_inc(made, 1)
                pool.wait_ge(made, n[0])

            p = nc.gpsimd
            done(p.memset(identb[:], 0.0))
            done(p.affine_select(out=identb[:], in_=identb[:], compare_op=ALU.not_equal, fill=1.0,
                                 base=0, pattern=[[-1, P]], channel_multiplier=1))
            done(p.memset(maskq[:], 0.0))
            done(p.affine_select(out=maskq[:], in_=maskq[:], compare_op=ALU.is_ge, fill=MASK,
                                 base=0, pattern=[[-1, P]], channel_multiplier=1))
            done(p.memset(maskk[:], 0.0))
            done(p.affine_select(out=maskk[:], in_=maskk[:], compare_op=ALU.is_ge, fill=MASK,
                                 base=0, pattern=[[1, P]], channel_multiplier=-1))
            done(p.memset(va[:], 0.0))
            done(p.memset(va[:, :, :, :, DK], 1.0))
            done(p.memset(qT[:].bitcast(F32), 0.0))
            done(p.memset(q2T[:].bitcast(F32), 0.0))
            done(p.memset(q4[:].bitcast(F32), 0.0))
            done(p.memset(k4[:].bitcast(F32), 0.0))
            done(p.memset(k4[:, :, :, :, 3 * DK].bitcast(F32), 1.0))
            pool.sem_inc(consts, 1)

            def gather(c, tiles, first):
                if tiles[0] == 0:
                    if not first:
                        pool.wait_ge(x1_done, c)
                    p.tensor_copy(idx[:], g.slot[:, bass.ds(c * (CT * TOPK), CT * TOPK)]).then_inc(idx_in, 1)
                    pool.wait_ge(idx_in, c + 1)
                    pool.sem_inc(held, 1)
                for t in tiles:
                    for k in range(TOPK):
                        p.indirect_dma_start(
                            yg[:, t, k, :], None, dram.ys,
                            bass.IndirectOffsetOnAxis(ap=idx[:, TOPK * t + k:TOPK * t + k + 1], axis=0)
                        ).then_inc(y_ld, 16)

            def deviation(i, c, var, eps, rs):
                pool.wait_ge(var, c + 1)
                p.tensor_tensor(veps[:, i, :], mv[:, i, :, 1], g.eps[:, 0:CT], ALU.add).then_inc(eps, 1)
                pool.wait_ge(eps, c + 1)
                p.tensor_tensor(rstd[:, i, :], veps[:, i, :], g.mhalf[:, 0:CT], ALU.pow).then_inc(rs, 1)

            def low(G, gr):
                pool.wait_ge(hi_done, G + 1)
                pool.sem_inc(held, 1)
                s = gr % 2
                q, k = (qk[:, :, i * D + gr * HG * DK:i * D + (gr + 1) * HG * DK]
                        .rearrange("p t (h d) -> p t h d", d=DK) for i in range(2))
                p.tensor_copy(q4[:, s, :, :, DK:2 * DK], q4[:, s, :, :, 0:DK])
                p.tensor_copy(k4[:, s, :, :, 2 * DK:3 * DK], k4[:, s, :, :, 0:DK])
                p.tensor_tensor(q4[:, s, :, :, 2 * DK:3 * DK], q, q4[:, s, :, :, 0:DK], ALU.subtract)
                p.tensor_tensor(k4[:, s, :, :, DK:2 * DK], k, k4[:, s, :, :, 0:DK], ALU.subtract
                                ).then_inc(lo_done, 1)

            def first():
                gather(0, range(CT), True)
                deviation(0, 0, var1, eps1, rs1)
                low(0, 0)
                low(1, 1)
                gather(1, range(CT), False)

            def phase(c, c2, u, kind, gr):
                if gr < 2 or kind != NB_ - 1:
                    low(c * NG + (gr + 2), (gr + 2) % NG)
                if gr == 0 and kind != NB_ - 1:
                    deviation(0, c + 1, var1, eps1, rs1)
                if gr == 1 and kind != 0:
                    deviation(1, c - 1, var2, eps2, rs2)
                more = kind in (0, 1) or (kind == 2 and not isinstance(c, int))
                if gr == 1 and more:
                    gather(c + 2, range(0, 2), False)
                if gr == 2 and more:
                    gather(c + 2, range(2, 4), False)

            def last():
                deviation(1, NB_ - 1, var2, eps2, rs2)

            phases(pool, first, phase, last)

        @block.scalar
        def _(act):
            act.sem_inc(g_free, 1)
            act.sem_inc(ex_done, 2)
            act.sem_inc(xnT2_st, 16)
            act.wait_ge(consts, 1)
            s_ = nc.scalar
            s_.copy(identr[:], g.ident[:]).then_inc(identr_in, 1)

            def out_of_g(i, dst, src=psG):
                act.wait_ge(g_full, i + 1)
                s_.copy(dst, src[:]).then_inc(g_free, 1)

            def queries_out_of_g(i, dst, n):
                act.wait_ge(g_full, i + 1)
                for half in range(2):
                    a = half * SL
                    ins = s_.copy(dst.rearrange("p (k h) n -> p k h n", h=2)[a:a + n, :, half, :], psG[a:a + n])
                ins.then_inc(g_free, 1)

            def project(i0, t, u, lo):
                if t == 0 and lo is not None:
                    act.wait_ge(lo_done, lo)
                    act.sem_inc(held, 1)
                act.wait_ge(g_full, i0 + (t + 1))
                s_.mul(qk[:, t, 0:D], psG[:, 0, 0:D], QSCALE)
                s_.copy(qk[:, t, D:2 * D], psG[:, 0, D:2 * D])
                s_.copy(va[:, u, t, :, 0:DK], psG[:, 1, 0:D].rearrange("p (h d) -> p h d", d=DK)
                        ).then_inc(g_free, 1)

            def high(G, gr, waited):
                act.wait_ge(g_free, waited)
                s = gr % 2
                for dst, i in ((q4, 0), (k4, 1)):
                    ins = s_.copy(dst[:, s, :, :, 0:DK], qk[:, :, i * D + gr * HG * DK:i * D + (gr + 1) * HG * DK]
                                  .rearrange("p t (h d) -> p t h d", d=DK))
                ins.then_inc(hi_done, 1)

            def first():
                out_of_g(gu(0, "first", "xnT"), xnT[:])
                for t in range(CT):
                    project(gu(0, "first", "proj0"), t, 0, None)
                high(0, 0, gu(0, "first", f"proj{CT - 1}") + 2)
                high(1, 1, gu(0, "first", f"proj{CT - 1}") + 2)
                for k in range(2):
                    queries_out_of_g(gu(0, "first", f"TQ_{k}"), qT[:, k], 3 * DK)
                    out_of_g(gu(0, "first", f"TK_{k}"), kT[:, k])
                queries_out_of_g(gu(0, "first", "T2"), q2T[:, 0], SL)

            def phase(c, c2, u, kind, gr):
                G = c * NG + gr
                more = gr < 2 or kind != NB_ - 1
                for n in range(STEPS):
                    if n == 0 and more:
                        high(G + 2, (gr + 2) % NG, g_before(c, kind, gr) + 1)
                    if n >= LAG:
                        k = n - LAG
                        ki, h, heads = UNITS2[k]
                        act.wait_ge(s2_done, G * UN + (k + 1))
                        act.wait_ge(pv_done, G * CT + (ki + 1))
                        w = CHUNK - ki * P
                        s = (ki * HG + h) % 8
                        s_.activation(pT[:, s:s + heads, 0:w], ps2[(gr + k) % 2][:, 0:heads * w]
                                      .rearrange("p (h w) -> p h w", h=heads), ACT.Exp).then_inc(ex_done, 1)
                    if gr == 0 and n == AT["attnT"] and kind != 0:
                        out_of_g(gu(c, kind, "attnT"), attnT[:])
                    if gr == 2 and n == AT["x2T"] and kind != 0:
                        turned2(c - 1, gu(c, kind, "x2T"))
                    if gr == 1 and n in PROJECT_AT and kind != NB_ - 1:
                        project(gu(c, kind, "proj0"), PROJECT_AT.index(n), 1 - u, c * NG + 4)
                    if turns(gr, n) == "TQ" and more:
                        queries_out_of_g(gu(c, kind, f"TQ_{gr}"), qT[:, gr % 2], 3 * DK)
                    if turns(gr, n) == "TK" and more:
                        out_of_g(gu(c, kind, f"TK_{gr}"), kT[:, (gr + 2) % NG])
                    if gr == 0 and n == AT["xnT"] and kind != NB_ - 1:
                        out_of_g(gu(c, kind, "xnT"), xnT[:])
                    if n == AT["T2"] and not (kind == NB_ - 1 and gr == NG - 1):
                        queries_out_of_g(gu(c, kind, f"T2_{gr}"), q2T[:, (gr + 1) % 2], SL)

            def turned2(c, i):
                act.wait_ge(xnT2_st, c * 16 + 16)
                out_of_g(i, xnT2[:])

            def last():
                out_of_g(gu(0, "end", "attnT"), attnT[:])
                turned2(NB_ - 1, gu(0, "end", "x2T"))

            phases(act, first, phase, last)

        @block.vector
        def _(dve):
            dve.sem_inc(mx_done, 2)
            dve.sem_inc(o_ev, 1)
            dve.sem_inc(m_free, 1)
            dve.sem_inc(xn2_st, 16)
            dve.wait_ge(consts, 1)
            v = nc.vector

            def combine(c, c2, u, tiles):
                for t in tiles:
                    if t == 0:
                        dve.wait_ge(x1_ld[u], c2 * 16 + 16)
                        dve.wait_ge(y_ld, c * (16 * CT * TOPK) + 16 * CT * TOPK)
                    v.scalar_tensor_tensor(x1[:, u, t, :], yg[:, t, 0, :], g.gate[:, bass.ds(c * CT + t, 1), 0],
                                           x1[:, u, t, :], ALU.mult, ALU.add).then_inc(x1_mid, 1)
                for t in tiles:
                    dve.wait_ge(x1_mid, c * CT + (t + 1))
                    ins = v.scalar_tensor_tensor(x1[:, u, t, :], yg[:, t, 1, :], g.gate[:, bass.ds(c * CT + t, 1), 1],
                                                 x1[:, u, t, :], ALU.mult, ALU.add)
                    if t == CT - 1:
                        ins.then_inc(x1_done, 1)

            def moments(i, src, wait, count, var):
                if wait is not None:
                    dve.wait_ge(*wait)
                for t in range(CT):
                    v.bn_stats(stat[:, i, t, :], src[:, t, :]).then_inc(st, 1)
                dve.wait_ge(st, count + CT)
                dve.sem_inc(held, 1)
                for t in range(CT):
                    ins = v.bn_aggr(mv[:, i, t, :], stat[:, i, t, :])
                ins.then_inc(var, 1)

            def normalize(i, dst, src, wait, done):
                dve.wait_ge(*wait)
                for t in range(CT):
                    ins = v.tensor_scalar(dst[:, t, :], src[:, t, :], mv[:, i, t, 0:1], rstd[:, i, t:t + 1],
                                          ALU.subtract, ALU.mult)
                ins.then_inc(done, 1)

            def maxima(G, gr, n):
                qi, h, heads = UNITS1[n]
                dve.wait_ge(s1_done, G * UN + (n + 1))
                w = (qi + 1) * P
                v.tensor_reduce(q4[:, gr % 2, qi, h:h + heads, 3 * DK:3 * DK + 1],
                                ps1[(gr + n) % 2][:, 0:heads * w].rearrange("p (h w) -> p h w", h=heads), AX.X,
                                ALU.max, negate=True).then_inc(mx_done, 1)

            def copy_o(G):
                dve.wait_ge(pv_done, G * CT + (CT + 2))
                v.tensor_copy(oT[:], psO[:]).then_inc(o_ev, 1)

            def divide(G, gr, i):
                dve.wait_ge(m_full, i + 1)
                o = psM[:].rearrange("p (t h w) -> p t h w", t=CT, h=HG)
                v.reciprocal(rec[:], o[:, :, :, DK]).then_inc(rc, 1)
                dve.wait_ge(rc, G + 1)
                for t in range(CT):
                    ins = v.tensor_tensor(attn[:, t, gr * HG * DK:(gr + 1) * HG * DK].rearrange("p (h d) -> p h d", d=DK),
                                          o[:, t, :, 0:DK],
                                          rec[:, t, :].rearrange("p (h o) -> p h o", o=1).to_broadcast([P, HG, DK]),
                                          ALU.mult)
                ins.then_inc(m_free, 1)

            def residual(c, i0):
                dve.wait_ge(xr_ld, c * 16 + 16)
                for t in range(CT):
                    dve.wait_ge(m_full, i0 + (t + 1))
                    v.tensor_tensor(xres[:, t, :], xres[:, t, :], psM[:, 0:D], ALU.add).then_inc(m_free, 1)

            def logits(c, i):
                dve.wait_ge(m_full, i + 1)
                v.tensor_copy(g.logits[:, bass.ds(c * (CT * E), CT * E)], psM[:, 0:CT * E]).then_inc(m_free, 1)

            def first():
                combine(0, 0, 0, range(CT))
                moments(0, x1[:, 0], (x1_done, 1), 0, var1)
                normalize(0, xn, x1[:, 0], (rs1, 1), normed1)
                for n in range(UN):
                    maxima(0, 0, n)

            def phase(c, c2, u, kind, gr):
                G = c * NG + gr
                nxt = not (kind == NB_ - 1 and gr == NG - 1)
                before = CT if kind == 0 else c * (2 * CT)
                for n in range(UN):
                    if nxt:
                        maxima(G + 1, (gr + 1) % NG, n)
                    if n == 2 and not (kind == 0 and gr == 0):
                        copy_o(G - 1)
                    if n == 5 and not (kind == 0 and gr == 0):
                        divide(G - 1, (gr - 1) % NG, mu(c, kind, f"OT_{(gr - 1) % NG}"))
                    if gr == 0 and kind != NB_ - 1:
                        un, c2n = 1 - u, (c2 if u == 0 else c2 + 1)
                        if n == 4:
                            combine(c + 1, c2n, un, range(0, 2))
                        if n == 6:
                            combine(c + 1, c2n, un, range(2, 4))
                        if n == 7:
                            moments(0, x1[:, un], (x1_done, c + 2), before, var1)
                        if n == 9:
                            normalize(0, xn, x1[:, un], (rs1, c + 2), normed1)
                    if gr == 0 and n == 10 and kind != 0:
                        residual(c - 1, mu(c, kind, "out0"))
                    if gr == 1 and n == 0 and kind != 0:
                        moments(1, xres, (m_free, mu(c, kind, f"out{CT - 1}") + 2),
                                before + (0 if kind == NB_ - 1 else CT), var2)
                    if gr == 1 and n == 2 and kind != 0:
                        dve.wait_ge(xn2_st, c * 16)
                        dve.sem_inc(held, 1)
                        normalize(1, xn2, xres, (rs2, c), normed2)
                    if gr == 2 and n == 7 and kind != 0:
                        logits(c - 1, mu(c, kind, "rt"))

            def last():
                c = NB_
                copy_o(NB_ * NG - 1)
                divide(NB_ * NG - 1, NG - 1, mu_end("OT_3"))
                residual(c - 1, mu_end("out0"))
                moments(1, xres, (m_free, mu_end(f"out{CT - 1}") + 2), (2 * NB_ - 1) * CT, var2)
                dve.wait_ge(xn2_st, c * 16)
                normalize(1, xn2, xres, (rs2, c), normed2)
                logits(c - 1, mu_end("rt"))

            phases(dve, first, phase, last)

        @block.tensor
        def _(pe):
            pe.sem_inc(pv_done, 2)
            pe.wait_ge(consts, 1)
            pe.wait_ge(w_in, 64)
            pe.wait_ge(identr_in, 1)

            def turn(i, src, ident=g.ident, out=psG):
                pe.wait_ge(g_free, i + 1)
                for t in range(CT):
                    for k in range(2):
                        ins = pe.transpose(out[:, k, t * P:(t + 1) * P], src(t, k), ident[:, :])
                ins.then_inc(g_full, 1)

            def turn_parts(i, parts):
                turn(i, lambda t, k: parts[:, t, 2 * k:2 * k + 2, :].rearrange("p h s -> p (h s)"),
                     identr, psG[:].bitcast(F32R))

            def project(i0, t):
                pe.wait_ge(g_free, i0 + (t + 1))
                for half, lo, w in ((0, 0, 2 * D), (1, 2 * D, D)):
                    for k in range(KD):
                        ins = pe.matmul(psG[:, half, 0:w], xnT[:, k, t * P:(t + 1) * P], wqkv[:, k, lo:lo + w],
                                        start=(k == 0), stop=(k == KD - 1))
                ins.then_inc(g_full, 1)

            def score1(G, gr, n, ready):
                qi, h0, heads = UNITS1[n]
                if n == 0:
                    pe.wait_ge(g_free, ready)
                pe.wait_ge(mx_done, G * UN + (n + 1))
                w = (qi + 1) * P
                ps = ps1[(gr + n) % 2]
                for i in range(heads):
                    h = h0 + i
                    pe.matmul(ps[:, i * w:(i + 1) * w], qT[:, gr % 2, h, qi * P:w], kT[:, gr, h // 2, 0:w],
                              start=True, stop=False)
                    ins = pe.matmul(ps[:, i * w + qi * P:(i + 1) * w], identb[:, :], maskq[:, :],
                                    start=False, stop=True)
                ins.then_inc(s1_done, 1)

            def score2(G, gr, n):
                ki, h0, heads = UNITS2[n]
                pe.wait_ge(ex_done, G * UN + (n + 1))
                w = CHUNK - ki * P
                ps = ps2[(gr + n) % 2]
                for i in range(heads):
                    h = h0 + i
                    pe.matmul(ps[:, i * w:(i + 1) * w], kT[:, gr, h // 2, ki * P:(ki + 1) * P],
                              q2T[:, gr % 2, h, ki * P:CHUNK], start=True, stop=False)
                    ins = pe.matmul(ps[:, i * w:i * w + P], identb[:, :], maskk[:, :], start=False, stop=True)
                ins.then_inc(s2_done, 1)

            def values(G, gr, u, ki):
                if ki == 0:
                    pe.wait_ge(o_ev, G + 1)
                pe.wait_ge(ex_done, G * UN + (LAST_UNIT[ki] + 3))
                w = CHUNK - ki * P
                for h in range(HG):
                    ins = pe.matmul(psO[32 * h:32 * h + 32, ki * P:CHUNK], va[:, u, ki, gr * HG + h, :],
                                    pT[:, (ki * HG + h) % 8, 0:w], start=(ki == 0), stop=(ki == CT - 1),
                                    skip_group_check=True)
                ins.then_inc(pv_done, 1)

            def turn_o(G, i):
                pe.wait_ge(o_ev, G + 2)
                pe.wait_ge(m_free, i + 1)
                for t in range(CT):
                    ins = pe.transpose(psM[:, t * P:(t + 1) * P], oT[:, t * P:(t + 1) * P], g.ident[:, :])
                ins.then_inc(m_full, 1)

            def turn_attn(i, mi):
                pe.wait_ge(m_free, mi + 2)
                turn(i, lambda t, k: attn[:, t, k * P:(k + 1) * P])

            def project_out(i0, ready):
                pe.wait_ge(g_free, ready)
                for t in range(CT):
                    pe.wait_ge(m_free, i0 + (t + 1))
                    for k in range(KD):
                        ins = pe.matmul(psM[:, 0:D], attnT[:, k, t * P:(t + 1) * P], wo[:, k, :],
                                        start=(k == 0), stop=(k == KD - 1))
                    ins.then_inc(m_full, 1)

            def route(i, ready):
                pe.wait_ge(g_free, ready)
                pe.wait_ge(m_free, i + 1)
                for t in range(CT):
                    for k in range(KD):
                        ins = pe.matmul(psM[:, t * E:(t + 1) * E], xnT2[:, k, t * P:(t + 1) * P], g.rw[:, k, :],
                                        start=(k == 0), stop=(k == KD - 1))
                ins.then_inc(m_full, 1)

            def first():
                pe.wait_ge(normed1, 1)
                turn(gu(0, "first", "xnT"), lambda t, k: xn[:, t, k * P:(k + 1) * P])
                for t in range(CT):
                    project(gu(0, "first", "proj0"), t)
                for k in range(2):
                    pe.wait_ge(lo_done, k + 1)
                    turn_parts(gu(0, "first", f"TQ_{k}"), q4[:, k])
                    turn_parts(gu(0, "first", f"TK_{k}"), k4[:, k])
                for n in range(UN):
                    score1(0, 0, n, gu(0, "first", "TK_0") + 2)
                pe.wait_ge(mx_done, UN + 2)
                turn_parts(gu(0, "first", "T2"), q4[:, 0])

            def phase(c, c2, u, kind, gr):
                G = c * NG + gr
                more = gr < 2 or kind != NB_ - 1
                nxt = not (kind == NB_ - 1 and gr == NG - 1)
                started = not (kind == 0 and gr == 0)
                for n in range(STEPS):
                    if nxt and n < UN:
                        score1(G + 1, (gr + 1) % NG, n, g_before(c, kind, gr))
                    if n == 1 and started:
                        values(G - 1, (gr - 1) % NG, u if gr else 1 - u, CT - 1)
                    if n == LAG:
                        pe.wait_ge(g_free, g_before(c, kind, gr) + 1)
                    if n >= LAG:
                        score2(G, gr, n - LAG)
                    if n == 4 and started:
                        turn_o(G - 1, mu(c, kind, f"OT_{(gr - 1) % NG}"))
                    if n in VALUES_AT:
                        values(G, gr, u, VALUES_AT.index(n))
                    if gr == 0 and n == AT["attnT"] and kind != 0:
                        turn_attn(gu(c, kind, "attnT"), mu(c, kind, "OT_3"))
                    if gr == 2 and n == AT["x2T"] and kind != 0:
                        pe.wait_ge(normed2, c)
                        turn(gu(c, kind, "x2T"), lambda t, k: xn2[:, t, k * P:(k + 1) * P])
                    if gr == 1 and n in PROJECT_AT and kind != NB_ - 1:
                        project(gu(c, kind, "proj0"), PROJECT_AT.index(n))
                    if gr == 2 and n == 6 and kind != 0:
                        route(mu(c, kind, "rt"), gu(c, kind, "x2T") + 2)
                    if turns(gr, n) == "TQ" and more:
                        pe.wait_ge(lo_done, G + 3)
                        turn_parts(gu(c, kind, f"TQ_{gr}"), q4[:, gr % 2])
                    if turns(gr, n) == "TK" and more:
                        turn_parts(gu(c, kind, f"TK_{gr}"), k4[:, gr % 2])
                    if gr == 0 and n == 10 and kind != 0:
                        project_out(mu(c, kind, "out0"), gu(c, kind, "attnT") + 2)
                    if gr == 0 and n == AT["xnT"] and kind != NB_ - 1:
                        pe.wait_ge(normed1, c + 2)
                        turn(gu(c, kind, "xnT"), lambda t, k: xn[:, t, k * P:(k + 1) * P])
                    if n == AT["T2"] and nxt:
                        pe.wait_ge(mx_done, G * UN + (2 * UN + 2))
                        turn_parts(gu(c, kind, f"T2_{gr}"), q4[:, (gr + 1) % 2])

            def last():
                values(NB_ * NG - 1, NG - 1, 1, CT - 1)
                turn_o(NB_ * NG - 1, mu_end("OT_3"))
                turn_attn(gu(0, "end", "attnT"), mu_end("OT_3"))
                project_out(mu_end("out0"), gu(0, "end", "attnT") + 2)
                pe.wait_ge(normed2, NB_)
                turn(gu(0, "end", "x2T"), lambda t, k: xn2[:, t, k * P:(k + 1) * P])
                route(mu_end("rt"), gu(0, "end", "x2T") + 2)

            phases(pe, first, phase, last)


def macaron_kernel(nc, x, W_q, W_k, W_v, W_o, router_w, expert_bias, shared_w1, shared_w2, shared_w3,
                   routed_w1, routed_w2, routed_w3, out):
    assert shared_w1.shape[0] == 1
    z = Shapes(x, router_w, shared_w1[0], routed_w1)
    dram = scratch(nc, z)
    dram.router_w, dram.expert_bias = router_w, expert_bias
    dram.shared_w1, dram.shared_w2, dram.shared_w3 = shared_w1[0], shared_w2[0], shared_w3[0]
    dram.routed_w1, dram.routed_w2, dram.routed_w3 = routed_w1, routed_w2, routed_w3
    dram.W_q, dram.W_k, dram.W_v, dram.W_o = W_q, W_k, W_v, W_o
    x_flat = x.rearrange("b s d -> (b s) d")
    with ExitStack() as ctx:
        g = residents(nc, z, ctx)
        setup(nc, z, g, dram)
        norm_first(nc, z, g, dram, x_flat)
        feed_forward(nc, z, g, dram, "f1_", x_flat)
        attention(nc, z, g, dram)
        feed_forward(nc, z, g, dram, "f2_", dram.x2)
        combine_last(nc, z, g, dram, out.rearrange("b s d -> (b s) d"))


_INS = ['L0_attn_x', 'L0_attn_W_q', 'L0_attn_W_k', 'L0_attn_W_v', 'L0_attn_W_o', 'L0_ffn_router_w',
        'L0_ffn_expert_bias', 'L0_ffn_shared_w1', 'L0_ffn_shared_w2', 'L0_ffn_shared_w3', 'L0_ffn_routed_w1',
        'L0_ffn_routed_w2', 'L0_ffn_routed_w3']
_TURNED = ('L0_attn_W_q', 'L0_attn_W_k', 'L0_attn_W_v', 'L0_attn_W_o')


def kernel(**inputs):
    import numpy as _np
    import concourse.bacc as _bacc
    from concourse import mybir as _mybir
    from concourse.bass_utils import run_bass_kernel_spmd as _run

    nc = _bacc.Bacc("TRN2", target_bir_lowering=False, num_devices=1)
    arrays, args = {}, []
    for name in _INS:
        a = _np.asarray(inputs[name])
        a = _np.ascontiguousarray(a.T if name in _TURNED else a)
        arrays[f"in_{name}_dram"] = a
        args.append(nc.dram_tensor(f"in_{name}_dram", a.shape, _mybir.dt.from_np(a.dtype), kind="ExternalInput").ap())
    out = nc.dram_tensor("out_0_dram", args[0].shape, _mybir.dt.float32, kind="ExternalOutput").ap()
    macaron_kernel(nc, *args, out)
    r = _run(nc, [arrays], core_ids=[0])
    return r.results[0]["out_0_dram"]
```

```python
import math
from contextlib import ExitStack

import concourse.bass as bass
from concourse import mybir

P = 128
F32 = mybir.dt.float32
F32R = mybir.dt.float32r
BF16 = mybir.dt.bfloat16
I32 = mybir.dt.int32
U32 = mybir.dt.uint32
ALU = mybir.AluOpType
ACT = mybir.ActivationFunctionType
AX = mybir.AxisListType

CT = 4
CHUNK = CT * P
EPS = 1e-5
TOPK = 2


class Shapes:

    def __init__(self, x, router_w, shared_w1, routed_w1):
        self.B, self.S, self.D = x.shape
        self.T = self.B * self.S
        self.NT = self.T // P
        self.NC = self.T // CHUNK
        self.KD = self.D // P
        self.E = router_w.shape[1]
        self.RH = routed_w1.shape[2]
        self.KR = self.RH // P
        self.SH = shared_w1.shape[-1]
        self.JS = self.SH // P
        most = (self.T * TOPK + self.E * (P - 1)) // P
        self.NB = -(-most // 4) * 4
        assert self.S == CHUNK and self.D % P == 0 and self.RH == self.D


class Mem:

    def __init__(self, nc, ctx, tag=""):
        self.nc, self.ctx, self.tag = nc, ctx, tag

    def sb(self, name, shape, dt=F32):
        return self.ctx.enter_context(self.nc.sbuf_tensor(self.tag + name, shape, dt))

    def ps(self, name, shape, dt=F32):
        return self.ctx.enter_context(self.nc.psum_tensor(self.tag + name, shape, dt))

    def sem(self, name):
        return self.nc.alloc_semaphore(self.tag + name)

    def sems(self, name, n):
        return [self.sem(f"{name}{i}") for i in range(n)]


def setup(nc, z, g, dram):
    with ExitStack() as ctx:
        m = Mem(nc, ctx, "set_")
        made = m.sem("made")
        loaded = m.sem("loaded")
        block = ctx.enter_context(nc.Block())
        KD, E = z.KD, z.E

        @block.gpsimd
        def _(pool):
            n = [0]

            def done(ins):
                n[0] += 1
                ins.then_inc(made, 1)
                pool.wait_ge(made, n[0])

            done(nc.gpsimd.memset(g.ident[:], 0.0))
            done(nc.gpsimd.affine_select(out=g.ident[:], in_=g.ident[:], compare_op=ALU.not_equal, fill=1.0,
                                         base=0, pattern=[[-1, P]], channel_multiplier=1))
            done(nc.gpsimd.memset(g.before[:], 1.0))
            done(nc.gpsimd.affine_select(out=g.before[:], in_=g.before[:], compare_op=ALU.is_gt, fill=0.0,
                                         base=0, pattern=[[1, P]], channel_multiplier=-1))
            done(nc.gpsimd.memset(g.ones[:], 1.0))
            done(nc.gpsimd.memset(g.zero[:], 0.0))
            done(nc.gpsimd.memset(g.mhalf[:], -0.5))
            done(nc.gpsimd.memset(g.eps[:], EPS))
            done(nc.gpsimd.iota(g.rev_i[:], pattern=[[-1, E]], base=E, channel_multiplier=0))
            done(nc.gpsimd.iota(g.blk_i[:], pattern=[[1, z.NB]], base=0, channel_multiplier=0))
            done(nc.gpsimd.tensor_copy(g.rev[:], g.rev_i[:]))
            done(nc.gpsimd.tensor_copy(g.blk[:], g.blk_i[:]))
            done(nc.gpsimd.memset(g.keep[:], 1.0))
            done(nc.gpsimd.memset(g.keep[:, :, 0:1], 0.0))

        @block.sync
        def _(sp):
            n = 0

            def load(dst, src):
                nonlocal n
                sp.dma_start(dst, src).then_inc(loaded, 16)
                n += 16

            load(g.rw[:], dram.router_w.rearrange("(k p) e -> p k e", p=P))
            load(g.bias[:], dram.expert_bias.rearrange("(o e) -> o e", o=1).to_broadcast([P, E]))
            sp.wait_ge(loaded, n)


def norm_first(nc, z, g, dram, x_src):
    with ExitStack() as ctx:
        m = Mem(nc, ctx, "nf_")
        x = m.sb("x", [P, z.NT * z.D])
        xn = m.sb("xn", [P, 2, CT, z.D])
        xnT = m.sb("xnT", [P, 2, z.KD, CHUNK])
        stat = m.sb("stat", [P, 2, CT, 6])
        mv = m.sb("mv", [P, 2, CT, 2])
        veps = m.sb("veps", [P, 2, CT])
        rstd = m.sb("rstd", [P, 2, CT])
        psT = m.ps("psT", [P, 2, z.KD, CHUNK])
        psL = m.ps("psL", [P, 512])
        x_in = m.sems("x_in", 2)
        stats = m.sem("stats")
        var = m.sem("var")
        eps_in = m.sem("eps_in")
        rs = m.sem("rs")
        normed = m.sem("normed")
        turned = m.sem("turned")
        xnT_in = m.sem("xnT_in")
        logit = m.sem("logit")
        logit_in = m.sem("logit_in")
        xn_out = m.sems("xn_out", 2)
        block = ctx.enter_context(nc.Block())

        @block.sync
        def _(sp):
            def load(c, u):
                sp.dma_start(x[:, bass.ds(c * (CT * z.D), CT * z.D)].rearrange("p (t d) -> p t d", d=z.D),
                             x_src[bass.ds(c * CHUNK, CHUNK), :].rearrange("(t p) d -> p t d", p=P)
                             ).then_inc(x_in[u], 16)

            def store(c, c2, u, more):
                sp.wait_ge(normed, c + 1)
                sp.sem_inc(g.held, 1)
                sp.dma_start(dram.xn[bass.ds(c * CHUNK, CHUNK), :].rearrange("(t p) d -> p t d", p=P), xn[:, u]
                             ).then_inc(xn_out[u], 16)
                if more:
                    sp.wait_ge(x_in[u], c2 * 16 + 32)
                    sp.sem_inc(g.held, 1)
                    load(c + 4, u)
                sp.wait_ge(xnT_in, c + 1)
                sp.sem_inc(g.held, 1)
                sp.dma_start(dram.xnT[:, :, bass.ds(c * CHUNK, CHUNK)], xnT[:, u]).then_inc(xn_out[u], 16)

            load(0, 0)
            load(1, 1)
            for u in range(2):
                sp.wait_ge(x_in[u], 16)
                load(2 + u, u)
            with sp.Fori(0, z.NC // 2 - 2) as c2:
                for u in range(2):
                    store(c2 * 2 + u, c2, u, True)
            for c in range(z.NC - 4, z.NC):
                store(c, c // 2, c % 2, False)
            for u in range(2):
                sp.wait_ge(xn_out[u], 32 * (z.NC // 2))

        @block.vector
        def _(dve):
            def tile(c, t):
                return x[:, bass.ds(c * (CT * z.D) + t * z.D, z.D)]

            def moments(c, c2, u):
                dve.wait_ge(x_in[u], c2 * 16 + 16)
                for t in range(CT):
                    nc.vector.bn_stats(stat[:, u, t, :], tile(c, t)).then_inc(stats, 1)
                dve.wait_ge(stats, c * CT + CT)
                dve.sem_inc(g.held, 1)
                for t in range(CT):
                    ins = nc.vector.bn_aggr(mv[:, u, t, :], stat[:, u, t, :])
                ins.then_inc(var, 1)

            def normalize(c, c2, u, first):
                dve.wait_ge(rs, c + 1)
                if not first:
                    dve.wait_ge(xn_out[u], c2 * 32)
                for t in range(CT):
                    ins = nc.vector.tensor_scalar(xn[:, u, t, :], tile(c, t), mv[:, u, t, 0:1],
                                                  rstd[:, u, t:t + 1], ALU.subtract, ALU.mult)
                ins.then_inc(normed, 1)

            def logits(c):
                dve.wait_ge(logit, c + 1)
                nc.vector.tensor_copy(g.logits[:, bass.ds(c * (CT * z.E), CT * z.E)],
                                      psL[:, 0:CT * z.E]).then_inc(logit_in, 1)

            def chunk(c, c2, u, first):
                moments(c + 1, c2 + u, 1 - u)
                normalize(c, c2, u, first)
                if not first:
                    logits(c - 2)

            moments(0, 0, 0)
            for u in range(2):
                chunk(u, 0, u, True)
            with dve.Fori(1, z.NC // 2 - 1) as c2:
                for u in range(2):
                    chunk(c2 * 2 + u, c2, u, False)
            chunk(z.NC - 2, z.NC // 2 - 1, 0, False)
            normalize(z.NC - 1, z.NC // 2 - 1, 1, False)
            logits(z.NC - 3)
            logits(z.NC - 2)
            logits(z.NC - 1)

        @block.gpsimd
        def _(pool):
            with pool.Fori(0, z.NC // 2) as c2:
                for u in range(2):
                    c = c2 * 2 + u
                    pool.wait_ge(var, c + 1)
                    nc.gpsimd.tensor_tensor(veps[:, u, :], mv[:, u, :, 1], g.eps[:, 0:CT], ALU.add).then_inc(eps_in, 1)
                    pool.wait_ge(eps_in, c + 1)
                    nc.gpsimd.tensor_tensor(rstd[:, u, :], veps[:, u, :], g.mhalf[:, 0:CT], ALU.pow).then_inc(rs, 1)

        @block.tensor
        def _(pe):
            def turn(c, u, first):
                pe.wait_ge(normed, c + 1)
                if not first:
                    pe.wait_ge(xnT_in, c - 1)
                for t in range(CT):
                    for k in range(z.KD):
                        ins = pe.transpose(psT[:, u, k, t * P:(t + 1) * P], xn[:, u, t, k * P:(k + 1) * P],
                                           g.ident[:, :])
                ins.then_inc(turned, 1)

            def route(c, u, first):
                pe.wait_ge(xnT_in, c + 1)
                if not first:
                    pe.wait_ge(logit_in, c)
                for t in range(CT):
                    for k in range(z.KD):
                        ins = pe.matmul(psL[:, t * z.E:(t + 1) * z.E], xnT[:, u, k, t * P:(t + 1) * P],
                                        g.rw[:, k, :], start=(k == 0), stop=(k == z.KD - 1))
                ins.then_inc(logit, 1)

            turn(0, 0, True)
            turn(1, 1, True)
            route(0, 0, True)
            with pe.Fori(1, z.NC // 2) as c2:
                for u in range(2):
                    turn(c2 * 2 + u, u, False)
                    route(c2 * 2 + u - 1, 1 - u, False)
            route(z.NC - 1, 1, False)

        @block.scalar
        def _(act):
            def chunk(c, c2, u, first):
                act.wait_ge(turned, c + 1)
                if not first:
                    act.wait_ge(xn_out[u], c2 * 32)
                    act.wait_ge(logit, c - 1)
                nc.scalar.copy(xnT[:, u], psT[:, u]).then_inc(xnT_in, 1)

            for u in range(2):
                chunk(u, 0, u, True)
            with act.Fori(1, z.NC // 2) as c2:
                for u in range(2):
                    chunk(c2 * 2 + u, c2, u, False)


def feed_forward(nc, z, g, dram, tag, x_src, fill):
    KD, KR, E, NT, RH = z.KD, z.KR, z.E, z.NT, z.RH
    TE = NT * E
    NB, NC = z.NB, z.NC
    with ExitStack() as ctx:
        m = Mem(nc, ctx, tag)
        ew12 = m.sb("ew12", [P, E, KD, 2 * RH])
        ew3 = m.sb("ew3", [P, E, KR, z.D])
        ewf = ew12[:].rearrange("p e k n -> p (e k n)")
        used = [0]

        def early(shape):
            at, n = used[0], math.prod(shape)
            used[0] += n
            axes = dict(zip("abc", shape))
            names = " ".join(axes)
            return ewf[:, at:at + n].rearrange(f"p ({names}) -> p {names}", **axes)

        raw12 = early([KD, 2, z.SH])
        raw3 = early([z.JS, z.D])
        sw12 = m.sb("sw12", [P, 2, KD, 2, z.SH], F32R)
        sw3 = m.sb("sw3", [P, 2, z.JS, z.D], F32R)
        rawx = m.sb("rawx", [P, KD, CHUNK])
        xparts = m.sb("xparts", [P, 2, 2, KD, CHUNK], F32R)
        xr = m.sb("xr", [P, 2, CT, z.D])
        sil = m.sb("sil", [P, 2, CHUNK])
        hid = m.sb("hid", [P, 2, CHUNK])
        hparts = m.sb("hparts", [P, 2, 2, CHUNK], F32R)
        score, sel, tmp, one1, one2 = (early([NT, E]) for _ in range(5))
        count, upto = early([E, NT]), early([E, NT])
        both = m.sb("both", [P, NT, E], BF16)
        top = m.sb("top", [P, 6, NT])
        small = m.sb("small", [P, 8, E])
        small_i = m.sb("small_i", [P, 2, E], I32)
        bexp = m.sb("bexp", [1, NB])
        bexp_i = m.sb("bexp_i", [1, NB], I32)
        slot_f = m.sb("slot_f", [P, NT, TOPK])
        xq = m.sb("xq", [P, 2, CT, z.D])
        idx = m.sb("idx", [P, 2, CT * TOPK], U32)
        bcmp = xq[0:1].rearrange("p u t d -> p (u t d)")[:, 0:NB * E].rearrange("p (b e) -> p b e", e=E)
        xs = rawx[:].rearrange("p k (s d) -> p (k s) d", d=z.D)
        silr, hr = sil[:, 0].rearrange("p (s d) -> p s d", s=2), sil[:, 1].rearrange("p (s d) -> p s d", s=2)
        xsT, hrT = hid[:, 0].rearrange("p (s d) -> p s d", s=2), hid[:, 1].rearrange("p (s d) -> p s d", s=2)
        yr = xq[:, 0]
        assert used[0] <= E * KD * 2 * RH and KD * CHUNK == 4 * z.D and CHUNK == 2 * RH
        bank = [m.ps(f"bank{i}", [P, 512]) for i in range(8)]
        psA, psB = bank[0:2], bank[2:4]
        psO = [bank[4 + t // 2][:, (t % 2) * z.D:(t % 2 + 1) * z.D] for t in range(CT)]
        psR, psC = bank[6], bank[7]
        rUp, rTx, rTh, rY = bank[0:2], bank[2], bank[3], bank[4:6]

        sw_in = m.sems("sw_in", 6)
        w_hi = m.sem("w_hi")
        w_lo = m.sem("w_lo")
        ew_in = m.sem("ew_in")
        rawx_ld = m.sem("rawx_ld")
        x_hi = m.sem("x_hi")
        x_lo = m.sem("x_lo")
        xr_ld = m.sems("xr_ld", 2)
        sh_st = m.sems("sh_st", 2)
        scored = m.sem("scored")
        rt = m.sem("rt")
        picked = m.sem("picked")
        ranked = m.sem("ranked")
        placed = m.sem("placed")
        a_done = m.sem("a_done")
        b_done = m.sem("b_done")
        s_done = m.sem("s_done")
        h_done = m.sem("h_done")
        h_hi = m.sem("h_hi")
        h_lo = m.sem("h_lo")
        o_done = m.sem("o_done")
        sh_done = m.sem("sh_done")
        xq_ld = m.sems("xq_ld", 2)
        idx_in = m.sem("idx_in")
        scat = m.sems("scat", 2)
        all_scat = m.sem("all_scat")
        xs_ld = m.sems("xs_ld", 4)
        tx_done = m.sem("tx_done")
        xT_ev = m.sem("xT_ev")
        rup_done = m.sem("rup_done")
        rs_done = m.sem("rs_done")
        rh_done = m.sem("rh_done")
        th_done = m.sem("th_done")
        hT_ev = m.sem("hT_ev")
        dn_done = m.sem("dn_done")
        y_done = m.sem("y_done")
        y_st = m.sems("y_st", 4)
        block = ctx.enter_context(nc.Block())

        LAST = NB + 1

        def steps(eng, body):
            for r in range(4):
                body(0, r, lambda lag, n=r: 0 <= n - lag < NB)
            with eng.Fori(1, NB // 4 - 1) as q:
                for r in range(4):
                    body(q, r, lambda lag: True)
            for n in range(NB - 4, LAST + 1):
                body(n // 4, n % 4, lambda lag, n=n: 0 <= n - lag < NB)

        def chunks(eng, body):
            body(0, 0, 0, True, False)
            body(1, 0, 1, False, False)
            with eng.Fori(1, NC // 2 - 1) as c2:
                for u in range(2):
                    body(c2 * 2 + u, c2, u, False, False)
            body(NC - 2, NC // 2 - 1, 0, False, False)
            body(NC - 1, NC // 2 - 1, 1, False, True)

        HALF = z.SH // 2
        cols = [(w, h) for h in range(2) for w in range(2)]
        PIECES = ([(raw12[:, :, w, h * HALF:(h + 1) * HALF], sw12[:, :, :, w, h * HALF:(h + 1) * HALF])
                   for w, h in cols]
                  + [(raw3[:, h * (z.JS // 2):(h + 1) * (z.JS // 2)], sw3[:, :, h * (z.JS // 2):(h + 1) * (z.JS // 2)])
                     for h in range(2)])

        @block.sync
        def _(sp):
            def load_x(c):
                sp.dma_start(rawx[:], dram.xnT[:, :, bass.ds(c * CHUNK, CHUNK)]).then_inc(rawx_ld, 16)

            def load_res(c, u):
                sp.dma_start(xr[:, u], x_src[bass.ds(c * CHUNK, CHUNK), :].rearrange("(t p) d -> p t d", p=P)
                             ).then_inc(xr_ld[u], 16)

            def store(c, u):
                sp.wait_ge(sh_done, c * 4 + 8)
                sp.sem_inc(g.held, 1)
                sp.dma_start(dram.sh[bass.ds(c * CHUNK, CHUNK), :].rearrange("(t p) d -> p t d", p=P), xr[:, u]
                             ).then_inc(sh_st[u], 16)

            load_x(0)
            wsrc = [w.rearrange("(k p) n -> p k n", p=P) for w in (dram.shared_w1, dram.shared_w2, dram.shared_w3)]
            for i, (w, h) in enumerate(cols):
                sp.dma_start(PIECES[i][0], wsrc[w][:, :, h * HALF:(h + 1) * HALF]).then_inc(sw_in[i], 16)
            for h in range(2):
                sp.dma_start(PIECES[4 + h][0], wsrc[2][:, h * (z.JS // 2):(h + 1) * (z.JS // 2), :]
                             ).then_inc(sw_in[4 + h], 16)
            load_res(0, 0)
            load_res(1, 1)
            sp.wait_ge(x_lo, 1)
            load_x(1)
            if fill:
                for b0 in range(0, NB, 8):
                    sp.dma_start(dram.xs[b0 * P:(b0 + 8) * P, :].rearrange("(b p) d -> p b d", p=P),
                                 g.zero[:].rearrange("p (o d) -> p o d", o=1).to_broadcast([P, 8, z.D])
                                 ).then_inc(g.filled, 16)
            sp.wait_ge(placed, 1)
            sp.wait_ge(w_lo, 6)

            PER = 2
            HEAD = E - PER * (NC - 2)

            def load_expert(e):
                for dst, src in ((ew12[:, bass.ds(e, 1), :, 0:RH], dram.routed_w1),
                                 (ew12[:, bass.ds(e, 1), :, RH:], dram.routed_w2),
                                 (ew3[:, bass.ds(e, 1)], dram.routed_w3)):
                    sp.dma_start(dst, src[bass.ds(e, 1)].rearrange("e (k p) n -> p e k n", p=P)).then_inc(ew_in, 16)

            for e in range(HEAD):
                load_expert(e)
            with sp.Fori(1, NC // 2) as c2:
                for u in range(2):
                    sp.wait_ge(x_lo, c2 * 2 + u)
                    sp.sem_inc(g.held, 1)
                    load_x(c2 * 2 + u)
                    store(c2 * 2 + u - 2, u)
                    sp.wait_ge(sh_st[u], c2 * 16)
                    sp.sem_inc(g.held, 1)
                    load_res(c2 * 2 + u, u)
                    for i in range(PER):
                        load_expert(c2 * (2 * PER) + (u * PER + i + HEAD - 2 * PER))
            for u in range(2):
                store(NC - 2 + u, u)
            sp.wait_ge(x_lo, NC)
            sp.sem_inc(g.held, 1)

            def fetch(q, r):
                sp.wait_ge(tx_done, q * 4 + r + 1)
                sp.sem_inc(g.held, 1)
                sp.dma_start(xs[:, r], dram.xs[bass.ds(q * (4 * P) + r * P, P), :]).then_inc(xs_ld[r], 16)

            def put(q, r):
                sp.wait_ge(y_done, q * 4 + r + 3)
                sp.sem_inc(g.held, 1)
                sp.dma_start(dram.ys[bass.ds(q * (4 * P) + r * P, P), :], yr[:, r]).then_inc(y_st[r], 16)

            sp.wait_ge(all_scat, 1)
            for r in range(4):
                fetch(0, r)
            with sp.Fori(0, NB // 4 - 1) as q:
                for r in range(4):
                    fetch(q + 1, r)
                    put(q, r)
            for r in range(4):
                put(NB // 4 - 1, r)
            for u in range(2):
                sp.wait_ge(sh_st[u], 16 * (NC // 2))
            for r in range(4):
                sp.wait_ge(y_st[r], 16 * (NB // 4 + 1))

        @block.gpsimd
        def _(pool):
            for i, (raw, parts) in enumerate(PIECES):
                pool.wait_ge(w_hi, i + 1)
                nc.gpsimd.tensor_tensor(parts[:, 1], raw, parts[:, 0], ALU.subtract).then_inc(w_lo, 1)
            pool.wait_ge(placed, 1)

            def load(c, u):
                pool.dma_start(xq[:, u], dram.xn[bass.ds(c * CHUNK, CHUNK), :].rearrange("(t p) d -> p t d", p=P)
                               ).then_inc(xq_ld[u], 16)

            def send(c, c2, u):
                pool.wait_ge(xq_ld[u], c2 * 16 + 16)
                nc.gpsimd.tensor_copy(idx[:, u, :], g.slot[:, bass.ds(c * (CT * TOPK), CT * TOPK)]
                                      ).then_inc(idx_in, 1)
                pool.wait_ge(idx_in, c + 1)
                pool.sem_inc(g.held, 1)
                for t in range(CT):
                    for k in range(TOPK):
                        nc.gpsimd.indirect_dma_start(
                            dram.xs, bass.IndirectOffsetOnAxis(ap=idx[:, u, TOPK * t + k:TOPK * t + k + 1], axis=0),
                            xq[:, u, t, :], None).then_inc(scat[u], 16)

            per = 16 * CT * TOPK
            pool.wait_ge(g.filled, 16 * (NB // 8))
            pool.sem_inc(g.held, 1)
            load(0, 0)
            load(1, 1)
            send(0, 0, 0)
            send(1, 0, 1)
            with pool.Fori(1, NC // 2) as c2:
                for u in range(2):
                    pool.wait_ge(scat[u], c2 * per)
                    load(c2 * 2 + u, u)
                for u in range(2):
                    send(c2 * 2 + u, c2, u)
            for u in range(2):
                pool.wait_ge(scat[u], per * (NC // 2))
            pool.sem_inc(all_scat, 1)

        @block.scalar
        def _(act):
            def split_x(c, u):
                act.wait_ge(rawx_ld, c * 16 + 16)
                nc.scalar.copy(xparts[:, u, 0], rawx[:]).then_inc(x_hi, 1)

            nc.scalar.activation(score.rearrange("p t e -> p (t e)"), g.logits[:], ACT.Sigmoid).then_inc(scored, 1)
            split_x(0, 0)
            for i, (raw, parts) in enumerate(PIECES):
                act.wait_ge(sw_in[i], 16)
                nc.scalar.copy(parts[:, 0], raw).then_inc(w_hi, 1)

            def chunk(c, c2, u, first, last):
                for j in range(z.JS):
                    n = c * z.JS + j
                    act.wait_ge(a_done, n + 1)
                    nc.scalar.activation(sil[:, j % 2, :], psA[j % 2][:, :], ACT.Silu).then_inc(s_done, 1)
                    act.wait_ge(h_done, n + 3)
                    nc.scalar.copy(hparts[:, j % 2, 0], hid[:, j % 2]).then_inc(h_hi, 1)
                    if j == 2 and not last:
                        split_x(c + 1, 1 - u)

            chunks(act, chunk)
            act.sem_inc(xT_ev, 1)

            def step(q, r, has):
                i = q * 4 + r
                if has(0):
                    act.wait_ge(rup_done, i + 3)
                    nc.scalar.activation(silr[:, r % 2, :], rUp[r % 2][:, 0:RH], ACT.Silu).then_inc(rs_done, 1)
                if has(-1):
                    evacuate(i + 1, (r + 1) % 2)

            def evacuate(i, s):
                act.wait_ge(tx_done, i + 5)
                act.wait_ge(rup_done, i + 1)
                nc.scalar.copy(xsT[:, s, :], rTx[:, 0:KD * P]).then_inc(xT_ev, 1)

            evacuate(0, 0)
            steps(act, step)

        @block.vector
        def _(dve):
            dve.sem_inc(h_done, 2)
            dve.sem_inc(sh_done, 4)
            n = [0]

            def link(ins):
                n[0] += 1
                ins.then_inc(rt, 1)
                dve.wait_ge(rt, n[0])

            v = nc.vector
            over_t = lambda a: a.rearrange("p (o e) -> p o e", o=1).to_broadcast([P, NT, E])
            over_e = lambda a: a.rearrange("p (t o) -> p t o", o=1).to_broadcast([P, NT, E])
            def low_x(u, c):
                dve.wait_ge(x_hi, c + 1)
                v.tensor_tensor(xparts[:, u, 1], rawx[:], xparts[:, u, 0], ALU.subtract).then_inc(x_lo, 1)

            def largest(k, one):
                link(v.tensor_reduce(top[:, k, :], sel, AX.X, ALU.max))
                link(v.tensor_tensor(tmp, sel, over_e(top[:, k, :]), ALU.is_equal))
                link(v.tensor_tensor(tmp, tmp, over_t(g.rev[:]), ALU.mult))
                link(v.tensor_reduce(top[:, 2 + k, :], tmp, AX.X, ALU.max))
                link(v.tensor_tensor(one, over_t(g.rev[:]), over_e(top[:, 2 + k, :]), ALU.is_equal))

            def pick_first():
                dve.wait_ge(scored, 1)
                link(v.tensor_tensor(sel, score, over_t(g.bias[:]), ALU.add))
                largest(0, one1)

            def pick_second():
                link(v.scalar_tensor_tensor(sel, one1, -3.0e38, sel, ALU.mult, ALU.add))
                largest(1, one2)
                link(v.tensor_tensor(both[:], one1, one2, ALU.add))
                dve.sem_inc(picked, 1)

            def gates():
                for k, one in enumerate((one1, one2)):
                    link(v.tensor_tensor(tmp, score, one, ALU.mult))
                    link(v.tensor_reduce(top[:, 4 + k, :], tmp, AX.X, ALU.add))
                    link(v.tensor_scalar(g.gate[:, :, k], top[:, 4 + k, :], 0.5, None, ALU.mult))

            def experts_blocks():
                dve.wait_ge(ranked, 1)
                link(v.tensor_copy(count, psC[:, :].rearrange("p (t e) -> p e t", e=E)))
                link(v.tensor_tensor_scan(upto.rearrange("p e t -> p (e t)"), g.keep[:].rearrange("p e t -> p (e t)"),
                                          count.rearrange("p e t -> p (e t)"), 0.0, ALU.mult, ALU.add))
                link(v.tensor_scalar(small[:, 0, :], upto[:, :, NT - 1], float(P - 1), None, ALU.add))
                link(v.tensor_copy(small_i[:, 0, :], small[:, 0, :]))
                link(v.tensor_single_scalar(small_i[:, 1, :], small_i[:, 0, :], int(math.log2(P)),
                                            ALU.logical_shift_right))
                link(v.tensor_copy(small[:, 1, :], small_i[:, 1, :]))
                link(v.memset(small[:, 2, :], 1.0))
                link(v.tensor_tensor_scan(small[:, 3, :], small[:, 2, :], small[:, 1, :], 0.0, ALU.mult, ALU.add))
                link(v.tensor_tensor(small[:, 4, :], small[:, 3, :], small[:, 1, :], ALU.subtract))
                link(v.tensor_scalar(small[:, 5, :], small[:, 4, :], float(P), None, ALU.mult))

            def place():
                link(v.tensor_tensor(upto, upto, count, ALU.subtract))
                link(v.tensor_tensor(upto, upto, small[:, 5, :].rearrange("p (e o) -> p e o", o=1)
                                     .to_broadcast([P, E, NT]), ALU.add))
                link(v.tensor_tensor(sel, psR[:, :].rearrange("p (t e) -> p t e", e=E),
                                     upto.rearrange("p e t -> p t e"), ALU.add))
                for k, one in enumerate((one1, one2)):
                    link(v.tensor_tensor(tmp, sel, one, ALU.mult))
                    link(v.tensor_reduce(slot_f[:, :, k], tmp, AX.X, ALU.add))
                link(v.tensor_copy(g.slot[:], slot_f[:].rearrange("p t k -> p (t k)")))

            def block_experts():
                link(v.tensor_tensor(bcmp, small[0:1, 3, :].rearrange("p (o e) -> p o e", o=1).to_broadcast([1, NB, E]),
                                     g.blk[0:1, :].rearrange("p (b o) -> p b o", o=1).to_broadcast([1, NB, E]),
                                     ALU.is_le))
                link(v.tensor_reduce(bexp[:], bcmp, AX.X, ALU.add))
                link(v.tensor_scalar(bexp[:], bexp[:], float(E - 1), None, ALU.min))
                link(v.tensor_copy(bexp_i[:], bexp[:]))
                dve.sem_inc(placed, 1)

            def residual(c, c2, u):
                dve.wait_ge(xr_ld[u], c2 * 16 + 16)
                for t in range(CT):
                    if t % 2 == 0:
                        dve.wait_ge(o_done, c * CT + t + 2)
                    v.scalar_tensor_tensor(xr[:, u, t, :], psO[t], 0.5, xr[:, u, t, :],
                                           ALU.mult, ALU.add).then_inc(sh_done, 1)

            ROUTING = {0: pick_first, 1: pick_second, 3: gates, 4: experts_blocks, 5: place, 6: block_experts}

            def chunk(c, c2, u, first, last):
                for j in range(z.JS):
                    n = c * z.JS + j
                    dve.wait_ge(s_done, n + 1)
                    dve.wait_ge(b_done, n + 1)
                    v.tensor_tensor(hid[:, j % 2], sil[:, j % 2, :], psB[j % 2][:, :], ALU.mult).then_inc(h_done, 1)
                    dve.wait_ge(h_hi, n + 1)
                    v.tensor_tensor(hparts[:, j % 2, 1], hid[:, j % 2], hparts[:, j % 2, 0], ALU.subtract
                                    ).then_inc(h_lo, 1)
                    if j == 0 and not first:
                        residual(c - 1, c2 if u else c2 - 1, 1 - u)
                    if j == 3 and not last:
                        low_x(1 - u, c + 1)
                    if first and j in ROUTING:
                        ROUTING[j]()

            low_x(0, 0)
            chunks(dve, chunk)
            residual(NC - 1, NC // 2 - 1, 1)

            dve.sem_inc(rh_done, 2)
            dve.sem_inc(hT_ev, 1)
            dve.sem_inc(y_done, 2)
            for r in range(4):
                dve.sem_inc(y_st[r], 16)

            def step(q, r, has):
                i = q * 4 + r
                if has(1):
                    dve.wait_ge(th_done, i)
                    v.tensor_copy(hrT[:, (r - 1) % 2, :], rTh[:, 0:KR * P]).then_inc(hT_ev, 1)
                if has(0):
                    dve.wait_ge(rs_done, i + 1)
                    v.tensor_tensor(hr[:, r % 2, :], silr[:, r % 2, :], rUp[r % 2][:, RH:2 * RH], ALU.mult
                                    ).then_inc(rh_done, 1)
                if has(2):
                    s = (r - 2) % 4
                    dve.wait_ge(dn_done, i - 1)
                    dve.wait_ge(y_st[s], (q * 16 if r < 2 else q * 16 + 16))
                    v.tensor_copy(yr[:, s, :], rY[r % 2][:, 0:z.D]).then_inc(y_done, 1)

            steps(dve, step)

        @block.tensor
        def _(pe):
            pe.sem_inc(tx_done, 4)
            pe.sem_inc(rup_done, 2)

            def rank():
                pe.wait_ge(picked, 1)
                marks = both[:].rearrange("p t e -> p (t e)")
                pe.matmul(psR[:, 0:TE], g.before[:, :], marks, start=True, stop=True)
                pe.matmul(psC[:, 0:TE], g.ones[:, :], marks, start=True, stop=True).then_inc(ranked, 1)

            def up(c, u, j, first):
                n = c * z.JS + j
                pe.wait_ge(h_done, n + 1)
                for w, ps, sem in ((0, psA, a_done), (1, psB, b_done)):
                    if first and j % (z.JS // 2) == 0:
                        pe.wait_ge(w_lo, 2 * (j // (z.JS // 2)) + w + 1)
                    i = 0
                    for wp, xp in ((0, 0), (0, 1), (1, 0)):
                        for k in range(KD):
                            ins = pe.matmul(ps[j % 2][:, :], sw12[:, wp, k, w, j * P:(j + 1) * P], xparts[:, u, xp, k, :],
                                            start=(i == 0), stop=(i == 3 * KD - 1))
                            i += 1
                    ins.then_inc(sem, 1)

            def down(c, j, first):
                n = c * z.JS + j
                if first and j % (z.JS // 2) == 0:
                    pe.wait_ge(w_lo, 5 + j // (z.JS // 2))
                pe.wait_ge(h_hi, n + 1)
                for t in range(CT):
                    if j == 0 and t % 2 == 0:
                        pe.wait_ge(sh_done, c * CT + t + 2)
                    for wp in range(2):
                        pe.matmul(psO[t], hparts[:, j % 2, 0, t * P:(t + 1) * P], sw3[:, wp, j, :],
                                  start=(j == 0 and wp == 0 and t % 2 == 0), stop=False, skip_group_check=True)
                pe.wait_ge(h_lo, n + 1)
                for t in range(CT):
                    ins = pe.matmul(psO[t], hparts[:, j % 2, 1, t * P:(t + 1) * P], sw3[:, 0, j, :],
                                    start=False, stop=(j == z.JS - 1), skip_group_check=True)
                    if j == z.JS - 1:
                        ins.then_inc(o_done, 1)

            def chunk(c, c2, u, first, last):
                pe.wait_ge(x_lo, c + 1)
                for j in range(z.JS):
                    up(c, u, j, first)
                    if j > 0:
                        down(c, j - 1, first)
                    elif not first:
                        down(c - 1, z.JS - 1, False)
                    if first and j == 3:
                        rank()

            chunks(pe, chunk)
            down(NC - 1, z.JS - 1, False)
            pe.wait_ge(sh_done, NC * CT + 4)
            pe.wait_ge(ew_in, 3 * 16 * E)
            w12 = ewf
            w3 = ew3[:].rearrange("p e k n -> p (e k n)")

            def turn_x(q, r):
                i = q * 4 + r
                pe.wait_ge(xs_ld[r], q * 16 + 16)
                pe.wait_ge(xT_ev, i + 1)
                for k in range(KD):
                    ins = pe.transpose(rTx[:, k * P:(k + 1) * P], xs[:, r, k * P:(k + 1) * P], g.ident[:, :])
                ins.then_inc(tx_done, 1)

            def expert(i):
                return pe.value_load(bexp_i[0:1, bass.ds(i, 1)], min_val=0, max_val=E - 1)

            def step(q, r, has):
                i = q * 4 + r
                if has(0):
                    e = expert(i)
                    pe.wait_ge(xT_ev, i + 2)
                    pe.wait_ge(rh_done, i + 1)
                    for k in range(KD):
                        ins = pe.matmul(rUp[r % 2][:, :], xsT[:, r % 2, k * P:(k + 1) * P],
                                        w12[:, bass.ds(e * (KD * 2 * RH) + k * 2 * RH, 2 * RH)],
                                        start=(k == 0), stop=(k == KD - 1))
                    ins.then_inc(rup_done, 1)
                if has(1):
                    pe.wait_ge(rh_done, i + 2)
                    pe.wait_ge(hT_ev, i)
                    for k in range(KR):
                        ins = pe.transpose(rTh[:, k * P:(k + 1) * P], hr[:, (r - 1) % 2, k * P:(k + 1) * P],
                                           g.ident[:, :])
                    ins.then_inc(th_done, 1)
                if has(-1):
                    if r == 3:
                        turn_x(q + 1, 0)
                    else:
                        turn_x(q, r + 1)
                if has(2):
                    e = expert(i - 2)
                    pe.wait_ge(hT_ev, i)
                    pe.wait_ge(y_done, i - 1)
                    for k in range(KR):
                        ins = pe.matmul(rY[r % 2][:, 0:z.D], hrT[:, r % 2, k * P:(k + 1) * P],
                                        w3[:, bass.ds(e * (KR * z.D) + k * z.D, z.D)],
                                        start=(k == 0), stop=(k == KR - 1))
                    ins.then_inc(dn_done, 1)

            turn_x(0, 0)
            steps(pe, step)


def combine_last(nc, z, g, dram, out_flat):
    with ExitStack() as ctx:
        m = Mem(nc, ctx, "cl_")
        NC = z.NC
        acc = m.sb("acc", [P, 2, CT, z.D])
        yg = m.sb("yg", [P, 2, CT, TOPK, z.D])
        idx = m.sb("idx", [P, 2, CT * TOPK], U32)
        acc_ld = m.sems("acc_ld", 2)
        idx_in = m.sem("idx_in")
        y_ld = m.sems("y_ld", 2)
        mid = m.sem("mid")
        done = m.sem("done")
        out_st = m.sems("out_st", 2)
        block = ctx.enter_context(nc.Block())
        per = 16 * CT * TOPK

        @block.gpsimd
        def _(pool):
            def gather(c, u, first):
                if not first:
                    pool.wait_ge(done, c - 1)
                nc.gpsimd.tensor_copy(idx[:, u, :], g.slot[:, bass.ds(c * (CT * TOPK), CT * TOPK)]
                                      ).then_inc(idx_in, 1)
                pool.wait_ge(idx_in, c + 1)
                pool.sem_inc(g.held, 1)
                for t in range(CT):
                    for k in range(TOPK):
                        nc.gpsimd.indirect_dma_start(
                            yg[:, u, t, k, :], None, dram.ys,
                            bass.IndirectOffsetOnAxis(ap=idx[:, u, TOPK * t + k:TOPK * t + k + 1], axis=0)
                        ).then_inc(y_ld[u], 16)

            gather(0, 0, True)
            gather(1, 1, True)
            with pool.Fori(1, NC // 2) as c2:
                for u in range(2):
                    gather(c2 * 2 + u, u, False)

        @block.sync
        def _(sp):
            def load(c, u):
                sp.dma_start(acc[:, u], dram.sh[bass.ds(c * CHUNK, CHUNK), :].rearrange("(t p) d -> p t d", p=P)
                             ).then_inc(acc_ld[u], 16)

            def store(c, c2, u):
                sp.wait_ge(done, c + 1)
                sp.sem_inc(g.held, 1)
                sp.dma_start(out_flat[bass.ds(c * CHUNK, CHUNK), :].rearrange("(t p) d -> p t d", p=P), acc[:, u]
                             ).then_inc(out_st[u], 16)

            load(0, 0)
            load(1, 1)
            with sp.Fori(0, NC // 2 - 1) as c2:
                for u in range(2):
                    store(c2 * 2 + u, c2, u)
                    sp.wait_ge(out_st[u], c2 * 16 + 16)
                    sp.sem_inc(g.held, 1)
                    load(c2 * 2 + u + 2, u)
            for u in range(2):
                store(NC - 2 + u, NC // 2 - 1, u)
            for u in range(2):
                sp.wait_ge(out_st[u], 16 * (NC // 2))

        @block.vector
        def _(dve):
            with dve.Fori(0, NC // 2) as c2:
                for u in range(2):
                    c = c2 * 2 + u
                    dve.wait_ge(acc_ld[u], c2 * 16 + 16)
                    dve.wait_ge(y_ld[u], c2 * per + per)
                    for k in range(TOPK):
                        for t in range(CT):
                            ins = nc.vector.scalar_tensor_tensor(
                                acc[:, u, t, :], yg[:, u, t, k, :], g.gate[:, bass.ds(c * CT + t, 1), k],
                                acc[:, u, t, :], ALU.mult, ALU.add)
                            if k == 0:
                                ins.then_inc(mid, 1)
                        if k == 0:
                            dve.wait_ge(mid, c * CT + CT)
                    ins.then_inc(done, 1)


class Names:
    pass


def residents(nc, z, ctx):
    m = Mem(nc, ctx)
    g = Names()
    g.held = m.sem("held")
    g.filled = m.sem("filled")
    g.zero = m.sb("zero", [P, z.D])
    g.rw = m.sb("rw", [P, z.KD, z.E])
    g.bias = m.sb("bias", [P, z.E])
    g.ident = m.sb("ident", [P, P])
    g.before = m.sb("before", [P, P], BF16)
    g.ones = m.sb("ones", [P, P], BF16)
    g.mhalf = m.sb("mhalf", [P, CT])
    g.eps = m.sb("eps", [P, CT])
    g.rev_i = m.sb("rev_i", [P, z.E], I32)
    g.rev = m.sb("rev", [P, z.E])
    g.blk_i = m.sb("blk_i", [P, z.NB], I32)
    g.blk = m.sb("blk", [P, z.NB])
    g.keep = m.sb("keep", [P, z.E, z.NT])
    g.logits = m.sb("logits", [P, z.NT * z.E])
    g.slot = m.sb("slot", [P, z.NT * TOPK], U32)
    g.gate = m.sb("gate", [P, z.NT, TOPK])
    return g


def scratch(nc, z):
    d = Names()
    d.xn = nc.dram_tensor("xn_rows", [z.T, z.D], F32).ap()
    d.xnT = nc.dram_tensor("xn_turned", [P, z.KD, z.T], F32).ap()
    d.x1 = nc.dram_tensor("x1_rows", [z.T, z.D], F32).ap()
    d.x2 = nc.dram_tensor("x2_rows", [z.T, z.D], F32).ap()
    d.sh = nc.dram_tensor("x_plus_shared", [z.T, z.D], F32).ap()
    d.xs = nc.dram_tensor("rows_by_slot", [z.NB * P, z.D], F32).ap()
    d.ys = nc.dram_tensor("outputs_by_slot", [z.NB * P, z.D], F32).ap()
    return d


def attention(nc, z, g, dram):
    KD, E, D = z.KD, z.E, z.D
    H, DK = 16, 16
    HG = 4
    NG = H // HG
    MASK = -65536.0
    SL = 64
    NB_ = z.B
    UNITS1 = [(0, 0, 4), (1, 0, 2), (1, 2, 2)] + [(t, h, 1) for t in (2, 3) for h in range(HG)]
    UNITS2 = [(t, h, 1) for t in (0, 1) for h in range(HG)] + [(2, 0, 2), (2, 2, 2), (3, 0, 4)]
    UN = len(UNITS1)
    UG = CT * HG
    LAG = 2
    LAST_UNIT = [3, 7, 9, 10]
    STEPS = UN + LAG
    QSCALE = float(DK) ** -0.5
    with ExitStack() as ctx:
        m = Mem(nc, ctx, "at_")
        wqkv = m.sb("wqkv", [P, KD, 3 * D])
        wo = m.sb("wo", [P, KD, D])
        identb = m.sb("identb", [P, P], BF16)
        maskq = m.sb("maskq", [P, P], BF16)
        x1 = m.sb("x1", [P, 2, CT, D])
        yg = m.sb("yg", [P, CT, TOPK, D])
        idx = m.sb("idx", [P, CT * TOPK], U32)
        xn = m.sb("xn", [P, CT, D])
        xnT = m.sb("xnT", [P, KD, CHUNK])
        qk = m.sb("qk", [P, 2, NG, CT, HG * DK])
        va = m.sb("va", [P, 2, CT, H, 32])
        q4 = m.sb("q4", [P, 2, CT, HG, SL], F32R)
        k4 = m.sb("k4", [P, 2, CT, HG, SL], F32R)
        identr = m.sb("identr", [P, P], F32R)
        qT = m.sb("qT", [P, 2, HG, CHUNK], F32R)
        kT = m.sb("kT", [P, NG, HG // 2, CHUNK], F32R)
        q2T = m.sb("q2T", [P, 2, HG, CHUNK], F32R)
        pT = m.sb("pT", [P, 8, CHUNK])
        oT = m.sb("oT", [P, CHUNK])
        rec = m.sb("rec", [P, CT, HG])
        attn = m.sb("attn", [P, CT, D])
        attnT = m.sb("attnT", [P, KD, CHUNK])
        xres = m.sb("xres", [P, CT, D])
        xn2 = m.sb("xn2", [P, CT, D])
        xnT2 = m.sb("xnT2", [P, KD, CHUNK])
        stat = m.sb("stat", [P, 2, CT, 6])
        mv = m.sb("mv", [P, 2, CT, 2])
        veps = m.sb("veps", [P, 2, CT])
        rstd = m.sb("rstd", [P, 2, CT])
        ps1 = [m.ps(f"ps1_{i}", [P, 512]) for i in range(2)]
        ps2 = [m.ps(f"ps2_{i}", [P, 512]) for i in range(2)]
        psO = m.ps("psO", [P, 512])
        psG = m.ps("psG", [P, 2, 512])
        psM = m.ps("psM", [P, 512])

        w_in = m.sem("w_in")
        made = m.sem("made")
        identr_in = m.sem("identr_in")
        consts = m.sem("consts")
        filled = m.sem("filled")
        x1_ld = m.sems("x1_ld", 2)
        y_ld = m.sem("y_ld")
        idx_in = m.sem("idx_in")
        x1_mid = m.sem("x1_mid")
        x1_done = m.sem("x1_done")
        x1_st = m.sems("x1_st", 2)
        st = m.sem("st")
        var1 = m.sem("var1")
        eps1 = m.sem("eps1")
        rs1 = m.sem("rs1")
        normed1 = m.sem("normed1")
        g_full = m.sem("g_full")
        g_free = m.sem("g_free")
        hi_done = m.sem("hi_done")
        lo_done = m.sem("lo_done")
        s1_done = m.sem("s1_done")
        mx_done = m.sem("mx_done")
        s2_done = m.sem("s2_done")
        ex_done = m.sem("ex_done")
        cut_done = m.sem("cut_done")
        pv_done = m.sem("pv_done")
        o_ev = m.sem("o_ev")
        rc = m.sem("rc")
        m_full = m.sem("m_full")
        m_free = m.sem("m_free")
        xr_ld = m.sem("xr_ld")
        var2 = m.sem("var2")
        eps2 = m.sem("eps2")
        rs2 = m.sem("rs2")
        normed2 = m.sem("normed2")
        x2_st = m.sem("x2_st")
        xn2_st = m.sem("xn2_st")
        xnT2_st = m.sem("xnT2_st")
        block = ctx.enter_context(nc.Block())

        def g_uses(c, gr):
            has_last, has_next = c != 0, c != NB_ - 1
            names = []
            if gr == 0 and has_last:
                names.append("attnT")
            if gr == 1 and has_next:
                names += [f"proj{t}" for t in range(CT)]
            if gr == 2 and has_last:
                names.append("x2T")
            if gr < 2 or has_next:
                names += [f"TQ_{gr}", f"TK_{gr}"]
            if gr == 0 and has_next:
                names.append("xnT")
            if gr < NG - 1 or has_next:
                names.append(f"T2_{gr}")
            return names

        def g_batch(c):
            return sum((g_uses(c, gr) for gr in range(NG)), [])

        FIRST_G = ["xnT"] + [f"proj{t}" for t in range(CT)] + ["TQ_0", "TK_0", "TQ_1", "TK_1", "T2"]
        PER_G = len(g_batch(1))

        def g_base(c, kind):
            if kind == 0:
                return len(FIRST_G)
            return c * PER_G + (len(FIRST_G) + len(g_batch(0)) - PER_G)

        def g_before(c, kind, gr):
            return g_base(c, kind) + sum(len(g_uses(kind, i)) for i in range(gr))

        def gu(c, kind, name):
            if kind == "first":
                return FIRST_G.index(name)
            if kind == "end":
                return g_base(NB_ - 1, NB_ - 1) + len(g_batch(NB_ - 1)) + ["attnT", "x2T"].index(name)
            return g_base(c, kind) + g_batch(kind).index(name)

        M_FIRST = ["OT_0", "OT_1", "OT_2"]
        M_USES = ["OT_3"] + [f"out{t}" for t in range(CT)] + ["OT_0", "OT_1", "rt", "OT_2"]
        M_END = ["OT_3"] + [f"out{t}" for t in range(CT)] + ["rt"]

        def mu(c, kind, name):
            if kind == 0:
                return M_FIRST.index(name)
            return c * len(M_USES) + (len(M_FIRST) - len(M_USES) + M_USES.index(name))

        def mu_end(name):
            return len(M_FIRST) + len(M_USES) * (NB_ - 1) + M_END.index(name)


        VALUES_AT = {LAG + 6: 0, LAG + 10: 1}
        VALUES_LATE = {0: 2, 1: 3}
        AT = dict(attnT=7, x2T=3, xnT=11, T2=STEPS - 1)
        OUT_AT = [9, 10, 11, 12]
        GATHERS_AT = [3, 6, 7, 8]
        PROJECT_AT = [2, 3, 5, 6]

        def turns(gr, n):
            q, k = {0: (7, 9), 1: (8, 10)}.get(gr, (6, 9))
            return "TQ" if n == q else "TK" if n == k else None

        def phases(eng, first, phase, last):
            first()
            for u in range(2):
                for gr in range(NG):
                    phase(u, 0, u, u, gr)
            with eng.Fori(1, NB_ // 2 - 1) as c2:
                for u in range(2):
                    for gr in range(NG):
                        phase(c2 * 2 + u, c2, u, 2, gr)
            for u in range(2):
                for gr in range(NG):
                    phase(NB_ - 2 + u, NB_ // 2 - 1, u, 2 if u == 0 else NB_ - 1, gr)
            last()

        def rows(ap, c):
            return ap[bass.ds(c * CHUNK, CHUNK), :].rearrange("(t p) d -> p t d", p=P)

        @block.sync
        def _(sp):
            def hold(sem, value):
                sp.wait_ge(sem, value)
                sp.sem_inc(g.held, 1)

            def load_x1(c, c2, u, first):
                if not first:
                    hold(x1_st[u], c2 * 16)
                    hold(normed1, c - 1)
                sp.dma_start(x1[:, u], rows(dram.sh, c)).then_inc(x1_ld[u], 16)

            def store_x1(c, u):
                hold(x1_done, c + 1)
                sp.dma_start(rows(dram.x1, c), x1[:, u]).then_inc(x1_st[u], 16)

            def load_res(c, c2, u, first):
                hold(x1_st[u], c2 * 16 + 16)
                if not first:
                    hold(x2_st, c * 16)
                    hold(normed2, c)
                sp.dma_start(xres[:], rows(dram.x1, c)).then_inc(xr_ld, 16)

            def store_x2(c):
                hold(var2, c + 1)
                sp.dma_start(rows(dram.x2, c), xres[:]).then_inc(x2_st, 16)
                hold(normed2, c + 1)
                sp.dma_start(rows(dram.xn, c), xn2[:]).then_inc(xn2_st, 16)

            def store_x2T(c, done):
                hold(g_free, done)
                sp.dma_start(dram.xnT[:, :, bass.ds(c * CHUNK, CHUNK)], xnT2[:]).then_inc(xnT2_st, 16)

            def first():
                load_x1(0, 0, 0, True)
                for i, w in enumerate((dram.W_q, dram.W_k, dram.W_v)):
                    sp.dma_start(wqkv[:, :, i * D:(i + 1) * D], w.rearrange("(k p) n -> p k n", p=P)).then_inc(w_in, 16)
                sp.dma_start(wo[:], dram.W_o.rearrange("(k p) n -> p k n", p=P)).then_inc(w_in, 16)
                load_x1(1, 0, 1, True)
                store_x1(0, 0)
                load_res(0, 0, 0, True)

            def phase(c, c2, u, kind, gr):
                if gr == 0 and kind != NB_ - 1:
                    store_x1(c + 1, 1 - u)
                if gr == 1 and kind != 0:
                    store_x2(c - 1)
                    load_res(c, c2, u, False)
                if gr == 2 and kind != 0:
                    store_x2T(c - 1, gu(c, kind, "x2T") + 2)
                if gr == 2 and (kind in (0, 1) or (kind == 2 and not isinstance(c, int))):
                    load_x1(c + 2, c2 + 1, u, False)

            def last():
                store_x2(NB_ - 1)
                store_x2T(NB_ - 1, gu(0, "end", "x2T") + 2)
                sp.wait_ge(x2_st, 16 * NB_)
                sp.wait_ge(xn2_st, 16 * NB_ + 16)
                sp.wait_ge(xnT2_st, 16 * NB_ + 16)
                for u in range(2):
                    sp.wait_ge(x1_st[u], 16 * (NB_ // 2))

            phases(sp, first, phase, last)

        @block.gpsimd
        def _(pool):
            p = nc.gpsimd

            def take_slots(c, first):
                if not first:
                    pool.wait_ge(x1_done, c)
                p.tensor_copy(idx[:], g.slot[:, bass.ds(c * (CT * TOPK), CT * TOPK)]).then_inc(idx_in, 1)
                pool.wait_ge(idx_in, c + 1)
                pool.sem_inc(g.held, 1)

            def gather(i):
                p.indirect_dma_start(yg[:, i // TOPK, i % TOPK, :], None, dram.ys,
                                     bass.IndirectOffsetOnAxis(ap=idx[:, i:i + 1], axis=0)).then_inc(y_ld, 16)

            def gather_all(c, first):
                take_slots(c, first)
                for i in range(CT * TOPK):
                    gather(i)

            def cut(G, ki):
                pool.wait_ge(ex_done, G * UN + (LAST_UNIT[ki] + 3))
                pool.sem_inc(g.held, 1)
                s = ki % 2 * HG
                p.affine_select(out=pT[:, s:s + HG, 0:P], in_=pT[:, s:s + HG, 0:P], compare_op=ALU.is_ge, fill=0.0,
                                base=0, pattern=[[0, HG], [1, P]], channel_multiplier=-1).then_inc(cut_done, 1)

            def deviation(i, c, var, eps, rs):
                pool.wait_ge(var, c + 1)
                p.tensor_tensor(veps[:, i, :], mv[:, i, :, 1], g.eps[:, 0:CT], ALU.add).then_inc(eps, 1)
                pool.wait_ge(eps, c + 1)
                p.tensor_tensor(rstd[:, i, :], veps[:, i, :], g.mhalf[:, 0:CT], ALU.pow).then_inc(rs, 1)

            def low(G, gr):
                pool.wait_ge(hi_done, G + 1)
                pool.sem_inc(g.held, 1)
                s = gr % 2
                q, k = (qk[:, i, gr].rearrange("p t (h d) -> p t h d", d=DK) for i in range(2))
                p.tensor_tensor(q4[:, s, :, :, 2 * DK:3 * DK], q, q4[:, s, :, :, 0:DK], ALU.subtract)
                p.tensor_tensor(k4[:, s, :, :, DK:2 * DK], k, k4[:, s, :, :, 0:DK], ALU.subtract
                                ).then_inc(lo_done, 1)

            n = [0]

            def done(ins):
                n[0] += 1
                ins.then_inc(made, 1)
                pool.wait_ge(made, n[0])

            def constants():
                done(p.memset(identb[:], 0.0))
                done(p.affine_select(out=identb[:], in_=identb[:], compare_op=ALU.not_equal, fill=1.0,
                                     base=0, pattern=[[-1, P]], channel_multiplier=1))
                done(p.memset(maskq[:], 0.0))
                done(p.affine_select(out=maskq[:], in_=maskq[:], compare_op=ALU.is_ge, fill=MASK,
                                     base=0, pattern=[[-1, P]], channel_multiplier=1))

            def zeros():
                done(p.memset(qT[:].bitcast(F32), 0.0))
                done(p.memset(q2T[:].bitcast(F32), 0.0))
                pool.sem_inc(consts, 1)

            def first():
                gather_all(0, True)
                constants()
                deviation(0, 0, var1, eps1, rs1)
                zeros()
                low(0, 0)
                low(1, 1)
                gather_all(1, False)

            def phase(c, c2, u, kind, gr):
                G = c * NG + gr
                more = kind in (0, 1) or (kind == 2 and not isinstance(c, int))
                for n in range(STEPS):
                    if n - LAG in LAST_UNIT:
                        cut(G, LAST_UNIT.index(n - LAG))
                    if n == 1 and (gr < 2 or kind != NB_ - 1):
                        low(G + 2, (gr + 2) % NG)
                    if n == 7 and gr == 0 and kind != NB_ - 1:
                        deviation(0, c + 1, var1, eps1, rs1)
                    if n == 2 and gr == 1 and kind != 0:
                        deviation(1, c - 1, var2, eps2, rs2)
                    if n == 3 and gr == 1 and more:
                        take_slots(c + 2, False)
                    if n in GATHERS_AT and gr in (1, 2) and more:
                        gather((gr - 1) * CT + GATHERS_AT.index(n))

            def last():
                deviation(1, NB_ - 1, var2, eps2, rs2)

            phases(pool, first, phase, last)

        @block.scalar
        def _(act):
            act.sem_inc(g_free, 1)
            act.sem_inc(ex_done, 2)
            act.sem_inc(xnT2_st, 16)
            s_ = nc.scalar
            s_.copy(identr[:], g.ident[:]).then_inc(identr_in, 1)

            def out_of_g(i, dst, src=psG):
                act.wait_ge(g_full, i + 1)
                s_.copy(dst, src[:]).then_inc(g_free, 1)

            def queries_out_of_g(i, dst, n):
                act.wait_ge(g_full, i + 1)
                for half in range(2):
                    a = half * SL
                    ins = s_.copy(dst.rearrange("p (k h) n -> p k h n", h=2)[a:a + n, :, half, :], psG[a:a + n])
                ins.then_inc(g_free, 1)

            def project(i0, t, u, lo):
                if t == 0 and lo is not None:
                    act.wait_ge(lo_done, lo)
                    act.sem_inc(g.held, 1)
                act.wait_ge(g_full, i0 + (t + 1))
                q, k = (psG[:, 0, i * D:(i + 1) * D].rearrange("p (g n) -> p g n", g=NG) for i in range(2))
                s_.mul(qk[:, 0, :, t, :], q, QSCALE)
                s_.copy(qk[:, 1, :, t, :], k)
                s_.copy(va[:, u, t, :, 0:DK], psG[:, 1, 0:D].rearrange("p (h d) -> p h d", d=DK)
                        ).then_inc(g_free, 1)

            def high(G, gr, waited):
                act.wait_ge(g_free, waited)
                s = gr % 2
                for part, i, step in ((q4, 0, 1), (k4, 1, 2)):
                    dst = (part[:, s].rearrange("p t h (s d) -> p (t h) s d", d=DK))[:, :, 0:1 + step:step, :]
                    src = qk[:, i, gr].rearrange("p t (h o d) -> p (t h) o d", o=1, d=DK)
                    ins = s_.copy(dst, src.to_broadcast([P, UG, 2, DK]))
                ins.then_inc(hi_done, 1)

            def first():
                out_of_g(gu(0, "first", "xnT"), xnT[:])
                act.wait_ge(filled, 5)
                act.sem_inc(g.held, 1)
                for t in range(CT):
                    project(gu(0, "first", "proj0"), t, 0, None)
                high(0, 0, gu(0, "first", f"proj{CT - 1}") + 2)
                high(1, 1, gu(0, "first", f"proj{CT - 1}") + 2)
                act.wait_ge(consts, 1)
                act.sem_inc(g.held, 1)
                for k in range(2):
                    queries_out_of_g(gu(0, "first", f"TQ_{k}"), qT[:, k], 3 * DK)
                queries_out_of_g(gu(0, "first", "T2"), q2T[:, 0], SL)

            def phase(c, c2, u, kind, gr):
                G = c * NG + gr
                more = gr < 2 or kind != NB_ - 1
                for n in range(STEPS):
                    if n == 0 and more:
                        high(G + 2, (gr + 2) % NG, g_before(c, kind, gr) + 1)
                    if n >= LAG:
                        k = n - LAG
                        ki, h, heads = UNITS2[k]
                        act.wait_ge(s2_done, G * UN + (k + 1))
                        act.wait_ge(pv_done, G * CT + (ki + 1))
                        w = CHUNK - ki * P
                        s = (ki * HG + h) % 8
                        s_.activation(pT[:, s:s + heads, 0:w], ps2[(gr + k) % 2][:, 0:heads * w]
                                      .rearrange("p (h w) -> p h w", h=heads), ACT.Exp).then_inc(ex_done, 1)
                    if gr == 0 and n == AT["attnT"] and kind != 0:
                        out_of_g(gu(c, kind, "attnT"), attnT[:])
                    if gr == 2 and n == AT["x2T"] and kind != 0:
                        turned2(c - 1, gu(c, kind, "x2T"))
                    if gr == 1 and n in PROJECT_AT and kind != NB_ - 1:
                        project(gu(c, kind, "proj0"), PROJECT_AT.index(n), 1 - u, c * NG + 4)
                    if turns(gr, n) == "TQ" and more:
                        queries_out_of_g(gu(c, kind, f"TQ_{gr}"), qT[:, gr % 2], 3 * DK)
                    if gr == 0 and n == AT["xnT"] and kind != NB_ - 1:
                        out_of_g(gu(c, kind, "xnT"), xnT[:])
                    if n == AT["T2"] and not (kind == NB_ - 1 and gr == NG - 1):
                        queries_out_of_g(gu(c, kind, f"T2_{gr}"), q2T[:, (gr + 1) % 2], SL)

            def turned2(c, i):
                act.wait_ge(xnT2_st, c * 16 + 16)
                out_of_g(i, xnT2[:])

            def last():
                out_of_g(gu(0, "end", "attnT"), attnT[:])
                turned2(NB_ - 1, gu(0, "end", "x2T"))

            phases(act, first, phase, last)

        @block.vector
        def _(dve):
            dve.sem_inc(mx_done, 2)
            dve.sem_inc(o_ev, 1)
            dve.sem_inc(m_free, 1)
            dve.sem_inc(xn2_st, 16)
            v = nc.vector
            v.memset(va[:], 0.0).then_inc(filled, 1)
            v.memset(q4[:].bitcast(F32), 0.0).then_inc(filled, 1)
            v.memset(k4[:].bitcast(F32), 0.0).then_inc(filled, 1)
            dve.wait_ge(filled, 3)
            v.memset(va[:, :, :, :, DK], 1.0).then_inc(filled, 1)
            v.memset(k4[:, :, :, :, 3 * DK].bitcast(F32), 1.0).then_inc(filled, 1)

            def keys_out_of_g(i, gr):
                dve.wait_ge(g_full, i + 1)
                v.tensor_copy(kT[:, gr], psG[:]).then_inc(g_free, 1)

            def combine(c, c2, u, t, k):
                if t == 0 and k == 0:
                    dve.wait_ge(x1_ld[u], c2 * 16 + 16)
                    dve.wait_ge(y_ld, c * (16 * CT * TOPK) + 16 * CT * TOPK)
                if k == 1:
                    dve.wait_ge(x1_mid, c * CT + (t + 1))
                ins = v.scalar_tensor_tensor(x1[:, u, t, :], yg[:, t, k, :], g.gate[:, bass.ds(c * CT + t, 1), k],
                                             x1[:, u, t, :], ALU.mult, ALU.add)
                if k == 0:
                    ins.then_inc(x1_mid, 1)
                elif t == CT - 1:
                    ins.then_inc(x1_done, 1)

            def moments(i, src, wait, count, var):
                if wait is not None:
                    dve.wait_ge(*wait)
                for t in range(CT):
                    v.bn_stats(stat[:, i, t, :], src[:, t, :]).then_inc(st, 1)
                dve.wait_ge(st, count + CT)
                dve.sem_inc(g.held, 1)
                for t in range(CT):
                    ins = v.bn_aggr(mv[:, i, t, :], stat[:, i, t, :])
                ins.then_inc(var, 1)

            def normalize(i, dst, src, wait, done):
                dve.wait_ge(*wait)
                for t in range(CT):
                    ins = v.tensor_scalar(dst[:, t, :], src[:, t, :], mv[:, i, t, 0:1], rstd[:, i, t:t + 1],
                                          ALU.subtract, ALU.mult)
                ins.then_inc(done, 1)

            def maxima(G, gr, n):
                qi, h, heads = UNITS1[n]
                dve.wait_ge(s1_done, G * UN + (n + 1))
                w = (qi + 1) * P
                v.tensor_reduce(q4[:, gr % 2, qi, h:h + heads, 3 * DK:3 * DK + 1],
                                ps1[(gr + n) % 2][:, 0:heads * w].rearrange("p (h w) -> p h w", h=heads), AX.X,
                                ALU.max, negate=True).then_inc(mx_done, 1)

            def copy_o(G):
                dve.wait_ge(pv_done, G * CT + (CT + 2))
                v.tensor_copy(oT[:], psO[:]).then_inc(o_ev, 1)

            def divide(G, gr, i):
                dve.wait_ge(m_full, i + 1)
                o = psM[:].rearrange("p (t h w) -> p t h w", t=CT, h=HG)
                v.reciprocal(rec[:], o[:, :, :, DK]).then_inc(rc, 1)
                dve.wait_ge(rc, G + 1)
                for t in range(CT):
                    ins = v.tensor_tensor(attn[:, t, gr * HG * DK:(gr + 1) * HG * DK].rearrange("p (h d) -> p h d", d=DK),
                                          o[:, t, :, 0:DK],
                                          rec[:, t, :].rearrange("p (h o) -> p h o", o=1).to_broadcast([P, HG, DK]),
                                          ALU.mult)
                ins.then_inc(m_free, 1)

            def residual(c, t, i0):
                if t == 0:
                    dve.wait_ge(xr_ld, c * 16 + 16)
                dve.wait_ge(m_full, i0 + (t + 1))
                v.tensor_tensor(xres[:, t, :], xres[:, t, :], psM[:, 0:D], ALU.add).then_inc(m_free, 1)

            def logits(c, i):
                dve.wait_ge(m_full, i + 1)
                v.tensor_copy(g.logits[:, bass.ds(c * (CT * E), CT * E)], psM[:, 0:CT * E]).then_inc(m_free, 1)

            def first():
                for k in range(2):
                    for t in range(CT):
                        combine(0, 0, 0, t, k)
                moments(0, x1[:, 0], (x1_done, 1), 0, var1)
                normalize(0, xn, x1[:, 0], (rs1, 1), normed1)
                for k in range(2):
                    keys_out_of_g(gu(0, "first", f"TK_{k}"), k)
                for n in range(UN):
                    maxima(0, 0, n)

            def phase(c, c2, u, kind, gr):
                G = c * NG + gr
                nxt = not (kind == NB_ - 1 and gr == NG - 1)
                before = CT if kind == 0 else c * (2 * CT)
                for n in range(STEPS):
                    if nxt and n < UN:
                        maxima(G + 1, (gr + 1) % NG, n)
                    if n == 2 and not (kind == 0 and gr == 0):
                        copy_o(G - 1)
                    if n == 5 and not (kind == 0 and gr == 0):
                        divide(G - 1, (gr - 1) % NG, mu(c, kind, f"OT_{(gr - 1) % NG}"))
                    if turns(gr, n) == "TK" and (gr < 2 or kind != NB_ - 1):
                        keys_out_of_g(gu(c, kind, f"TK_{gr}"), (gr + 2) % NG)
                    if gr == 0 and kind != NB_ - 1:
                        un, c2n = 1 - u, (c2 if u == 0 else c2 + 1)
                        if n < CT:
                            combine(c + 1, c2n, un, n, 0)
                        if 1 <= n <= CT:
                            combine(c + 1, c2n, un, n - 1, 1)
                        if n == 6:
                            moments(0, x1[:, un], (x1_done, c + 2), before, var1)
                        if n == 8:
                            normalize(0, xn, x1[:, un], (rs1, c + 2), normed1)
                    if gr == 0 and n in OUT_AT and kind != 0:
                        residual(c - 1, OUT_AT.index(n), mu(c, kind, "out0"))
                    if gr == 1 and n == 0 and kind != 0:
                        moments(1, xres, (m_free, mu(c, kind, f"out{CT - 1}") + 2),
                                before + (0 if kind == NB_ - 1 else CT), var2)
                    if gr == 1 and n == 2 and kind != 0:
                        dve.wait_ge(xn2_st, c * 16)
                        dve.sem_inc(g.held, 1)
                        normalize(1, xn2, xres, (rs2, c), normed2)
                    if gr == 2 and n == 7 and kind != 0:
                        logits(c - 1, mu(c, kind, "rt"))

            def last():
                c = NB_
                copy_o(NB_ * NG - 1)
                divide(NB_ * NG - 1, NG - 1, mu_end("OT_3"))
                for t in range(CT):
                    residual(c - 1, t, mu_end("out0"))
                moments(1, xres, (m_free, mu_end(f"out{CT - 1}") + 2), (2 * NB_ - 1) * CT, var2)
                dve.wait_ge(xn2_st, c * 16)
                normalize(1, xn2, xres, (rs2, c), normed2)
                logits(c - 1, mu_end("rt"))

            phases(dve, first, phase, last)

        @block.tensor
        def _(pe):
            pe.sem_inc(pv_done, 2)
            pe.wait_ge(w_in, 64)
            pe.wait_ge(identr_in, 1)

            def turn(i, src, ident=g.ident, out=psG):
                pe.wait_ge(g_free, i + 1)
                for t in range(CT):
                    for k in range(2):
                        ins = pe.transpose(out[:, k, t * P:(t + 1) * P], src(t, k), ident[:, :])
                ins.then_inc(g_full, 1)

            def turn_parts(i, parts):
                turn(i, lambda t, k: parts[:, t, 2 * k:2 * k + 2, :].rearrange("p h s -> p (h s)"),
                     identr, psG[:].bitcast(F32R))

            def project(i0, t):
                pe.wait_ge(g_free, i0 + (t + 1))
                for half, lo, w in ((0, 0, 2 * D), (1, 2 * D, D)):
                    for k in range(KD):
                        ins = pe.matmul(psG[:, half, 0:w], xnT[:, k, t * P:(t + 1) * P], wqkv[:, k, lo:lo + w],
                                        start=(k == 0), stop=(k == KD - 1))
                ins.then_inc(g_full, 1)

            def score1(G, gr, n, ready):
                qi, h0, heads = UNITS1[n]
                if n == 0:
                    pe.wait_ge(g_free, ready)
                pe.wait_ge(mx_done, G * UN + (n + 1))
                w = (qi + 1) * P
                ps = ps1[(gr + n) % 2]
                for i in range(heads):
                    h = h0 + i
                    pe.matmul(ps[:, i * w:(i + 1) * w], qT[:, gr % 2, h, qi * P:w], kT[:, gr, h // 2, 0:w],
                              start=True, stop=False)
                    ins = pe.matmul(ps[:, i * w + qi * P:(i + 1) * w], identb[:, :], maskq[:, :],
                                    start=False, stop=True)
                ins.then_inc(s1_done, 1)

            def score2(G, gr, n):
                ki, h0, heads = UNITS2[n]
                pe.wait_ge(ex_done, G * UN + (n + 1))
                w = CHUNK - ki * P
                ps = ps2[(gr + n) % 2]
                some = min(heads, 2)
                for i in range(0, heads, some):
                    h = h0 + i
                    ins = pe.matmul(ps[:, i * w:(i + some) * w], kT[:, gr, h // 2, ki * P:(ki + 1) * P],
                                    q2T[:, gr % 2, h:h + some, ki * P:CHUNK], start=True, stop=True)
                ins.then_inc(s2_done, 1)

            def values(G, gr, u, ki):
                if ki == 0:
                    pe.wait_ge(o_ev, G + 1)
                pe.wait_ge(cut_done, G * CT + (ki + 1))
                w = CHUNK - ki * P
                for h in range(HG):
                    ins = pe.matmul(psO[32 * h:32 * h + 32, ki * P:CHUNK], va[:, u, ki, gr * HG + h, :],
                                    pT[:, (ki * HG + h) % 8, 0:w], start=(ki == 0), stop=(ki == CT - 1),
                                    skip_group_check=True)
                ins.then_inc(pv_done, 1)

            def turn_o(G, i):
                pe.wait_ge(o_ev, G + 2)
                pe.wait_ge(m_free, i + 1)
                for t in range(CT):
                    ins = pe.transpose(psM[:, t * P:(t + 1) * P], oT[:, t * P:(t + 1) * P], g.ident[:, :])
                ins.then_inc(m_full, 1)

            def turn_attn(i, mi):
                pe.wait_ge(m_free, mi + 2)
                turn(i, lambda t, k: attn[:, t, k * P:(k + 1) * P])

            def project_out(t, i0, ready):
                if t == 0:
                    pe.wait_ge(g_free, ready)
                pe.wait_ge(m_free, i0 + (t + 1))
                for k in range(KD):
                    ins = pe.matmul(psM[:, 0:D], attnT[:, k, t * P:(t + 1) * P], wo[:, k, :],
                                    start=(k == 0), stop=(k == KD - 1))
                ins.then_inc(m_full, 1)

            def route(i, ready):
                pe.wait_ge(g_free, ready)
                pe.wait_ge(m_free, i + 1)
                for t in range(CT):
                    for k in range(KD):
                        ins = pe.matmul(psM[:, t * E:(t + 1) * E], xnT2[:, k, t * P:(t + 1) * P], g.rw[:, k, :],
                                        start=(k == 0), stop=(k == KD - 1))
                ins.then_inc(m_full, 1)

            def first():
                pe.wait_ge(normed1, 1)
                turn(gu(0, "first", "xnT"), lambda t, k: xn[:, t, k * P:(k + 1) * P])
                for t in range(CT):
                    project(gu(0, "first", "proj0"), t)
                for k in range(2):
                    pe.wait_ge(lo_done, k + 1)
                    turn_parts(gu(0, "first", f"TQ_{k}"), q4[:, k])
                    turn_parts(gu(0, "first", f"TK_{k}"), k4[:, k])
                pe.wait_ge(consts, 1)
                pe.sem_inc(g.held, 1)
                for n in range(UN):
                    score1(0, 0, n, gu(0, "first", "TK_0") + 2)
                pe.wait_ge(mx_done, UN + 2)
                turn_parts(gu(0, "first", "T2"), q4[:, 0])

            def phase(c, c2, u, kind, gr):
                G = c * NG + gr
                more = gr < 2 or kind != NB_ - 1
                nxt = not (kind == NB_ - 1 and gr == NG - 1)
                started = not (kind == 0 and gr == 0)
                for n in range(STEPS):
                    if nxt and n < UN:
                        score1(G + 1, (gr + 1) % NG, n, g_before(c, kind, gr))
                    if n in VALUES_LATE and started:
                        values(G - 1, (gr - 1) % NG, u if gr else 1 - u, VALUES_LATE[n])
                    if n == LAG:
                        pe.wait_ge(g_free, g_before(c, kind, gr) + 1)
                    if n >= LAG:
                        score2(G, gr, n - LAG)
                    if n == 4 and started:
                        turn_o(G - 1, mu(c, kind, f"OT_{(gr - 1) % NG}"))
                    if n in VALUES_AT:
                        values(G, gr, u, VALUES_AT[n])
                    if gr == 0 and n == AT["attnT"] and kind != 0:
                        turn_attn(gu(c, kind, "attnT"), mu(c, kind, "OT_3"))
                    if gr == 2 and n == AT["x2T"] and kind != 0:
                        pe.wait_ge(normed2, c)
                        turn(gu(c, kind, "x2T"), lambda t, k: xn2[:, t, k * P:(k + 1) * P])
                    if gr == 1 and n in PROJECT_AT and kind != NB_ - 1:
                        project(gu(c, kind, "proj0"), PROJECT_AT.index(n))
                    if gr == 2 and n == 6 and kind != 0:
                        route(mu(c, kind, "rt"), gu(c, kind, "x2T") + 2)
                    if turns(gr, n) == "TQ" and more:
                        pe.wait_ge(lo_done, G + 3)
                        turn_parts(gu(c, kind, f"TQ_{gr}"), q4[:, gr % 2])
                    if turns(gr, n) == "TK" and more:
                        turn_parts(gu(c, kind, f"TK_{gr}"), k4[:, gr % 2])
                    if gr == 0 and n in OUT_AT and kind != 0:
                        project_out(OUT_AT.index(n), mu(c, kind, "out0"), gu(c, kind, "attnT") + 2)
                    if gr == 0 and n == AT["xnT"] and kind != NB_ - 1:
                        pe.wait_ge(normed1, c + 2)
                        turn(gu(c, kind, "xnT"), lambda t, k: xn[:, t, k * P:(k + 1) * P])
                    if n == AT["T2"] and nxt:
                        pe.wait_ge(mx_done, G * UN + (2 * UN + 2))
                        turn_parts(gu(c, kind, f"T2_{gr}"), q4[:, (gr + 1) % 2])

            def last():
                for ki in (2, 3):
                    values(NB_ * NG - 1, NG - 1, 1, ki)
                turn_o(NB_ * NG - 1, mu_end("OT_3"))
                turn_attn(gu(0, "end", "attnT"), mu_end("OT_3"))
                for t in range(CT):
                    project_out(t, mu_end("out0"), gu(0, "end", "attnT") + 2)
                pe.wait_ge(normed2, NB_)
                turn(gu(0, "end", "x2T"), lambda t, k: xn2[:, t, k * P:(k + 1) * P])
                route(mu_end("rt"), gu(0, "end", "x2T") + 2)

            phases(pe, first, phase, last)


def macaron_kernel(nc, x, W_q, W_k, W_v, W_o, router_w, expert_bias, shared_w1, shared_w2, shared_w3,
                   routed_w1, routed_w2, routed_w3, out):
    assert shared_w1.shape[0] == 1
    z = Shapes(x, router_w, shared_w1[0], routed_w1)
    dram = scratch(nc, z)
    dram.router_w, dram.expert_bias = router_w, expert_bias
    dram.shared_w1, dram.shared_w2, dram.shared_w3 = shared_w1[0], shared_w2[0], shared_w3[0]
    dram.routed_w1, dram.routed_w2, dram.routed_w3 = routed_w1, routed_w2, routed_w3
    dram.W_q, dram.W_k, dram.W_v, dram.W_o = W_q, W_k, W_v, W_o
    x_flat = x.rearrange("b s d -> (b s) d")
    with ExitStack() as ctx:
        g = residents(nc, z, ctx)
        with nc.cleanup_on_exit():
            setup(nc, z, g, dram)
            norm_first(nc, z, g, dram, x_flat)
        feed_forward(nc, z, g, dram, "f1_", x_flat, True)
        attention(nc, z, g, dram)
        feed_forward(nc, z, g, dram, "f2_", dram.x2, False)
        combine_last(nc, z, g, dram, out.rearrange("b s d -> (b s) d"))


_INS = ['L0_attn_x', 'L0_attn_W_q', 'L0_attn_W_k', 'L0_attn_W_v', 'L0_attn_W_o', 'L0_ffn_router_w',
        'L0_ffn_expert_bias', 'L0_ffn_shared_w1', 'L0_ffn_shared_w2', 'L0_ffn_shared_w3', 'L0_ffn_routed_w1',
        'L0_ffn_routed_w2', 'L0_ffn_routed_w3']
_TURNED = ('L0_attn_W_q', 'L0_attn_W_k', 'L0_attn_W_v', 'L0_attn_W_o')


def kernel(**inputs):
    import numpy as _np
    import concourse.bacc as _bacc
    from concourse import mybir as _mybir
    from concourse.bass_utils import run_bass_kernel_spmd as _run

    nc = _bacc.Bacc("TRN2", target_bir_lowering=False, num_devices=1)
    arrays, args = {}, []
    for name in _INS:
        a = _np.asarray(inputs[name])
        a = _np.ascontiguousarray(a.T if name in _TURNED else a)
        arrays[f"in_{name}_dram"] = a
        args.append(nc.dram_tensor(f"in_{name}_dram", a.shape, _mybir.dt.from_np(a.dtype), kind="ExternalInput").ap())
    out = nc.dram_tensor("out_0_dram", args[0].shape, _mybir.dt.float32, kind="ExternalOutput").ap()
    macaron_kernel(nc, *args, out)
    r = _run(nc, [arrays], core_ids=[0])
    return r.results[0]["out_0_dram"]
```

```python
import math
from contextlib import ExitStack

import concourse.bass as bass
from concourse import mybir

P = 128
F32 = mybir.dt.float32
F32R = mybir.dt.float32r
BF16 = mybir.dt.bfloat16
I32 = mybir.dt.int32
U32 = mybir.dt.uint32
ALU = mybir.AluOpType
ACT = mybir.ActivationFunctionType
AX = mybir.AxisListType

CT = 4
CHUNK = CT * P
EPS = 1e-5
TOPK = 2


class Shapes:

    def __init__(self, x, router_w, shared_w1, routed_w1):
        self.B, self.S, self.D = x.shape
        self.T = self.B * self.S
        self.NT = self.T // P
        self.NC = self.T // CHUNK
        self.KD = self.D // P
        self.E = router_w.shape[1]
        self.RH = routed_w1.shape[2]
        self.KR = self.RH // P
        self.SH = shared_w1.shape[-1]
        self.JS = self.SH // P
        most = (self.T * TOPK + self.E * (P - 1)) // P
        self.NB = -(-most // 4) * 4
        assert self.S == CHUNK and self.D % P == 0 and self.RH == self.D


class Mem:

    def __init__(self, nc, ctx, tag=""):
        self.nc, self.ctx, self.tag = nc, ctx, tag

    def sb(self, name, shape, dt=F32):
        return self.ctx.enter_context(self.nc.sbuf_tensor(self.tag + name, shape, dt))

    def ps(self, name, shape, dt=F32):
        return self.ctx.enter_context(self.nc.psum_tensor(self.tag + name, shape, dt))

    def sem(self, name):
        return self.nc.alloc_semaphore(self.tag + name)

    def sems(self, name, n):
        return [self.sem(f"{name}{i}") for i in range(n)]


def setup(nc, z, g, dram):
    with ExitStack() as ctx:
        m = Mem(nc, ctx, "set_")
        made = m.sem("made")
        loaded = m.sem("loaded")
        block = ctx.enter_context(nc.Block())
        KD, E = z.KD, z.E

        @block.gpsimd
        def _(pool):
            n = [0]

            def done(ins):
                n[0] += 1
                ins.then_inc(made, 1)
                pool.wait_ge(made, n[0])

            done(nc.gpsimd.memset(g.ident[:], 0.0))
            done(nc.gpsimd.affine_select(out=g.ident[:], in_=g.ident[:], compare_op=ALU.not_equal, fill=1.0,
                                         base=0, pattern=[[-1, P]], channel_multiplier=1))
            done(nc.gpsimd.memset(g.before[:], 1.0))
            done(nc.gpsimd.affine_select(out=g.before[:], in_=g.before[:], compare_op=ALU.is_gt, fill=0.0,
                                         base=0, pattern=[[1, P]], channel_multiplier=-1))
            done(nc.gpsimd.memset(g.ones[:], 1.0))
            done(nc.gpsimd.memset(g.zero[:], 0.0))
            done(nc.gpsimd.memset(g.mhalf[:], -0.5))
            done(nc.gpsimd.memset(g.eps[:], EPS))
            done(nc.gpsimd.iota(g.rev_i[:], pattern=[[-1, E]], base=E, channel_multiplier=0))
            done(nc.gpsimd.iota(g.blk_i[:], pattern=[[1, z.NB]], base=0, channel_multiplier=0))
            done(nc.gpsimd.tensor_copy(g.rev[:], g.rev_i[:]))
            done(nc.gpsimd.tensor_copy(g.blk[:], g.blk_i[:]))
            done(nc.gpsimd.memset(g.keep[:], 1.0))
            done(nc.gpsimd.memset(g.keep[:, :, 0:1], 0.0))

        @block.sync
        def _(sp):
            n = 0

            def load(dst, src):
                nonlocal n
                sp.dma_start(dst, src).then_inc(loaded, 16)
                n += 16

            load(g.rw[:], dram.router_w.rearrange("(k p) e -> p k e", p=P))
            load(g.bias[:], dram.expert_bias.rearrange("(o e) -> o e", o=1).to_broadcast([P, E]))
            sp.wait_ge(loaded, n)


def norm_first(nc, z, g, dram, x_src):
    with ExitStack() as ctx:
        m = Mem(nc, ctx, "nf_")
        x = m.sb("x", [P, z.NT * z.D])
        xn = m.sb("xn", [P, 2, CT, z.D])
        xnT = m.sb("xnT", [P, 2, z.KD, CHUNK])
        stat = m.sb("stat", [P, 2, CT, 6])
        mv = m.sb("mv", [P, 2, CT, 2])
        veps = m.sb("veps", [P, 2, CT])
        rstd = m.sb("rstd", [P, 2, CT])
        psT = m.ps("psT", [P, 2, z.KD, CHUNK])
        psL = m.ps("psL", [P, 512])
        x_in = m.sems("x_in", 2)
        stats = m.sem("stats")
        var = m.sem("var")
        eps_in = m.sem("eps_in")
        rs = m.sem("rs")
        normed = m.sem("normed")
        turned = m.sem("turned")
        xnT_in = m.sem("xnT_in")
        logit = m.sem("logit")
        logit_in = m.sem("logit_in")
        xn_out = m.sems("xn_out", 2)
        block = ctx.enter_context(nc.Block())

        @block.sync
        def _(sp):
            def load(c, u):
                sp.dma_start(x[:, bass.ds(c * (CT * z.D), CT * z.D)].rearrange("p (t d) -> p t d", d=z.D),
                             x_src[bass.ds(c * CHUNK, CHUNK), :].rearrange("(t p) d -> p t d", p=P)
                             ).then_inc(x_in[u], 16)

            def store(c, c2, u, more):
                sp.wait_ge(normed, c + 1)
                sp.sem_inc(g.held, 1)
                sp.dma_start(dram.xn[bass.ds(c * CHUNK, CHUNK), :].rearrange("(t p) d -> p t d", p=P), xn[:, u]
                             ).then_inc(xn_out[u], 16)
                if more:
                    sp.wait_ge(x_in[u], c2 * 16 + 32)
                    sp.sem_inc(g.held, 1)
                    load(c + 4, u)
                sp.wait_ge(xnT_in, c + 1)
                sp.sem_inc(g.held, 1)
                sp.dma_start(dram.xnT[:, :, bass.ds(c * CHUNK, CHUNK)], xnT[:, u]).then_inc(xn_out[u], 16)

            load(0, 0)
            load(1, 1)
            for u in range(2):
                sp.wait_ge(x_in[u], 16)
                load(2 + u, u)
            with sp.Fori(0, z.NC // 2 - 2) as c2:
                for u in range(2):
                    store(c2 * 2 + u, c2, u, True)
            for c in range(z.NC - 4, z.NC):
                store(c, c // 2, c % 2, False)
            for u in range(2):
                sp.wait_ge(xn_out[u], 32 * (z.NC // 2))

        @block.vector
        def _(dve):
            def tile(c, t):
                return x[:, bass.ds(c * (CT * z.D) + t * z.D, z.D)]

            def moments(c, c2, u):
                dve.wait_ge(x_in[u], c2 * 16 + 16)
                for t in range(CT):
                    nc.vector.bn_stats(stat[:, u, t, :], tile(c, t)).then_inc(stats, 1)
                dve.wait_ge(stats, c * CT + CT)
                dve.sem_inc(g.held, 1)
                for t in range(CT):
                    ins = nc.vector.bn_aggr(mv[:, u, t, :], stat[:, u, t, :])
                ins.then_inc(var, 1)

            def normalize(c, c2, u, first):
                dve.wait_ge(rs, c + 1)
                if not first:
                    dve.wait_ge(xn_out[u], c2 * 32)
                for t in range(CT):
                    ins = nc.vector.tensor_scalar(xn[:, u, t, :], tile(c, t), mv[:, u, t, 0:1],
                                                  rstd[:, u, t:t + 1], ALU.subtract, ALU.mult)
                ins.then_inc(normed, 1)

            def logits(c):
                dve.wait_ge(logit, c + 1)
                nc.vector.tensor_copy(g.logits[:, bass.ds(c * (CT * z.E), CT * z.E)],
                                      psL[:, 0:CT * z.E]).then_inc(logit_in, 1)

            def chunk(c, c2, u, first):
                moments(c + 1, c2 + u, 1 - u)
                normalize(c, c2, u, first)
                if not first:
                    logits(c - 2)

            moments(0, 0, 0)
            for u in range(2):
                chunk(u, 0, u, True)
            with dve.Fori(1, z.NC // 2 - 1) as c2:
                for u in range(2):
                    chunk(c2 * 2 + u, c2, u, False)
            chunk(z.NC - 2, z.NC // 2 - 1, 0, False)
            normalize(z.NC - 1, z.NC // 2 - 1, 1, False)
            logits(z.NC - 3)
            logits(z.NC - 2)
            logits(z.NC - 1)

        @block.gpsimd
        def _(pool):
            with pool.Fori(0, z.NC // 2) as c2:
                for u in range(2):
                    c = c2 * 2 + u
                    pool.wait_ge(var, c + 1)
                    nc.gpsimd.tensor_tensor(veps[:, u, :], mv[:, u, :, 1], g.eps[:, 0:CT], ALU.add).then_inc(eps_in, 1)
                    pool.wait_ge(eps_in, c + 1)
                    nc.gpsimd.tensor_tensor(rstd[:, u, :], veps[:, u, :], g.mhalf[:, 0:CT], ALU.pow).then_inc(rs, 1)

        @block.tensor
        def _(pe):
            def turn(c, u, first):
                pe.wait_ge(normed, c + 1)
                if not first:
                    pe.wait_ge(xnT_in, c - 1)
                for t in range(CT):
                    for k in range(z.KD):
                        ins = pe.transpose(psT[:, u, k, t * P:(t + 1) * P], xn[:, u, t, k * P:(k + 1) * P],
                                           g.ident[:, :])
                ins.then_inc(turned, 1)

            def route(c, u, first):
                pe.wait_ge(xnT_in, c + 1)
                if not first:
                    pe.wait_ge(logit_in, c)
                for t in range(CT):
                    for k in range(z.KD):
                        ins = pe.matmul(psL[:, t * z.E:(t + 1) * z.E], xnT[:, u, k, t * P:(t + 1) * P],
                                        g.rw[:, k, :], start=(k == 0), stop=(k == z.KD - 1))
                ins.then_inc(logit, 1)

            turn(0, 0, True)
            turn(1, 1, True)
            route(0, 0, True)
            with pe.Fori(1, z.NC // 2) as c2:
                for u in range(2):
                    turn(c2 * 2 + u, u, False)
                    route(c2 * 2 + u - 1, 1 - u, False)
            route(z.NC - 1, 1, False)

        @block.scalar
        def _(act):
            def chunk(c, c2, u, first):
                act.wait_ge(turned, c + 1)
                if not first:
                    act.wait_ge(xn_out[u], c2 * 32)
                    act.wait_ge(logit, c - 1)
                nc.scalar.copy(xnT[:, u], psT[:, u]).then_inc(xnT_in, 1)

            for u in range(2):
                chunk(u, 0, u, True)
            with act.Fori(1, z.NC // 2) as c2:
                for u in range(2):
                    chunk(c2 * 2 + u, c2, u, False)


def feed_forward(nc, z, g, dram, tag, x_src, fill, out):
    KD, KR, E, NT, RH = z.KD, z.KR, z.E, z.NT, z.RH
    TE = NT * E
    NB, NC = z.NB, z.NC
    with ExitStack() as ctx:
        m = Mem(nc, ctx, tag)
        ew12 = m.sb("ew12", [P, E, KD, 2 * RH])
        ew3 = m.sb("ew3", [P, E, KR, z.D])
        ewf = ew12[:].rearrange("p e k n -> p (e k n)")
        used = [0]

        def early(shape):
            at, n = used[0], math.prod(shape)
            used[0] += n
            axes = dict(zip("abc", shape))
            names = " ".join(axes)
            return ewf[:, at:at + n].rearrange(f"p ({names}) -> p {names}", **axes)

        raw12 = early([KD, 2, z.SH])
        raw3 = early([z.JS, z.D])
        sw12 = m.sb("sw12", [P, 2, KD, 2, z.SH], F32R)
        sw3 = m.sb("sw3", [P, 2, z.JS, z.D], F32R)
        rawx = m.sb("rawx", [P, KD, CHUNK])
        xparts = m.sb("xparts", [P, 2, 2, KD, CHUNK], F32R)
        xr = m.sb("xr", [P, 2, CT, z.D])
        sil = m.sb("sil", [P, 2, CHUNK])
        hid = m.sb("hid", [P, 2, CHUNK])
        hparts = m.sb("hparts", [P, 2, 2, CHUNK], F32R)
        score, sel, tmp, one1, one2 = (early([NT, E]) for _ in range(5))
        count, upto = early([E, NT]), early([E, NT])
        both = m.sb("both", [P, NT, E], BF16)
        top = m.sb("top", [P, 6, NT])
        small = m.sb("small", [P, 8, E])
        small_i = m.sb("small_i", [P, 2, E], I32)
        bexp = m.sb("bexp", [1, NB])
        bexp_i = m.sb("bexp_i", [1, NB], I32)
        slot_f = m.sb("slot_f", [P, NT, TOPK])
        xq = m.sb("xq", [P, 2, CT, z.D])
        idx = m.sb("idx", [P, 4, CT * TOPK], U32)
        bcmp = xq[0:1].rearrange("p u t d -> p (u t d)")[:, 0:NB * E].rearrange("p (b e) -> p b e", e=E)
        xs = rawx[:].rearrange("p k (s d) -> p (k s) d", d=z.D)
        silr, hr = sil[:, 0].rearrange("p (s d) -> p s d", s=2), sil[:, 1].rearrange("p (s d) -> p s d", s=2)
        xsT, hrT = hid[:, 0].rearrange("p (s d) -> p s d", s=2), hid[:, 1].rearrange("p (s d) -> p s d", s=2)
        yr = xq[:, 0]
        assert used[0] <= E * KD * 2 * RH and KD * CHUNK == 4 * z.D and CHUNK == 2 * RH
        GS = 4
        GW = CT * TOPK * z.D
        yg = ewf[:, 0:GS * GW].rearrange("p (s t k d) -> p s t k d", s=GS, t=CT, k=TOPK)
        acc = ewf[:, GS * GW:GS * GW + 2 * CT * z.D].rearrange("p (u t d) -> p u t d", u=2, t=CT)
        bank = [m.ps(f"bank{i}", [P, 512]) for i in range(8)]
        psA, psB = bank[0:2], bank[2:4]
        psO = [bank[4 + t // 2][:, (t % 2) * z.D:(t % 2 + 1) * z.D] for t in range(CT)]
        psR, psC = bank[6], bank[7]
        rUp, rTx, rTh, rY = bank[0:2], bank[2], bank[3], bank[4:6]

        sw_in = m.sems("sw_in", 6)
        w_hi = m.sem("w_hi")
        w_lo01 = m.sem("w_lo01")
        w_lo = m.sem("w_lo")
        ew_in = m.sem("ew_in")
        rawx_ld = m.sem("rawx_ld")
        x_hi = m.sem("x_hi")
        x_lo = m.sem("x_lo")
        xr_ld = m.sems("xr_ld", 2)
        sh_st = m.sems("sh_st", 2)
        scored = m.sem("scored")
        rt = m.sem("rt")
        picked = m.sem("picked")
        ranked = m.sem("ranked")
        placed = m.sem("placed")
        a_done = m.sem("a_done")
        b_done = m.sem("b_done")
        s_done = m.sem("s_done")
        h_done = m.sem("h_done")
        h_hi = m.sem("h_hi")
        h_lo = m.sem("h_lo")
        o_done = m.sem("o_done")
        sh_done = m.sem("sh_done")
        xq_ld = m.sems("xq_ld", 2)
        idx_in = m.sem("idx_in")
        scat = m.sems("scat", 2)
        all_scat = m.sem("all_scat")
        xs_ld = m.sems("xs_ld", 4)
        tx_done = m.sem("tx_done")
        xT_ev = m.sem("xT_ev")
        rup_done = m.sem("rup_done")
        rs_done = m.sem("rs_done")
        rh_done = m.sem("rh_done")
        th_done = m.sem("th_done")
        hT_ev = m.sem("hT_ev")
        dn_done = m.sem("dn_done")
        y_done = m.sem("y_done")
        y_st = m.sems("y_st", 4)
        acc_ld = m.sems("acc_ld", 2)
        y_ld = m.sems("y_ld", GS)
        mid = m.sem("mid")
        summed = m.sem("summed")
        out_st = m.sems("out_st", 2)
        block = ctx.enter_context(nc.Block())

        LAST = NB + 1

        def steps(eng, body):
            for r in range(4):
                body(0, r, lambda lag, n=r: 0 <= n - lag < NB)
            assert (NB // 4 - 2) % 3 == 0
            with eng.Fori(0, (NB // 4 - 2) // 3) as turn:
                for part in range(3):
                    for r in range(4):
                        body(turn * 3 + (part + 1), r, lambda lag: True)
            for n in range(NB - 4, LAST + 1):
                body(n // 4, n % 4, lambda lag, n=n: 0 <= n - lag < NB)

        BEHIND = NC - 2

        def chunks_before(eng, body):
            body(0, 0, 0, True, False)
            body(1, 0, 1, False, False)
            with eng.Fori(1, NC // 2 - 1) as c2:
                for u in range(2):
                    body(c2 * 2 + u, c2, u, False, False)

        def chunks_behind(eng, body):
            body(NC - 2, NC // 2 - 1, 0, True, False)
            body(NC - 1, NC // 2 - 1, 1, False, True)

        HALF = z.SH // 2
        cols = [(w, h) for h in range(2) for w in range(2)]
        PIECES = ([(raw12[:, :, w, h * HALF:(h + 1) * HALF], sw12[:, :, :, w, h * HALF:(h + 1) * HALF])
                   for w, h in cols]
                  + [(raw3[:, h * (z.JS // 2):(h + 1) * (z.JS // 2)], sw3[:, :, h * (z.JS // 2):(h + 1) * (z.JS // 2)])
                     for h in range(2)])

        @block.sync
        def _(sp):
            def load_x(c):
                sp.dma_start(rawx[:], dram.xnT[:, :, bass.ds(c * CHUNK, CHUNK)]).then_inc(rawx_ld, 16)

            def load_res(c, u):
                sp.dma_start(xr[:, u], x_src[bass.ds(c * CHUNK, CHUNK), :].rearrange("(t p) d -> p t d", p=P)
                             ).then_inc(xr_ld[u], 16)

            def store(c, u):
                sp.wait_ge(sh_done, c * 4 + 8)
                sp.sem_inc(g.held, 1)
                sp.dma_start(dram.sh[bass.ds(c * CHUNK, CHUNK), :].rearrange("(t p) d -> p t d", p=P), xr[:, u]
                             ).then_inc(sh_st[u], 16)

            load_x(0)
            wsrc = [w.rearrange("(k p) n -> p k n", p=P) for w in (dram.shared_w1, dram.shared_w2, dram.shared_w3)]
            for i, (w, h) in enumerate(cols):
                sp.dma_start(PIECES[i][0], wsrc[w][:, :, h * HALF:(h + 1) * HALF]).then_inc(sw_in[i], 16)
            for h in range(2):
                sp.dma_start(PIECES[4 + h][0], wsrc[2][:, h * (z.JS // 2):(h + 1) * (z.JS // 2), :]
                             ).then_inc(sw_in[4 + h], 16)
            load_res(0, 0)
            load_res(1, 1)
            sp.wait_ge(x_lo, 1)
            load_x(1)
            if fill:
                for b0 in range(0, NB, 8):
                    sp.dma_start(dram.xs[b0 * P:(b0 + 8) * P, :].rearrange("(b p) d -> p b d", p=P),
                                 g.zero[:].rearrange("p (o d) -> p o d", o=1).to_broadcast([P, 8, z.D])
                                 ).then_inc(g.filled, 16)

            PER = E // (BEHIND - 2)
            assert PER * (BEHIND - 2) == E

            def load_expert(e):
                for dst, src in ((ew12[:, bass.ds(e, 1), :, 0:RH], dram.routed_w1),
                                 (ew12[:, bass.ds(e, 1), :, RH:], dram.routed_w2),
                                 (ew3[:, bass.ds(e, 1)], dram.routed_w3)):
                    sp.dma_start(dst, src[bass.ds(e, 1)].rearrange("e (k p) n -> p e k n", p=P)).then_inc(ew_in, 16)

            with sp.Fori(1, NC // 2 - 1) as c2:
                for u in range(2):
                    sp.wait_ge(x_lo, c2 * 2 + u)
                    sp.sem_inc(g.held, 1)
                    load_x(c2 * 2 + u)
                    store(c2 * 2 + u - 2, u)
                    sp.wait_ge(sh_st[u], c2 * 16)
                    sp.sem_inc(g.held, 1)
                    load_res(c2 * 2 + u, u)
                    sp.wait_ge(placed, 1)
                    sp.sem_inc(g.held, 1)
                    sp.wait_ge(w_lo, 4)
                    sp.sem_inc(g.held, 1)
                    for i in range(PER):
                        load_expert((c2 - 1) * (2 * PER) + (u * PER + i))
            sp.wait_ge(x_lo, BEHIND)
            load_x(BEHIND)
            for u in range(2):
                store(BEHIND - 2 + u, u)
                sp.wait_ge(sh_st[u], BEHIND // 2 * 16)
                load_res(BEHIND + u, u)
            sp.wait_ge(x_lo, BEHIND + 1)
            sp.sem_inc(g.held, 1)

            def fetch(q, r):
                sp.wait_ge(tx_done, q * 4 + r + 1)
                sp.sem_inc(g.held, 1)
                sp.dma_start(xs[:, r], dram.xs[bass.ds(q * (4 * P) + r * P, P), :]).then_inc(xs_ld[r], 16)

            def put(q, r):
                sp.wait_ge(y_done, q * 4 + r + 3)
                sp.sem_inc(g.held, 1)
                sp.dma_start(dram.ys[bass.ds(q * (4 * P) + r * P, P), :], yr[:, r]).then_inc(y_st[r], 16)

            sp.wait_ge(all_scat, 1)
            for r in range(4):
                fetch(0, r)
            with sp.Fori(0, NB // 4 - 1) as q:
                for r in range(4):
                    fetch(q + 1, r)
                    put(q, r)
            for r in range(4):
                put(NB // 4 - 1, r)
            sp.wait_ge(tx_done, NB + 4)
            load_x(NC - 1)
            for r in range(4):
                sp.wait_ge(y_st[r], 16 * (NB // 4 + 1))
            def load_acc(c, u):
                sp.dma_start(acc[:, u], dram.sh[bass.ds(c * CHUNK, CHUNK), :].rearrange("(t p) d -> p t d", p=P)
                             ).then_inc(acc_ld[u], 16)

            def store_out(c, u, src):
                sp.wait_ge(summed, c + 1)
                sp.sem_inc(g.held, 1)
                sp.dma_start(out[bass.ds(c * CHUNK, CHUNK), :].rearrange("(t p) d -> p t d", p=P), src[:, u]
                             ).then_inc(out_st[u], 16)

            load_acc(0, 0)
            load_acc(1, 1)
            with sp.Fori(0, BEHIND // 2 - 1) as c2:
                for u in range(2):
                    store_out(c2 * 2 + u, u, acc)
                    sp.wait_ge(out_st[u], c2 * 16 + 16)
                    sp.sem_inc(g.held, 1)
                    load_acc(c2 * 2 + u + 2, u)
            for c in range(BEHIND - 2, NC):
                store_out(c, c % 2, acc if c < BEHIND else xr)
            for u in range(2):
                sp.wait_ge(out_st[u], 16 * (NC // 2))

        @block.gpsimd
        def _(pool):
            for i, (raw, parts) in enumerate(PIECES[2:]):
                pool.wait_ge(w_hi, i + 3)
                nc.gpsimd.tensor_tensor(parts[:, 1], raw, parts[:, 0], ALU.subtract).then_inc(w_lo, 1)
            pool.wait_ge(placed, 1)

            def load(c, u):
                pool.dma_start(xq[:, u], dram.xn[bass.ds(c * CHUNK, CHUNK), :].rearrange("(t p) d -> p t d", p=P)
                               ).then_inc(xq_ld[u], 16)

            def send(c, c2, u):
                pool.wait_ge(xq_ld[u], c2 * 16 + 16)
                nc.gpsimd.tensor_copy(idx[:, u, :], g.slot[:, bass.ds(c * (CT * TOPK), CT * TOPK)]
                                      ).then_inc(idx_in, 1)
                pool.wait_ge(idx_in, c + 1)
                pool.sem_inc(g.held, 1)
                for t in range(CT):
                    for k in range(TOPK):
                        nc.gpsimd.indirect_dma_start(
                            dram.xs, bass.IndirectOffsetOnAxis(ap=idx[:, u, TOPK * t + k:TOPK * t + k + 1], axis=0),
                            xq[:, u, t, :], None).then_inc(scat[u], 16)

            per = 16 * CT * TOPK
            pool.wait_ge(g.filled, 16 * (NB // 8))
            pool.sem_inc(g.held, 1)
            load(0, 0)
            load(1, 1)
            send(0, 0, 0)
            send(1, 0, 1)
            with pool.Fori(1, NC // 2) as c2:
                for u in range(2):
                    pool.wait_ge(scat[u], c2 * per)
                    load(c2 * 2 + u, u)
                for u in range(2):
                    send(c2 * 2 + u, c2, u)
            for u in range(2):
                pool.wait_ge(scat[u], per * (NC // 2))
            pool.sem_inc(all_scat, 1)

            def gather(c, s, first):
                if not first:
                    pool.wait_ge(summed, c - (GS - 1))
                nc.gpsimd.tensor_copy(idx[:, s, :], g.slot[:, bass.ds(c * (CT * TOPK), CT * TOPK)]
                                      ).then_inc(idx_in, 1)
                pool.wait_ge(idx_in, c + (NC + 1))
                pool.sem_inc(g.held, 1)
                for t in range(CT):
                    for k in range(TOPK):
                        nc.gpsimd.indirect_dma_start(
                            yg[:, s, t, k, :], None, dram.ys,
                            bass.IndirectOffsetOnAxis(ap=idx[:, s, TOPK * t + k:TOPK * t + k + 1], axis=0)
                        ).then_inc(y_ld[s], 16)

            for r in range(4):
                pool.wait_ge(y_st[r], 16 * (NB // 4 + 1))
            for s in range(GS):
                gather(s, s, True)
            with pool.Fori(1, NC // GS) as cs:
                for s in range(GS):
                    gather(cs * GS + s, s, False)

        @block.scalar
        def _(act):
            def split_x(c, u):
                act.wait_ge(rawx_ld, c * 16 + 16)
                nc.scalar.copy(xparts[:, u, 0], rawx[:]).then_inc(x_hi, 1)

            nc.scalar.activation(score.rearrange("p t e -> p (t e)"), g.logits[:], ACT.Sigmoid).then_inc(scored, 1)
            split_x(0, 0)
            for i, (raw, parts) in enumerate(PIECES):
                act.wait_ge(sw_in[i], 16)
                nc.scalar.copy(parts[:, 0], raw).then_inc(w_hi, 1)

            def chunk(c, c2, u, fresh, last):
                for j in range(z.JS):
                    n = c * z.JS + j
                    act.wait_ge(a_done, n + 1)
                    nc.scalar.activation(sil[:, j % 2, :], psA[j % 2][:, :], ACT.Silu).then_inc(s_done, 1)
                    act.wait_ge(h_done, n + 3)
                    nc.scalar.copy(hparts[:, j % 2, 0], hid[:, j % 2]).then_inc(h_hi, 1)
                    if j == 2 and not last:
                        split_x(c + 1, 1 - u)

            chunks_before(act, chunk)
            act.sem_inc(xT_ev, 1)

            def step(q, r, has):
                i = q * 4 + r
                if has(0):
                    act.wait_ge(rup_done, i + 3)
                    nc.scalar.activation(silr[:, r % 2, :], rUp[r % 2][:, 0:RH], ACT.Silu).then_inc(rs_done, 1)
                if has(-1):
                    evacuate(i + 1, (r + 1) % 2)

            def evacuate(i, s):
                act.wait_ge(tx_done, i + 5)
                act.wait_ge(rup_done, i + 1)
                nc.scalar.copy(xsT[:, s, :], rTx[:, 0:KD * P]).then_inc(xT_ev, 1)

            evacuate(0, 0)
            steps(act, step)
            chunks_behind(act, chunk)

        @block.vector
        def _(dve):
            dve.sem_inc(h_done, 2)
            dve.sem_inc(sh_done, 4)
            n = [0]

            def link(ins):
                n[0] += 1
                ins.then_inc(rt, 1)
                dve.wait_ge(rt, n[0])

            v = nc.vector
            over_t = lambda a: a.rearrange("p (o e) -> p o e", o=1).to_broadcast([P, NT, E])
            over_e = lambda a: a.rearrange("p (t o) -> p t o", o=1).to_broadcast([P, NT, E])
            def low_x(u, c):
                dve.wait_ge(x_hi, c + 1)
                v.tensor_tensor(xparts[:, u, 1], rawx[:], xparts[:, u, 0], ALU.subtract).then_inc(x_lo, 1)

            def largest(k):
                link(v.tensor_reduce(top[:, k, :], sel, AX.X, ALU.max))
                link(v.tensor_tensor(tmp, sel, over_e(top[:, k, :]), ALU.is_equal))

            def first_of(k, one):
                link(v.tensor_tensor(tmp, tmp, over_t(g.rev[:]), ALU.mult))
                link(v.tensor_reduce(top[:, 2 + k, :], tmp, AX.X, ALU.max))
                link(v.tensor_tensor(one, over_t(g.rev[:]), over_e(top[:, 2 + k, :]), ALU.is_equal))

            def biased():
                dve.wait_ge(scored, 1)
                link(v.tensor_tensor(sel, score, over_t(g.bias[:]), ALU.add))
                largest(0)

            def without_first():
                link(v.scalar_tensor_tensor(sel, one1, -3.0e38, sel, ALU.mult, ALU.add))
                largest(1)

            def second():
                first_of(1, one2)
                link(v.tensor_tensor(both[:], one1, one2, ALU.add))
                dve.sem_inc(picked, 1)

            def gates(k, one):
                link(v.tensor_tensor(tmp, score, one, ALU.mult))
                link(v.tensor_reduce(top[:, 4 + k, :], tmp, AX.X, ALU.add))
                link(v.tensor_scalar(g.gate[:, :, k], top[:, 4 + k, :], 0.5, None, ALU.mult))

            def tile_counts():
                dve.wait_ge(ranked, 1)
                link(v.tensor_copy(count, psC[:, :].rearrange("p (t e) -> p e t", e=E)))
                link(v.tensor_tensor_scan(upto.rearrange("p e t -> p (e t)"), g.keep[:].rearrange("p e t -> p (e t)"),
                                          count.rearrange("p e t -> p (e t)"), 0.0, ALU.mult, ALU.add))

            def expert_blocks():
                link(v.tensor_scalar(small[:, 0, :], upto[:, :, NT - 1], float(P - 1), None, ALU.add))
                link(v.tensor_copy(small_i[:, 0, :], small[:, 0, :]))
                link(v.tensor_single_scalar(small_i[:, 1, :], small_i[:, 0, :], int(math.log2(P)),
                                            ALU.logical_shift_right))
                link(v.tensor_copy(small[:, 1, :], small_i[:, 1, :]))
                link(v.memset(small[:, 2, :], 1.0))
                link(v.tensor_tensor_scan(small[:, 3, :], small[:, 2, :], small[:, 1, :], 0.0, ALU.mult, ALU.add))
                link(v.tensor_tensor(small[:, 4, :], small[:, 3, :], small[:, 1, :], ALU.subtract))
                link(v.tensor_scalar(small[:, 5, :], small[:, 4, :], float(P), None, ALU.mult))

            def ranks():
                link(v.tensor_tensor(upto, upto, count, ALU.subtract))
                link(v.tensor_tensor(upto, upto, small[:, 5, :].rearrange("p (e o) -> p e o", o=1)
                                     .to_broadcast([P, E, NT]), ALU.add))
                link(v.tensor_tensor(sel, psR[:, :].rearrange("p (t e) -> p t e", e=E),
                                     upto.rearrange("p e t -> p t e"), ALU.add))

            def slots():
                for k, one in enumerate((one1, one2)):
                    link(v.tensor_tensor(tmp, sel, one, ALU.mult))
                    link(v.tensor_reduce(slot_f[:, :, k], tmp, AX.X, ALU.add))
                link(v.tensor_copy(g.slot[:], slot_f[:].rearrange("p t k -> p (t k)")))

            def block_experts():
                link(v.tensor_tensor(bcmp, small[0:1, 3, :].rearrange("p (o e) -> p o e", o=1).to_broadcast([1, NB, E]),
                                     g.blk[0:1, :].rearrange("p (b o) -> p b o", o=1).to_broadcast([1, NB, E]),
                                     ALU.is_le))
                link(v.tensor_reduce(bexp[:], bcmp, AX.X, ALU.add))
                link(v.tensor_scalar(bexp[:], bexp[:], float(E - 1), None, ALU.min))
                link(v.tensor_copy(bexp_i[:], bexp[:]))
                dve.sem_inc(placed, 1)

            def residual(c, c2, u):
                dve.wait_ge(xr_ld[u], c2 * 16 + 16)
                for t in range(CT):
                    if t % 2 == 0:
                        dve.wait_ge(o_done, c * CT + t + 2)
                    v.scalar_tensor_tensor(xr[:, u, t, :], psO[t], 0.5, xr[:, u, t, :],
                                           ALU.mult, ALU.add).then_inc(sh_done, 1)

            def routing(n):
                if n == 0:
                    biased()
                elif n == 1:
                    first_of(0, one1)
                elif n == 2:
                    without_first()
                elif n == 3:
                    second()
                elif n in (4, 5):
                    gates(n - 4, (one1, one2)[n - 4])
                elif n == 6:
                    tile_counts()
                elif n == 7:
                    expert_blocks()
                elif n == 9:
                    ranks()
                elif n == 10:
                    slots()
                elif n == 11:
                    block_experts()

            def chunk(c, c2, u, fresh, last):
                for j in range(z.JS):
                    n = c * z.JS + j
                    dve.wait_ge(s_done, n + 1)
                    dve.wait_ge(b_done, n + 1)
                    v.tensor_tensor(hid[:, j % 2], sil[:, j % 2, :], psB[j % 2][:, :], ALU.mult).then_inc(h_done, 1)
                    dve.wait_ge(h_hi, n + 1)
                    v.tensor_tensor(hparts[:, j % 2, 1], hid[:, j % 2], hparts[:, j % 2, 0], ALU.subtract
                                    ).then_inc(h_lo, 1)
                    if j == 0 and not fresh:
                        residual(c - 1, c2 if u else c2 - 1, 1 - u)
                    if j == 3 and not last:
                        low_x(1 - u, c + 1)
                    if isinstance(c, int) and c < 2:
                        routing(n)
                    if isinstance(c, int) and 0 <= n - BEHIND * z.JS - 3 < BEHIND * TOPK:
                        i = n - BEHIND * z.JS - 3
                        combine(i // TOPK, i % TOPK, acc)

            def combine(c, k, base):
                if k == 0:
                    if c < BEHIND:
                        dve.wait_ge(acc_ld[c % 2], c // 2 * 16 + 16)
                    else:
                        dve.wait_ge(sh_done, c * CT + CT + 4)
                    dve.wait_ge(y_ld[c % GS], (c // GS + 1) * (16 * CT * TOPK))
                else:
                    dve.wait_ge(mid, c * CT + CT)
                for t in range(CT):
                    ins = v.scalar_tensor_tensor(base[:, c % 2, t, :], yg[:, c % GS, t, k, :],
                                                 g.gate[:, c * CT + t:c * CT + t + 1, k], base[:, c % 2, t, :],
                                                 ALU.mult, ALU.add)
                    if k == 0:
                        ins.then_inc(mid, 1)
                if k == 1:
                    ins.then_inc(summed, 1)

            low_x(0, 0)
            for i, (raw, parts) in enumerate(PIECES[:2]):
                dve.wait_ge(w_hi, i + 1)
                v.tensor_tensor(parts[:, 1], raw, parts[:, 0], ALU.subtract).then_inc(w_lo01, 1)
            chunks_before(dve, chunk)
            residual(BEHIND - 1, BEHIND // 2 - 1, 1)

            dve.sem_inc(rh_done, 2)
            dve.sem_inc(hT_ev, 1)
            dve.sem_inc(y_done, 2)
            for r in range(4):
                dve.sem_inc(y_st[r], 16)

            def step(q, r, has):
                i = q * 4 + r
                if has(1):
                    dve.wait_ge(th_done, i)
                    v.tensor_copy(hrT[:, (r - 1) % 2, :], rTh[:, 0:KR * P]).then_inc(hT_ev, 1)
                if has(0):
                    dve.wait_ge(rs_done, i + 1)
                    v.tensor_tensor(hr[:, r % 2, :], silr[:, r % 2, :], rUp[r % 2][:, RH:2 * RH], ALU.mult
                                    ).then_inc(rh_done, 1)
                if has(2):
                    s = (r - 2) % 4
                    dve.wait_ge(dn_done, i - 1)
                    dve.wait_ge(y_st[s], (q * 16 if r < 2 else q * 16 + 16))
                    v.tensor_copy(yr[:, s, :], rY[r % 2][:, 0:z.D]).then_inc(y_done, 1)

            steps(dve, step)
            chunks_behind(dve, chunk)
            for k in range(TOPK):
                combine(NC - 2, k, xr)
            residual(NC - 1, NC // 2 - 1, 1)
            for k in range(TOPK):
                combine(NC - 1, k, xr)

        @block.tensor
        def _(pe):
            pe.sem_inc(tx_done, 4)
            pe.sem_inc(rup_done, 2)

            def rank():
                pe.wait_ge(picked, 1)
                marks = both[:].rearrange("p t e -> p (t e)")
                pe.matmul(psR[:, 0:TE], g.before[:, :], marks, start=True, stop=True)
                pe.matmul(psC[:, 0:TE], g.ones[:, :], marks, start=True, stop=True).then_inc(ranked, 1)

            def up(c, u, j, first):
                n = c * z.JS + j
                pe.wait_ge(h_done, n + 1)
                for w, ps, sem in ((0, psA, a_done), (1, psB, b_done)):
                    if first and j == 0:
                        pe.wait_ge(w_lo01, w + 1)
                    if first and j == z.JS // 2:
                        pe.wait_ge(w_lo, w + 1)
                    i = 0
                    for wp, xp in ((0, 0), (0, 1), (1, 0)):
                        for k in range(KD):
                            ins = pe.matmul(ps[j % 2][:, :], sw12[:, wp, k, w, j * P:(j + 1) * P], xparts[:, u, xp, k, :],
                                            start=(i == 0), stop=(i == 3 * KD - 1))
                            i += 1
                    ins.then_inc(sem, 1)

            def down(c, j, first):
                n = c * z.JS + j
                if first and j % (z.JS // 2) == 0:
                    pe.wait_ge(w_lo, 3 + j // (z.JS // 2))
                pe.wait_ge(h_hi, n + 1)
                for t in range(CT):
                    if j == 0 and t % 2 == 0:
                        pe.wait_ge(sh_done, c * CT + t + 2)
                    for wp in range(2):
                        pe.matmul(psO[t], hparts[:, j % 2, 0, t * P:(t + 1) * P], sw3[:, wp, j, :],
                                  start=(j == 0 and wp == 0 and t % 2 == 0), stop=False, skip_group_check=True)
                pe.wait_ge(h_lo, n + 1)
                for t in range(CT):
                    ins = pe.matmul(psO[t], hparts[:, j % 2, 1, t * P:(t + 1) * P], sw3[:, 0, j, :],
                                    start=False, stop=(j == z.JS - 1), skip_group_check=True)
                    if j == z.JS - 1:
                        ins.then_inc(o_done, 1)

            def chunk(c, c2, u, fresh, last):
                pe.wait_ge(x_lo, c + 1)
                for j in range(z.JS):
                    up(c, u, j, fresh)
                    if j > 0:
                        down(c, j - 1, fresh)
                    elif not fresh:
                        down(c - 1, z.JS - 1, False)
                    if isinstance(c, int) and c == 0 and j == 5:
                        rank()

            chunks_before(pe, chunk)
            down(BEHIND - 1, z.JS - 1, False)
            pe.wait_ge(sh_done, BEHIND * CT + 4)
            pe.wait_ge(ew_in, 3 * 16 * E)
            w12 = ewf
            w3 = ew3[:].rearrange("p e k n -> p (e k n)")

            def turn_x(q, r):
                i = q * 4 + r
                pe.wait_ge(xs_ld[r], q * 16 + 16)
                pe.wait_ge(xT_ev, i + 1)
                for k in range(KD):
                    ins = pe.transpose(rTx[:, k * P:(k + 1) * P], xs[:, r, k * P:(k + 1) * P], g.ident[:, :])
                ins.then_inc(tx_done, 1)

            def expert(i):
                return pe.value_load(bexp_i[0:1, bass.ds(i, 1)], min_val=0, max_val=E - 1)

            def step(q, r, has):
                i = q * 4 + r
                if has(0):
                    e = expert(i)
                    pe.wait_ge(xT_ev, i + 2)
                    pe.wait_ge(rh_done, i + 1)
                    for k in range(KD):
                        ins = pe.matmul(rUp[r % 2][:, :], xsT[:, r % 2, k * P:(k + 1) * P],
                                        w12[:, bass.ds(e * (KD * 2 * RH) + k * 2 * RH, 2 * RH)],
                                        start=(k == 0), stop=(k == KD - 1))
                    ins.then_inc(rup_done, 1)
                if has(1):
                    pe.wait_ge(rh_done, i + 2)
                    pe.wait_ge(hT_ev, i)
                    for k in range(KR):
                        ins = pe.transpose(rTh[:, k * P:(k + 1) * P], hr[:, (r - 1) % 2, k * P:(k + 1) * P],
                                           g.ident[:, :])
                    ins.then_inc(th_done, 1)
                if has(-1):
                    if r == 3:
                        turn_x(q + 1, 0)
                    else:
                        turn_x(q, r + 1)
                if has(2):
                    e = expert(i - 2)
                    pe.wait_ge(hT_ev, i)
                    pe.wait_ge(y_done, i - 1)
                    for k in range(KR):
                        ins = pe.matmul(rY[r % 2][:, 0:z.D], hrT[:, r % 2, k * P:(k + 1) * P],
                                        w3[:, bass.ds(e * (KR * z.D) + k * z.D, z.D)],
                                        start=(k == 0), stop=(k == KR - 1))
                    ins.then_inc(dn_done, 1)

            turn_x(0, 0)
            steps(pe, step)
            pe.wait_ge(rh_done, NB + 2)
            pe.wait_ge(xT_ev, NB + 1)
            pe.wait_ge(hT_ev, NB + 1)
            pe.wait_ge(y_done, NB + 2)
            chunks_behind(pe, chunk)
            down(NC - 1, z.JS - 1, False)


class Names:
    pass


def residents(nc, z, ctx):
    m = Mem(nc, ctx)
    g = Names()
    g.held = m.sem("held")
    g.filled = m.sem("filled")
    g.zero = m.sb("zero", [P, z.D])
    g.rw = m.sb("rw", [P, z.KD, z.E])
    g.bias = m.sb("bias", [P, z.E])
    g.ident = m.sb("ident", [P, P])
    g.before = m.sb("before", [P, P], BF16)
    g.ones = m.sb("ones", [P, P], BF16)
    g.mhalf = m.sb("mhalf", [P, CT])
    g.eps = m.sb("eps", [P, CT])
    g.rev_i = m.sb("rev_i", [P, z.E], I32)
    g.rev = m.sb("rev", [P, z.E])
    g.blk_i = m.sb("blk_i", [P, z.NB], I32)
    g.blk = m.sb("blk", [P, z.NB])
    g.keep = m.sb("keep", [P, z.E, z.NT])
    g.logits = m.sb("logits", [P, z.NT * z.E])
    g.slot = m.sb("slot", [P, z.NT * TOPK], U32)
    g.gate = m.sb("gate", [P, z.NT, TOPK])
    return g


def scratch(nc, z):
    d = Names()
    d.xn = nc.dram_tensor("xn_rows", [z.T, z.D], F32).ap()
    d.xnT = nc.dram_tensor("xn_turned", [P, z.KD, z.T], F32).ap()
    d.x1 = nc.dram_tensor("x1_rows", [z.T, z.D], F32).ap()
    d.x2 = nc.dram_tensor("x2_rows", [z.T, z.D], F32).ap()
    d.sh = nc.dram_tensor("x_plus_shared", [z.T, z.D], F32).ap()
    d.xs = nc.dram_tensor("rows_by_slot", [z.NB * P, z.D], F32).ap()
    d.ys = nc.dram_tensor("outputs_by_slot", [z.NB * P, z.D], F32).ap()
    return d


def attention(nc, z, g, dram):
    KD, E, D = z.KD, z.E, z.D
    H, DK = 16, 16
    HG = 4
    NG = H // HG
    MASK = -65536.0
    SL = 64
    NB_ = z.B
    UNITS1 = [(0, 0, 4), (1, 0, 2), (1, 2, 2)] + [(t, h, 1) for t in (2, 3) for h in range(HG)]
    UNITS2 = [(t, h, 1) for t in (0, 1) for h in range(HG)] + [(2, 0, 2), (2, 2, 2), (3, 0, 4)]
    UN = len(UNITS1)
    UG = CT * HG
    LAG = 2
    LAST_UNIT = [3, 7, 9, 10]
    STEPS = UN + LAG
    QSCALE = float(DK) ** -0.5
    with ExitStack() as ctx:
        m = Mem(nc, ctx, "at_")
        wraw = m.sb("wraw", [P, KD, 3 * D])
        wqkv = m.sb("wqkv", [P, 2, KD, 3 * D], F32R)
        wo = m.sb("wo", [P, KD, D])
        identb = m.sb("identb", [P, P], BF16)
        maskq = m.sb("maskq", [P, P], BF16)
        x1 = m.sb("x1", [P, 2, CT, D])
        xn = m.sb("xn", [P, CT, D])
        xnT = m.sb("xnT", [P, 2, KD, CHUNK], F32R)
        qk = m.sb("qk", [P, 2, NG, CT, HG * DK])
        va = m.sb("va", [P, 2, CT, H, 32])
        q4 = m.sb("q4", [P, 2, CT, HG, SL], F32R)
        k4 = m.sb("k4", [P, 2, CT, HG, SL], F32R)
        identr = m.sb("identr", [P, P], F32R)
        qT = m.sb("qT", [P, 2, HG, CHUNK], F32R)
        kT = m.sb("kT", [P, NG, HG // 2, CHUNK], F32R)
        q2T = m.sb("q2T", [P, 2, HG, CHUNK], F32R)
        pT = m.sb("pT", [P, 8, CHUNK])
        oT = m.sb("oT", [P, CHUNK])
        rec = m.sb("rec", [P, CT, HG])
        attn = m.sb("attn", [P, CT, D])
        attnT = m.sb("attnT", [P, KD, CHUNK])
        xres = m.sb("xres", [P, CT, D])
        xn2 = m.sb("xn2", [P, CT, D])
        xnT2 = m.sb("xnT2", [P, KD, CHUNK])
        stat = m.sb("stat", [P, 2, CT, 6])
        mv = m.sb("mv", [P, 2, CT, 2])
        veps = m.sb("veps", [P, 2, CT])
        rstd = m.sb("rstd", [P, 2, CT])
        ps1 = [m.ps(f"ps1_{i}", [P, 512]) for i in range(2)]
        ps2 = [m.ps(f"ps2_{i}", [P, 512]) for i in range(2)]
        psO = m.ps("psO", [P, 512])
        psG = m.ps("psG", [P, 2, 512])
        psM = m.ps("psM", [P, 512])

        w_in = m.sem("w_in")
        made = m.sem("made")
        w_hi = m.sem("w_hi")
        w_lo = m.sem("w_lo")
        x_hi = m.sem("x_hi")
        identr_in = m.sem("identr_in")
        consts = m.sem("consts")
        filled = m.sem("filled")
        x1_ld = m.sems("x1_ld", 2)
        st = m.sem("st")
        var1 = m.sem("var1")
        eps1 = m.sem("eps1")
        rs1 = m.sem("rs1")
        normed1 = m.sem("normed1")
        g_full = m.sem("g_full")
        g_free = m.sem("g_free")
        hi_done = m.sem("hi_done")
        lo_done = m.sem("lo_done")
        s1_done = m.sem("s1_done")
        mx_done = m.sem("mx_done")
        s2_done = m.sem("s2_done")
        ex_done = m.sem("ex_done")
        cut_done = m.sem("cut_done")
        pv_done = m.sem("pv_done")
        o_ev = m.sem("o_ev")
        rc = m.sem("rc")
        m_full = m.sem("m_full")
        m_free = m.sem("m_free")
        xr_ld = m.sem("xr_ld")
        var2 = m.sem("var2")
        eps2 = m.sem("eps2")
        rs2 = m.sem("rs2")
        normed2 = m.sem("normed2")
        x2_st = m.sem("x2_st")
        xn2_st = m.sem("xn2_st")
        xnT2_st = m.sem("xnT2_st")
        block = ctx.enter_context(nc.Block())

        def g_uses(c, gr):
            has_last, has_next = c != 0, c != NB_ - 1
            names = []
            if gr == 0 and has_last:
                names.append("attnT")
            if gr == 1 and has_next:
                names += [f"proj{t}" for t in range(CT)]
            if gr == 2 and has_last:
                names.append("x2T")
            if gr < 2 or has_next:
                names += [f"TQ_{gr}", f"TK_{gr}"]
            if gr == 0 and has_next:
                names.append("xnT")
            if gr < NG - 1 or has_next:
                names.append(f"T2_{gr}")
            return names

        def g_batch(c):
            return sum((g_uses(c, gr) for gr in range(NG)), [])

        FIRST_G = ["xnT"] + [f"proj{t}" for t in range(CT)] + ["TQ_0", "TK_0", "TQ_1", "TK_1", "T2"]
        PER_G = len(g_batch(1))

        def g_base(c, kind):
            if kind == 0:
                return len(FIRST_G)
            return c * PER_G + (len(FIRST_G) + len(g_batch(0)) - PER_G)

        def g_before(c, kind, gr):
            return g_base(c, kind) + sum(len(g_uses(kind, i)) for i in range(gr))

        def gu(c, kind, name):
            if kind == "first":
                return FIRST_G.index(name)
            if kind == "end":
                return g_base(NB_ - 1, NB_ - 1) + len(g_batch(NB_ - 1)) + ["attnT", "x2T"].index(name)
            return g_base(c, kind) + g_batch(kind).index(name)

        M_FIRST = ["OT_0", "OT_1", "OT_2"]
        M_USES = ["OT_3"] + [f"out{t}" for t in range(CT)] + ["OT_0", "OT_1", "rt", "OT_2"]
        M_END = ["OT_3"] + [f"out{t}" for t in range(CT)] + ["rt"]

        def mu(c, kind, name):
            if kind == 0:
                return M_FIRST.index(name)
            return c * len(M_USES) + (len(M_FIRST) - len(M_USES) + M_USES.index(name))

        def mu_end(name):
            return len(M_FIRST) + len(M_USES) * (NB_ - 1) + M_END.index(name)


        VALUES_AT = {LAG + 6: 0, LAG + 10: 1}
        VALUES_LATE = {0: 2, 1: 3}
        AT = dict(attnT=7, x2T=3, xnT=11, T2=STEPS - 1)
        OUT_AT = [9, 10, 11, 12]
        PROJECT_AT = [2, 3, 5, 6]

        def turns(gr, n):
            q, k = {0: (7, 9), 1: (8, 10)}.get(gr, (6, 9))
            return "TQ" if n == q else "TK" if n == k else None

        def phases(eng, first, phase, last):
            first()
            for u in range(2):
                for gr in range(NG):
                    phase(u, 0, u, u, gr)
            with eng.Fori(1, NB_ // 2 - 1) as c2:
                for u in range(2):
                    for gr in range(NG):
                        phase(c2 * 2 + u, c2, u, 2, gr)
            for u in range(2):
                for gr in range(NG):
                    phase(NB_ - 2 + u, NB_ // 2 - 1, u, 2 if u == 0 else NB_ - 1, gr)
            last()

        def rows(ap, c):
            return ap[bass.ds(c * CHUNK, CHUNK), :].rearrange("(t p) d -> p t d", p=P)

        @block.sync
        def _(sp):
            def hold(sem, value):
                sp.wait_ge(sem, value)
                sp.sem_inc(g.held, 1)

            def load_x1(c, c2, u, first):
                if not first:
                    hold(normed1, c - 1)
                sp.dma_start(x1[:, u], rows(dram.x1, c)).then_inc(x1_ld[u], 16)

            def load_res(c, c2, u, first):
                if not first:
                    hold(x2_st, c * 16)
                    hold(normed2, c)
                sp.dma_start(xres[:], rows(dram.x1, c)).then_inc(xr_ld, 16)

            def store_x2(c):
                hold(var2, c + 1)
                sp.dma_start(rows(dram.x2, c), xres[:]).then_inc(x2_st, 16)
                hold(normed2, c + 1)
                sp.dma_start(rows(dram.xn, c), xn2[:]).then_inc(xn2_st, 16)

            def store_x2T(c, done):
                hold(g_free, done)
                sp.dma_start(dram.xnT[:, :, bass.ds(c * CHUNK, CHUNK)], xnT2[:]).then_inc(xnT2_st, 16)

            def first():
                load_x1(0, 0, 0, True)
                for i, w in enumerate((dram.W_q, dram.W_k, dram.W_v)):
                    sp.dma_start(wraw[:, :, i * D:(i + 1) * D], w.rearrange("(k p) n -> p k n", p=P)).then_inc(w_in, 16)
                sp.dma_start(wo[:], dram.W_o.rearrange("(k p) n -> p k n", p=P)).then_inc(w_in, 16)
                load_x1(1, 0, 1, True)
                load_res(0, 0, 0, True)

            def phase(c, c2, u, kind, gr):
                if gr == 1 and kind != 0:
                    store_x2(c - 1)
                    load_res(c, c2, u, False)
                if gr == 2 and kind != 0:
                    store_x2T(c - 1, gu(c, kind, "x2T") + 2)
                if gr == 2 and (kind in (0, 1) or (kind == 2 and not isinstance(c, int))):
                    load_x1(c + 2, c2 + 1, u, False)

            def last():
                store_x2(NB_ - 1)
                store_x2T(NB_ - 1, gu(0, "end", "x2T") + 2)
                sp.wait_ge(x2_st, 16 * NB_)
                sp.wait_ge(xn2_st, 16 * NB_ + 16)
                sp.wait_ge(xnT2_st, 16 * NB_ + 16)

            phases(sp, first, phase, last)

        @block.gpsimd
        def _(pool):
            p = nc.gpsimd

            def cut(G, ki):
                pool.wait_ge(ex_done, G * UN + (LAST_UNIT[ki] + 3))
                pool.sem_inc(g.held, 1)
                s = ki % 2 * HG
                p.affine_select(out=pT[:, s:s + HG, 0:P], in_=pT[:, s:s + HG, 0:P], compare_op=ALU.is_ge, fill=0.0,
                                base=0, pattern=[[0, HG], [1, P]], channel_multiplier=-1).then_inc(cut_done, 1)

            def deviation(i, c, var, eps, rs):
                pool.wait_ge(var, c + 1)
                p.tensor_tensor(veps[:, i, :], mv[:, i, :, 1], g.eps[:, 0:CT], ALU.add).then_inc(eps, 1)
                pool.wait_ge(eps, c + 1)
                p.tensor_tensor(rstd[:, i, :], veps[:, i, :], g.mhalf[:, 0:CT], ALU.pow).then_inc(rs, 1)

            def low(G, gr):
                pool.wait_ge(hi_done, G + 1)
                pool.sem_inc(g.held, 1)
                s = gr % 2
                q, k = (qk[:, i, gr].rearrange("p t (h d) -> p t h d", d=DK) for i in range(2))
                p.tensor_tensor(q4[:, s, :, :, 2 * DK:3 * DK], q, q4[:, s, :, :, 0:DK], ALU.subtract)
                p.tensor_tensor(k4[:, s, :, :, DK:2 * DK], k, k4[:, s, :, :, 0:DK], ALU.subtract
                                ).then_inc(lo_done, 1)

            n = [0]

            def done(ins):
                n[0] += 1
                ins.then_inc(made, 1)
                pool.wait_ge(made, n[0])

            def constants():
                done(p.memset(identb[:], 0.0))
                done(p.affine_select(out=identb[:], in_=identb[:], compare_op=ALU.not_equal, fill=1.0,
                                     base=0, pattern=[[-1, P]], channel_multiplier=1))
                done(p.memset(maskq[:], 0.0))
                done(p.affine_select(out=maskq[:], in_=maskq[:], compare_op=ALU.is_ge, fill=MASK,
                                     base=0, pattern=[[-1, P]], channel_multiplier=1))

            def zeros():
                done(p.memset(qT[:].bitcast(F32), 0.0))
                done(p.memset(q2T[:].bitcast(F32), 0.0))
                pool.sem_inc(consts, 1)

            def first():
                constants()
                deviation(0, 0, var1, eps1, rs1)
                zeros()
                low(0, 0)
                low(1, 1)

            def phase(c, c2, u, kind, gr):
                G = c * NG + gr
                for n in range(STEPS):
                    if n - LAG in LAST_UNIT:
                        cut(G, LAST_UNIT.index(n - LAG))
                    if n == 1 and (gr < 2 or kind != NB_ - 1):
                        low(G + 2, (gr + 2) % NG)
                    if n == 7 and gr == 0 and kind != NB_ - 1:
                        deviation(0, c + 1, var1, eps1, rs1)
                    if n == 2 and gr == 1 and kind != 0:
                        deviation(1, c - 1, var2, eps2, rs2)

            def last():
                deviation(1, NB_ - 1, var2, eps2, rs2)

            phases(pool, first, phase, last)

        @block.scalar
        def _(act):
            act.sem_inc(g_free, 1)
            act.sem_inc(ex_done, 2)
            act.sem_inc(xnT2_st, 16)
            s_ = nc.scalar
            s_.copy(identr[:], g.ident[:]).then_inc(identr_in, 1)

            def out_of_g(i, dst, src=psG):
                act.wait_ge(g_full, i + 1)
                s_.copy(dst, src[:]).then_inc(g_free, 1)

            def queries_out_of_g(i, dst, n):
                act.wait_ge(g_full, i + 1)
                for half in range(2):
                    a = half * SL
                    ins = s_.copy(dst.rearrange("p (k h) n -> p k h n", h=2)[a:a + n, :, half, :], psG[a:a + n])
                ins.then_inc(g_free, 1)

            def project(i0, t, u, lo):
                if t == 0 and lo is not None:
                    act.wait_ge(lo_done, lo)
                    act.sem_inc(g.held, 1)
                act.wait_ge(g_full, i0 + (t + 1))
                q, k = (psG[:, 0, i * D:(i + 1) * D].rearrange("p (g n) -> p g n", g=NG) for i in range(2))
                s_.mul(qk[:, 0, :, t, :], q, QSCALE)
                s_.copy(qk[:, 1, :, t, :], k)
                s_.copy(va[:, u, t, :, 0:DK], psG[:, 1, 0:D].rearrange("p (h d) -> p h d", d=DK)
                        ).then_inc(g_free, 1)

            def high(G, gr, waited):
                act.wait_ge(g_free, waited)
                s = gr % 2
                for part, i, step in ((q4, 0, 1), (k4, 1, 2)):
                    dst = (part[:, s].rearrange("p t h (s d) -> p (t h) s d", d=DK))[:, :, 0:1 + step:step, :]
                    src = qk[:, i, gr].rearrange("p t (h o d) -> p (t h) o d", o=1, d=DK)
                    ins = s_.copy(dst, src.to_broadcast([P, UG, 2, DK]))
                ins.then_inc(hi_done, 1)

            def high_x(i):
                act.wait_ge(g_full, i + 1)
                s_.copy(xnT[:, 0], psG[:]).then_inc(x_hi, 1)

            def first():
                act.wait_ge(w_in, 64)
                s_.copy(wqkv[:, 0], wraw[:]).then_inc(w_hi, 1)
                high_x(gu(0, "first", "xnT"))
                act.wait_ge(filled, 5)
                act.sem_inc(g.held, 1)
                for t in range(CT):
                    project(gu(0, "first", "proj0"), t, 0, None)
                high(0, 0, gu(0, "first", f"proj{CT - 1}") + 2)
                high(1, 1, gu(0, "first", f"proj{CT - 1}") + 2)
                act.wait_ge(consts, 1)
                act.sem_inc(g.held, 1)
                for k in range(2):
                    queries_out_of_g(gu(0, "first", f"TQ_{k}"), qT[:, k], 3 * DK)
                queries_out_of_g(gu(0, "first", "T2"), q2T[:, 0], SL)

            def phase(c, c2, u, kind, gr):
                G = c * NG + gr
                more = gr < 2 or kind != NB_ - 1
                for n in range(STEPS):
                    if n == 0 and more:
                        high(G + 2, (gr + 2) % NG, g_before(c, kind, gr) + 1)
                    if n >= LAG:
                        k = n - LAG
                        ki, h, heads = UNITS2[k]
                        act.wait_ge(s2_done, G * UN + (k + 1))
                        act.wait_ge(pv_done, G * CT + (ki + 1))
                        w = CHUNK - ki * P
                        s = (ki * HG + h) % 8
                        s_.activation(pT[:, s:s + heads, 0:w], ps2[(gr + k) % 2][:, 0:heads * w]
                                      .rearrange("p (h w) -> p h w", h=heads), ACT.Exp).then_inc(ex_done, 1)
                    if gr == 0 and n == AT["attnT"] and kind != 0:
                        out_of_g(gu(c, kind, "attnT"), attnT[:])
                    if gr == 2 and n == AT["x2T"] and kind != 0:
                        turned2(c - 1, gu(c, kind, "x2T"))
                    if gr == 1 and n in PROJECT_AT and kind != NB_ - 1:
                        project(gu(c, kind, "proj0"), PROJECT_AT.index(n), 1 - u, c * NG + 4)
                    if turns(gr, n) == "TQ" and more:
                        queries_out_of_g(gu(c, kind, f"TQ_{gr}"), qT[:, gr % 2], 3 * DK)
                    if gr == 0 and n == AT["xnT"] and kind != NB_ - 1:
                        high_x(gu(c, kind, "xnT"))
                    if n == AT["T2"] and not (kind == NB_ - 1 and gr == NG - 1):
                        queries_out_of_g(gu(c, kind, f"T2_{gr}"), q2T[:, (gr + 1) % 2], SL)

            def turned2(c, i):
                act.wait_ge(xnT2_st, c * 16 + 16)
                out_of_g(i, xnT2[:])

            def last():
                out_of_g(gu(0, "end", "attnT"), attnT[:])
                turned2(NB_ - 1, gu(0, "end", "x2T"))

            phases(act, first, phase, last)

        @block.vector
        def _(dve):
            dve.sem_inc(mx_done, 2)
            dve.sem_inc(o_ev, 1)
            dve.sem_inc(m_free, 1)
            dve.sem_inc(xn2_st, 16)
            v = nc.vector
            v.memset(va[:], 0.0).then_inc(filled, 1)
            v.memset(q4[:].bitcast(F32), 0.0).then_inc(filled, 1)
            v.memset(k4[:].bitcast(F32), 0.0).then_inc(filled, 1)
            dve.wait_ge(filled, 3)
            v.memset(va[:, :, :, :, DK], 1.0).then_inc(filled, 1)
            v.memset(k4[:, :, :, :, 3 * DK].bitcast(F32), 1.0).then_inc(filled, 1)

            def keys_out_of_g(i, gr):
                dve.wait_ge(g_full, i + 1)
                v.tensor_copy(kT[:, gr], psG[:]).then_inc(g_free, 1)

            def low_x(c):
                dve.wait_ge(x_hi, c + 1)
                v.tensor_tensor(xnT[:, 1], psG[:], xnT[:, 0], ALU.subtract).then_inc(g_free, 1)

            def moments(i, src, wait, count, var):
                if wait is not None:
                    dve.wait_ge(*wait)
                for t in range(CT):
                    v.bn_stats(stat[:, i, t, :], src[:, t, :]).then_inc(st, 1)
                dve.wait_ge(st, count + CT)
                dve.sem_inc(g.held, 1)
                for t in range(CT):
                    ins = v.bn_aggr(mv[:, i, t, :], stat[:, i, t, :])
                ins.then_inc(var, 1)

            def normalize(i, dst, src, wait, done):
                dve.wait_ge(*wait)
                for t in range(CT):
                    ins = v.tensor_scalar(dst[:, t, :], src[:, t, :], mv[:, i, t, 0:1], rstd[:, i, t:t + 1],
                                          ALU.subtract, ALU.mult)
                ins.then_inc(done, 1)

            def maxima(G, gr, n):
                qi, h, heads = UNITS1[n]
                dve.wait_ge(s1_done, G * UN + (n + 1))
                w = (qi + 1) * P
                v.tensor_reduce(q4[:, gr % 2, qi, h:h + heads, 3 * DK:3 * DK + 1],
                                ps1[(gr + n) % 2][:, 0:heads * w].rearrange("p (h w) -> p h w", h=heads), AX.X,
                                ALU.max, negate=True).then_inc(mx_done, 1)

            def copy_o(G):
                dve.wait_ge(pv_done, G * CT + (CT + 2))
                v.tensor_copy(oT[:], psO[:]).then_inc(o_ev, 1)

            def divide(G, gr, i):
                dve.wait_ge(m_full, i + 1)
                o = psM[:].rearrange("p (t h w) -> p t h w", t=CT, h=HG)
                v.reciprocal(rec[:], o[:, :, :, DK]).then_inc(rc, 1)
                dve.wait_ge(rc, G + 1)
                for t in range(CT):
                    ins = v.tensor_tensor(attn[:, t, gr * HG * DK:(gr + 1) * HG * DK].rearrange("p (h d) -> p h d", d=DK),
                                          o[:, t, :, 0:DK],
                                          rec[:, t, :].rearrange("p (h o) -> p h o", o=1).to_broadcast([P, HG, DK]),
                                          ALU.mult)
                ins.then_inc(m_free, 1)

            def residual(c, t, i0):
                if t == 0:
                    dve.wait_ge(xr_ld, c * 16 + 16)
                dve.wait_ge(m_full, i0 + (t + 1))
                v.tensor_tensor(xres[:, t, :], xres[:, t, :], psM[:, 0:D], ALU.add).then_inc(m_free, 1)

            def logits(c, i):
                dve.wait_ge(m_full, i + 1)
                v.tensor_copy(g.logits[:, bass.ds(c * (CT * E), CT * E)], psM[:, 0:CT * E]).then_inc(m_free, 1)

            def first():
                moments(0, x1[:, 0], (x1_ld[0], 16), 0, var1)
                dve.wait_ge(w_hi, 1)
                v.tensor_tensor(wqkv[:, 1], wraw[:], wqkv[:, 0], ALU.subtract).then_inc(w_lo, 1)
                normalize(0, xn, x1[:, 0], (rs1, 1), normed1)
                low_x(0)
                for k in range(2):
                    keys_out_of_g(gu(0, "first", f"TK_{k}"), k)
                for n in range(UN):
                    maxima(0, 0, n)

            def phase(c, c2, u, kind, gr):
                G = c * NG + gr
                nxt = not (kind == NB_ - 1 and gr == NG - 1)
                before = CT if kind == 0 else c * (2 * CT)
                for n in range(STEPS):
                    if nxt and n < UN:
                        maxima(G + 1, (gr + 1) % NG, n)
                    if n == 2 and not (kind == 0 and gr == 0):
                        copy_o(G - 1)
                    if n == 5 and not (kind == 0 and gr == 0):
                        divide(G - 1, (gr - 1) % NG, mu(c, kind, f"OT_{(gr - 1) % NG}"))
                    if turns(gr, n) == "TK" and (gr < 2 or kind != NB_ - 1):
                        keys_out_of_g(gu(c, kind, f"TK_{gr}"), (gr + 2) % NG)
                    if gr == 0 and kind != NB_ - 1:
                        un, c2n = 1 - u, (c2 if u == 0 else c2 + 1)
                        if n == 6:
                            moments(0, x1[:, un], (x1_ld[un], c2n * 16 + 16), before, var1)
                        if n == 8:
                            normalize(0, xn, x1[:, un], (rs1, c + 2), normed1)
                    if gr == 0 and n in OUT_AT and kind != 0:
                        residual(c - 1, OUT_AT.index(n), mu(c, kind, "out0"))
                    if gr == 0 and n == AT["xnT"] and kind != NB_ - 1:
                        low_x(c + 1)
                    if gr == 1 and n == 0 and kind != 0:
                        moments(1, xres, (m_free, mu(c, kind, f"out{CT - 1}") + 2),
                                before + (0 if kind == NB_ - 1 else CT), var2)
                    if gr == 1 and n == 2 and kind != 0:
                        dve.wait_ge(xn2_st, c * 16)
                        dve.sem_inc(g.held, 1)
                        normalize(1, xn2, xres, (rs2, c), normed2)
                    if gr == 2 and n == 7 and kind != 0:
                        logits(c - 1, mu(c, kind, "rt"))

            def last():
                c = NB_
                copy_o(NB_ * NG - 1)
                divide(NB_ * NG - 1, NG - 1, mu_end("OT_3"))
                for t in range(CT):
                    residual(c - 1, t, mu_end("out0"))
                moments(1, xres, (m_free, mu_end(f"out{CT - 1}") + 2), (2 * NB_ - 1) * CT, var2)
                dve.wait_ge(xn2_st, c * 16)
                normalize(1, xn2, xres, (rs2, c), normed2)
                logits(c - 1, mu_end("rt"))

            phases(dve, first, phase, last)

        @block.tensor
        def _(pe):
            pe.sem_inc(pv_done, 2)
            pe.wait_ge(w_in, 64)
            pe.wait_ge(identr_in, 1)

            def turn(i, src, ident=g.ident, out=psG):
                pe.wait_ge(g_free, i + 1)
                for t in range(CT):
                    for k in range(2):
                        ins = pe.transpose(out[:, k, t * P:(t + 1) * P], src(t, k), ident[:, :])
                ins.then_inc(g_full, 1)

            def turn_parts(i, parts):
                turn(i, lambda t, k: parts[:, t, 2 * k:2 * k + 2, :].rearrange("p h s -> p (h s)"),
                     identr, psG[:].bitcast(F32R))

            def project(i0, t):
                pe.wait_ge(g_free, i0 + (t + 1))
                for half, lo, w in ((0, 0, 2 * D), (1, 2 * D, D)):
                    n = 0
                    for xp, wp in ((0, 0), (0, 1), (1, 0)):
                        for k in range(KD):
                            ins = pe.matmul(psG[:, half, 0:w], xnT[:, xp, k, t * P:(t + 1) * P],
                                            wqkv[:, wp, k, lo:lo + w], start=(n == 0), stop=(n == 3 * KD - 1))
                            n += 1
                ins.then_inc(g_full, 1)

            def score1(G, gr, n, ready):
                qi, h0, heads = UNITS1[n]
                if n == 0:
                    pe.wait_ge(g_free, ready)
                pe.wait_ge(mx_done, G * UN + (n + 1))
                w = (qi + 1) * P
                ps = ps1[(gr + n) % 2]
                for i in range(heads):
                    h = h0 + i
                    pe.matmul(ps[:, i * w:(i + 1) * w], qT[:, gr % 2, h, qi * P:w], kT[:, gr, h // 2, 0:w],
                              start=True, stop=False)
                    ins = pe.matmul(ps[:, i * w + qi * P:(i + 1) * w], identb[:, :], maskq[:, :],
                                    start=False, stop=True)
                ins.then_inc(s1_done, 1)

            def score2(G, gr, n):
                ki, h0, heads = UNITS2[n]
                pe.wait_ge(ex_done, G * UN + (n + 1))
                w = CHUNK - ki * P
                ps = ps2[(gr + n) % 2]
                some = min(heads, 2)
                for i in range(0, heads, some):
                    h = h0 + i
                    ins = pe.matmul(ps[:, i * w:(i + some) * w], kT[:, gr, h // 2, ki * P:(ki + 1) * P],
                                    q2T[:, gr % 2, h:h + some, ki * P:CHUNK], start=True, stop=True)
                ins.then_inc(s2_done, 1)

            def values(G, gr, u, ki):
                if ki == 0:
                    pe.wait_ge(o_ev, G + 1)
                pe.wait_ge(cut_done, G * CT + (ki + 1))
                w = CHUNK - ki * P
                for h in range(HG):
                    ins = pe.matmul(psO[32 * h:32 * h + 32, ki * P:CHUNK], va[:, u, ki, gr * HG + h, :],
                                    pT[:, (ki * HG + h) % 8, 0:w], start=(ki == 0), stop=(ki == CT - 1),
                                    skip_group_check=True)
                ins.then_inc(pv_done, 1)

            def turn_o(G, i):
                pe.wait_ge(o_ev, G + 2)
                pe.wait_ge(m_free, i + 1)
                for t in range(CT):
                    ins = pe.transpose(psM[:, t * P:(t + 1) * P], oT[:, t * P:(t + 1) * P], g.ident[:, :])
                ins.then_inc(m_full, 1)

            def turn_attn(i, mi):
                pe.wait_ge(m_free, mi + 2)
                turn(i, lambda t, k: attn[:, t, k * P:(k + 1) * P])

            def project_out(t, i0, ready):
                if t == 0:
                    pe.wait_ge(g_free, ready)
                pe.wait_ge(m_free, i0 + (t + 1))
                for k in range(KD):
                    ins = pe.matmul(psM[:, 0:D], attnT[:, k, t * P:(t + 1) * P], wo[:, k, :],
                                    start=(k == 0), stop=(k == KD - 1))
                ins.then_inc(m_full, 1)

            def route(i, ready):
                pe.wait_ge(g_free, ready)
                pe.wait_ge(m_free, i + 1)
                for t in range(CT):
                    for k in range(KD):
                        ins = pe.matmul(psM[:, t * E:(t + 1) * E], xnT2[:, k, t * P:(t + 1) * P], g.rw[:, k, :],
                                        start=(k == 0), stop=(k == KD - 1))
                ins.then_inc(m_full, 1)

            def first():
                pe.wait_ge(normed1, 1)
                turn(gu(0, "first", "xnT"), lambda t, k: xn[:, t, k * P:(k + 1) * P])
                pe.wait_ge(w_lo, 1)
                for t in range(CT):
                    project(gu(0, "first", "proj0"), t)
                for k in range(2):
                    pe.wait_ge(lo_done, k + 1)
                    turn_parts(gu(0, "first", f"TQ_{k}"), q4[:, k])
                    turn_parts(gu(0, "first", f"TK_{k}"), k4[:, k])
                pe.wait_ge(consts, 1)
                pe.sem_inc(g.held, 1)
                for n in range(UN):
                    score1(0, 0, n, gu(0, "first", "TK_0") + 2)
                pe.wait_ge(mx_done, UN + 2)
                turn_parts(gu(0, "first", "T2"), q4[:, 0])

            def phase(c, c2, u, kind, gr):
                G = c * NG + gr
                more = gr < 2 or kind != NB_ - 1
                nxt = not (kind == NB_ - 1 and gr == NG - 1)
                started = not (kind == 0 and gr == 0)
                for n in range(STEPS):
                    if nxt and n < UN:
                        score1(G + 1, (gr + 1) % NG, n, g_before(c, kind, gr))
                    if n in VALUES_LATE and started:
                        values(G - 1, (gr - 1) % NG, u if gr else 1 - u, VALUES_LATE[n])
                    if n == LAG:
                        pe.wait_ge(g_free, g_before(c, kind, gr) + 1)
                    if n >= LAG:
                        score2(G, gr, n - LAG)
                    if n == 4 and started:
                        turn_o(G - 1, mu(c, kind, f"OT_{(gr - 1) % NG}"))
                    if n in VALUES_AT:
                        values(G, gr, u, VALUES_AT[n])
                    if gr == 0 and n == AT["attnT"] and kind != 0:
                        turn_attn(gu(c, kind, "attnT"), mu(c, kind, "OT_3"))
                    if gr == 2 and n == AT["x2T"] and kind != 0:
                        pe.wait_ge(normed2, c)
                        turn(gu(c, kind, "x2T"), lambda t, k: xn2[:, t, k * P:(k + 1) * P])
                    if gr == 1 and n in PROJECT_AT and kind != NB_ - 1:
                        project(gu(c, kind, "proj0"), PROJECT_AT.index(n))
                    if gr == 2 and n == 6 and kind != 0:
                        route(mu(c, kind, "rt"), gu(c, kind, "x2T") + 2)
                    if turns(gr, n) == "TQ" and more:
                        pe.wait_ge(lo_done, G + 3)
                        turn_parts(gu(c, kind, f"TQ_{gr}"), q4[:, gr % 2])
                    if turns(gr, n) == "TK" and more:
                        turn_parts(gu(c, kind, f"TK_{gr}"), k4[:, gr % 2])
                    if gr == 0 and n in OUT_AT and kind != 0:
                        project_out(OUT_AT.index(n), mu(c, kind, "out0"), gu(c, kind, "attnT") + 2)
                    if gr == 0 and n == AT["xnT"] and kind != NB_ - 1:
                        pe.wait_ge(normed1, c + 2)
                        turn(gu(c, kind, "xnT"), lambda t, k: xn[:, t, k * P:(k + 1) * P])
                    if n == AT["T2"] and nxt:
                        pe.wait_ge(mx_done, G * UN + (2 * UN + 2))
                        turn_parts(gu(c, kind, f"T2_{gr}"), q4[:, (gr + 1) % 2])

            def last():
                for ki in (2, 3):
                    values(NB_ * NG - 1, NG - 1, 1, ki)
                turn_o(NB_ * NG - 1, mu_end("OT_3"))
                turn_attn(gu(0, "end", "attnT"), mu_end("OT_3"))
                for t in range(CT):
                    project_out(t, mu_end("out0"), gu(0, "end", "attnT") + 2)
                pe.wait_ge(normed2, NB_)
                turn(gu(0, "end", "x2T"), lambda t, k: xn2[:, t, k * P:(k + 1) * P])
                route(mu_end("rt"), gu(0, "end", "x2T") + 2)

            phases(pe, first, phase, last)


def macaron_kernel(nc, x, W_q, W_k, W_v, W_o, router_w, expert_bias, shared_w1, shared_w2, shared_w3,
                   routed_w1, routed_w2, routed_w3, out):
    assert shared_w1.shape[0] == 1
    z = Shapes(x, router_w, shared_w1[0], routed_w1)
    dram = scratch(nc, z)
    dram.router_w, dram.expert_bias = router_w, expert_bias
    dram.shared_w1, dram.shared_w2, dram.shared_w3 = shared_w1[0], shared_w2[0], shared_w3[0]
    dram.routed_w1, dram.routed_w2, dram.routed_w3 = routed_w1, routed_w2, routed_w3
    dram.W_q, dram.W_k, dram.W_v, dram.W_o = W_q, W_k, W_v, W_o
    x_flat = x.rearrange("b s d -> (b s) d")
    with ExitStack() as ctx:
        g = residents(nc, z, ctx)
        with nc.cleanup_on_exit():
            setup(nc, z, g, dram)
            norm_first(nc, z, g, dram, x_flat)
            feed_forward(nc, z, g, dram, "f1_", x_flat, True, dram.x1)
        attention(nc, z, g, dram)
        feed_forward(nc, z, g, dram, "f2_", dram.x2, False, out.rearrange("b s d -> (b s) d"))


_INS = ['L0_attn_x', 'L0_attn_W_q', 'L0_attn_W_k', 'L0_attn_W_v', 'L0_attn_W_o', 'L0_ffn_router_w',
        'L0_ffn_expert_bias', 'L0_ffn_shared_w1', 'L0_ffn_shared_w2', 'L0_ffn_shared_w3', 'L0_ffn_routed_w1',
        'L0_ffn_routed_w2', 'L0_ffn_routed_w3']
_TURNED = ('L0_attn_W_q', 'L0_attn_W_k', 'L0_attn_W_v', 'L0_attn_W_o')


def kernel(**inputs):
    import numpy as _np
    import concourse.bacc as _bacc
    from concourse import mybir as _mybir
    from concourse.bass_utils import run_bass_kernel_spmd as _run

    nc = _bacc.Bacc("TRN2", target_bir_lowering=False, num_devices=1)
    arrays, args = {}, []
    for name in _INS:
        a = _np.asarray(inputs[name])
        a = _np.ascontiguousarray(a.T if name in _TURNED else a)
        arrays[f"in_{name}_dram"] = a
        args.append(nc.dram_tensor(f"in_{name}_dram", a.shape, _mybir.dt.from_np(a.dtype), kind="ExternalInput").ap())
    out = nc.dram_tensor("out_0_dram", args[0].shape, _mybir.dt.float32, kind="ExternalOutput").ap()
    macaron_kernel(nc, *args, out)
    r = _run(nc, [arrays], core_ids=[0])
    return r.results[0]["out_0_dram"]
```
